# Optimizing a Trainium2 kernel written in Bass

```python
import numpy as np
import jax
import jax.numpy as jnp

def _softmax(x, axis=-1):
    return jax.nn.softmax(x, axis=axis)

def _gelu(x):
    return jax.nn.gelu(x, approximate=True)

def _silu(x):
    return jax.nn.silu(x)

def _sigmoid(x):
    return jax.nn.sigmoid(x)

def _layernorm(x, axis=-1, eps=1e-05):
    m = jnp.mean(x, axis=axis, keepdims=True)
    v = jnp.var(x, axis=axis, keepdims=True)
    return (x - m) / jnp.sqrt(v + eps)

def _scatter_add(tgt, idx, src, axis=0):
    return tgt.at[idx].add(src)

def _segment_sum(src, seg, n):
    return jax.ops.segment_sum(src, seg, n)
kernel_name = 'mk_xattn_ffn_d2_seqx_r4_1a2755'

def setup_inputs(seed: int=0):
    np.random.seed(seed)
    _w = jnp.asarray

    def _rec_inputs():
        import jax
        import jax.numpy as jnp
        _rk = jax.random.key(seed)
        x = -0.0002928 + 1 * jax.random.normal(jax.random.fold_in(_rk, 1), (4, 512, 256), jnp.float32)
        _lenS = 512 - jax.random.randint(jax.random.fold_in(_rk, 7), (4,), 0, max(1, 512 // 4) + 1, jnp.int32)
        _lenS2 = 64 - jax.random.randint(jax.random.fold_in(_rk, 8), (4,), 0, max(1, 64 // 4) + 1, jnp.int32)
        _ctx_1024P = jax.random.normal(jax.random.fold_in(_rk, 11), (4, 16, 256), jnp.float32)
        _ctx_1024c = jax.random.dirichlet(jax.random.fold_in(_rk, 511), 0.3 * jnp.ones((16,), jnp.float32), (4, 64))
        _ctx_1024t = jnp.einsum('bsk,bkd->bsd', _ctx_1024c, _ctx_1024P)
        _ctx_1024t = _ctx_1024t * jax.lax.rsqrt(jnp.mean(jnp.square(_ctx_1024t)) + 1e-12) * 0.953939
        ctx_1024 = 4.13588e-05 + 0.999923 * (_ctx_1024t + 0.3 * jax.random.normal(jax.random.fold_in(_rk, 611), (4, 64, 256), jnp.float32))
        _validS = jnp.arange(512)[None, :] < _lenS[:, None]
        _validS2 = jnp.arange(64)[None, :] < _lenS2[:, None]
        _causal = jnp.tril(jnp.ones((512, 512), dtype=bool))
        mask_BxS2_bf1 = jnp.ones((4, 64), dtype=bool)
        return (x, ctx_1024, mask_BxS2_bf1)
    x, ctx_1024, mask_BxS2_bf1 = _rec_inputs()

    def _L0_xattn_setup():
        import math
        import jax, jax.numpy as jnp
        import numpy as np
        DIM = 256
        HEADS = 16
        DIM_HEAD = DIM // HEADS
        SCALE = DIM_HEAD ** (-0.5)

        def _apply_rotary_emb(x, seq_len):
            pos = jnp.arange(seq_len, dtype=jnp.float32)[:, None]
            div = jnp.exp(jnp.arange(0, DIM_HEAD, 2, dtype=jnp.float32) * (-math.log(10000.0) / DIM_HEAD))
            freqs = pos * div
            emb = jnp.concatenate([freqs, freqs], axis=-1)[None, None].astype(x.dtype)
            x1, x2 = (x[..., :DIM_HEAD // 2], x[..., DIM_HEAD // 2:])
            x_rot = jnp.concatenate([-x2, x1], axis=-1)
            return x * jnp.cos(emb) + x_rot * jnp.sin(emb)
        key = jax.random.key(seed)
        ks = jax.random.split(key, 5)
        b, n_q, n_kv = (2, 512, 1024)
        q_x = jax.random.normal(ks[0], (b, n_q, DIM), dtype=jnp.float32)
        kv_x = jax.random.normal(ks[1], (b, n_kv, DIM), dtype=jnp.float32)
        mask = jnp.ones((b, n_kv), dtype=bool)

        def xavier(k, shape):
            bound = math.sqrt(6.0 / (shape[0] + shape[1]))
            return jax.random.uniform(k, shape, jnp.float32, -bound, bound)
        Wq = xavier(ks[2], (DIM, DIM))
        Wkv = xavier(ks[3], (DIM, 2 * DIM))
        Wout = xavier(ks[4], (DIM, DIM))
        return {'q_x': q_x, 'kv_x': kv_x, 'mask': mask, 'Wq': Wq, 'Wkv': Wkv, 'Wout': Wout}
    _L0_xattn_all = _L0_xattn_setup()
    _L0_xattn_in = {k: v for k, v in _L0_xattn_all.items() if k in ('Wq', 'Wkv', 'Wout')}
    del _L0_xattn_all

    def _L0_ffn_setup():
        import jax, jax.numpy as jnp
        import numpy as np
        H = 16
        TOP_K = 2
        LN_EPS = 1e-05
        key = jax.random.key(seed)
        ks = jax.random.split(key, 8)
        B, S, E, NE = (2, 256, 256, 8)
        w = lambda k, shp: jax.random.normal(k, shp, dtype=jnp.float32) * 0.02
        return {'x': jax.random.normal(ks[0], (B, S, E), dtype=jnp.float32), 'rW1': w(ks[1], (E // 2, E)), 'rb1': jnp.zeros((E // 2,), jnp.float32), 'ln_g': jnp.ones((E // 2,), jnp.float32), 'ln_b': jnp.zeros((E // 2,), jnp.float32), 'rW2': w(ks[2], (NE, E // 2)), 'rb2': jnp.zeros((NE,), jnp.float32), 'qW': w(ks[3], (NE, E, E)), 'qb': jnp.zeros((NE, E), jnp.float32), 'kW': w(ks[4], (NE, E, E)), 'kb': jnp.zeros((NE, E), jnp.float32), 'vW': w(ks[5], (NE, E, E)), 'vb': jnp.zeros((NE, E), jnp.float32), 'oW': w(ks[6], (NE, E, E)), 'ob': jnp.zeros((NE, E), jnp.float32)}
    _L0_ffn_all = _L0_ffn_setup()
    _L0_ffn_in = {k: v for k, v in _L0_ffn_all.items() if k in ('rW1', 'rb1', 'ln_g', 'ln_b', 'rW2', 'rb2', 'qW', 'qb', 'kW', 'kb', 'vW', 'vb', 'oW', 'ob')}
    del _L0_ffn_all

    def _L1_xattn_setup():
        import jax, jax.numpy as jnp
        import numpy as np
        import math
        D = 256
        H = 8
        HD = D // H
        TEMP = math.sqrt(D)
        EPS = 1e-05

        def _layernorm(x, g, b):
            mu = jnp.mean(x, axis=-1, keepdims=True)
            var = jnp.var(x, axis=-1, keepdims=True)
            return (x - mu) * jax.lax.rsqrt(var + EPS) * g + b
        key = jax.random.key(seed)
        ks = jax.random.split(key, 8)
        B, Lq, Lk = (4, 512, 512)
        Q = jax.random.normal(ks[0], (B, Lq, D), dtype=jnp.float32)
        K = jax.random.normal(ks[1], (B, Lk, D), dtype=jnp.float32)
        V = jax.random.normal(ks[2], (B, Lk, D), dtype=jnp.float32)
        Wq = jax.random.normal(ks[3], (D, D), dtype=jnp.float32) * 0.02
        Wk = jax.random.normal(ks[4], (D, D), dtype=jnp.float32) * 0.02
        Wv = jax.random.normal(ks[5], (D, D), dtype=jnp.float32) * 0.02
        Wo = jax.random.normal(ks[6], (D, D), dtype=jnp.float32) * 0.02
        pre_g = jnp.ones((D,), jnp.float32)
        pre_b = jnp.zeros((D,), jnp.float32)
        ln_g = jnp.ones((D,), jnp.float32)
        ln_b = jnp.zeros((D,), jnp.float32)
        return {'Q': Q, 'K': K, 'V': V, 'Wq': Wq, 'Wk': Wk, 'Wv': Wv, 'Wo': Wo, 'pre_g': pre_g, 'pre_b': pre_b, 'ln_g': ln_g, 'ln_b': ln_b}
    _L1_xattn_all = _L1_xattn_setup()
    _L1_xattn_in = {k: v for k, v in _L1_xattn_all.items() if k in ('Wq', 'Wk', 'Wv', 'Wo', 'pre_g', 'pre_b', 'ln_g', 'ln_b')}
    del _L1_xattn_all

    def _L1_ffn_setup():
        import jax, jax.numpy as jnp
        import numpy as np
        import math
        D_IN = 256
        FEATURES = (1024, 1024, 256)
        BATCH, SEQ = (8, 512)

        def _conn_dense(kernel_bool, x):
            w = jnp.where(kernel_bool, jnp.float32(1.0), jnp.float32(-1.0))
            return x @ w
        key = jax.random.key(seed)
        kx, kk0, kk1, kk2 = jax.random.split(key, 4)
        x = jax.random.normal(kx, (BATCH, SEQ, D_IN), dtype=jnp.float32)
        k0 = jax.random.randint(kk0, (2 * D_IN, FEATURES[0]), 0, 2).astype(jnp.bool_)
        k1 = jax.random.randint(kk1, (FEATURES[0], FEATURES[1]), 0, 2).astype(jnp.bool_)
        k2 = jax.random.randint(kk2, (FEATURES[1], FEATURES[2]), 0, 2).astype(jnp.bool_)
        s0 = jnp.asarray(1.0 / math.sqrt(2 * D_IN), dtype=jnp.float32)
        s1 = jnp.asarray(1.0 / math.sqrt(FEATURES[0]), dtype=jnp.float32)
        s2 = jnp.asarray(1.0 / math.sqrt(FEATURES[1]), dtype=jnp.float32)
        return {'x': x, 'k0': k0, 'k1': k1, 'k2': k2, 's0': s0, 's1': s1, 's2': s2}
    _L1_ffn_all = _L1_ffn_setup()
    _L1_ffn_in = {k: v for k, v in _L1_ffn_all.items() if k in ('k0', 'k1', 'k2', 's0', 's1', 's2')}
    del _L1_ffn_all
    return {'x': x, 'ctx_1024': ctx_1024, 'mask_BxS2_bf1': mask_BxS2_bf1, 'L0_xattn_Wq': _L0_xattn_in['Wq'], 'L0_xattn_Wkv': _L0_xattn_in['Wkv'], 'L0_xattn_Wout': _L0_xattn_in['Wout'], 'L0_ffn_rW1': _L0_ffn_in['rW1'], 'L0_ffn_rb1': _L0_ffn_in['rb1'], 'L0_ffn_ln_g': _L0_ffn_in['ln_g'], 'L0_ffn_ln_b': _L0_ffn_in['ln_b'], 'L0_ffn_rW2': _L0_ffn_in['rW2'], 'L0_ffn_rb2': _L0_ffn_in['rb2'], 'L0_ffn_qW': _L0_ffn_in['qW'], 'L0_ffn_qb': _L0_ffn_in['qb'], 'L0_ffn_kW': _L0_ffn_in['kW'], 'L0_ffn_kb': _L0_ffn_in['kb'], 'L0_ffn_vW': _L0_ffn_in['vW'], 'L0_ffn_vb': _L0_ffn_in['vb'], 'L0_ffn_oW': _L0_ffn_in['oW'], 'L0_ffn_ob': _L0_ffn_in['ob'], 'L1_xattn_Wq': _L1_xattn_in['Wq'], 'L1_xattn_Wk': _L1_xattn_in['Wk'], 'L1_xattn_Wv': _L1_xattn_in['Wv'], 'L1_xattn_Wo': _L1_xattn_in['Wo'], 'L1_xattn_pre_g': _L1_xattn_in['pre_g'], 'L1_xattn_pre_b': _L1_xattn_in['pre_b'], 'L1_xattn_ln_g': _L1_xattn_in['ln_g'], 'L1_xattn_ln_b': _L1_xattn_in['ln_b'], 'L1_ffn_k0': _L1_ffn_in['k0'], 'L1_ffn_k1': _L1_ffn_in['k1'], 'L1_ffn_k2': _L1_ffn_in['k2'], 'L1_ffn_s0': _L1_ffn_in['s0'], 'L1_ffn_s1': _L1_ffn_in['s1'], 'L1_ffn_s2': _L1_ffn_in['s2']}

def reference(x, ctx_1024, mask_BxS2_bf1, L0_xattn_Wq, L0_xattn_Wkv, L0_xattn_Wout, L0_ffn_rW1, L0_ffn_rb1, L0_ffn_ln_g, L0_ffn_ln_b, L0_ffn_rW2, L0_ffn_rb2, L0_ffn_qW, L0_ffn_qb, L0_ffn_kW, L0_ffn_kb, L0_ffn_vW, L0_ffn_vb, L0_ffn_oW, L0_ffn_ob, L1_xattn_Wq, L1_xattn_Wk, L1_xattn_Wv, L1_xattn_Wo, L1_xattn_pre_g, L1_xattn_pre_b, L1_xattn_ln_g, L1_xattn_ln_b, L1_ffn_k0, L1_ffn_k1, L1_ffn_k2, L1_ffn_s0, L1_ffn_s1, L1_ffn_s2):
    import jax
    import jax.numpy as jnp

    def _L0_xattn_ref(q_x, kv_x, mask, Wq, Wkv, Wout):
        import math
        import jax, jax.numpy as jnp
        import numpy as np
        DIM = 256
        HEADS = 16
        DIM_HEAD = DIM // HEADS
        SCALE = DIM_HEAD ** (-0.5)

        def _apply_rotary_emb(x, seq_len):
            pos = jnp.arange(seq_len, dtype=jnp.float32)[:, None]
            div = jnp.exp(jnp.arange(0, DIM_HEAD, 2, dtype=jnp.float32) * (-math.log(10000.0) / DIM_HEAD))
            freqs = pos * div
            emb = jnp.concatenate([freqs, freqs], axis=-1)[None, None].astype(x.dtype)
            x1, x2 = (x[..., :DIM_HEAD // 2], x[..., DIM_HEAD // 2:])
            x_rot = jnp.concatenate([-x2, x1], axis=-1)
            return x * jnp.cos(emb) + x_rot * jnp.sin(emb)
        b, n_q, _ = q_x.shape
        _, n_kv, _ = kv_x.shape
        q = (q_x @ Wq).reshape(b, n_q, HEADS, DIM_HEAD).transpose(0, 2, 1, 3)
        kv = kv_x @ Wkv
        k, v = jnp.split(kv, 2, axis=-1)
        k = k.reshape(b, n_kv, HEADS, DIM_HEAD).transpose(0, 2, 1, 3)
        v = v.reshape(b, n_kv, HEADS, DIM_HEAD).transpose(0, 2, 1, 3)
        q = _apply_rotary_emb(q, n_q)
        k = _apply_rotary_emb(k, n_kv)
        dots = jnp.einsum('bhqd,bhkd->bhqk', q, k) * SCALE
        neg = jnp.finfo(dots.dtype).min
        dots = jnp.where(mask[:, None, None, :], dots, neg)
        attn = jax.nn.softmax(dots, axis=-1)
        out = jnp.einsum('bhqk,bhkd->bhqd', attn, v)
        out = out.transpose(0, 2, 1, 3).reshape(b, n_q, DIM)
        return out @ Wout

    def _L0_ffn_ref(x, rW1, rb1, ln_g, ln_b, rW2, rb2, qW, qb, kW, kb, vW, vb, oW, ob):
        import jax, jax.numpy as jnp
        import numpy as np
        H = 16
        TOP_K = 2
        LN_EPS = 1e-05
        B, S, E = x.shape
        NE = qW.shape[0]
        Dh = E // H
        scale = 1.0 / jnp.sqrt(jnp.asarray(Dh, x.dtype))
        h = x @ rW1.T + rb1
        mu = h.mean(-1, keepdims=True)
        var = ((h - mu) ** 2).mean(-1, keepdims=True)
        h = (h - mu) * jax.lax.rsqrt(var + LN_EPS) * ln_g + ln_b
        h = jax.nn.relu(h)
        logits = h @ rW2.T + rb2
        probs = jax.nn.softmax(logits, axis=-1)
        tp, ti = jax.lax.top_k(probs, TOP_K)
        tp = tp / tp.sum(-1, keepdims=True)
        expert_mask = (jax.nn.one_hot(ti, NE, dtype=probs.dtype) * tp[..., None]).sum(-2)
        gates = jnp.moveaxis(expert_mask, -1, 0)

        def expert_step(acc, params):
            qw, qb_, kw, kb_, vw, vb_, ow, ob_, g = params
            q = (x @ qw.T + qb_).reshape(B, S, H, Dh).transpose(0, 2, 1, 3)
            k = (x @ kw.T + kb_).reshape(B, S, H, Dh).transpose(0, 2, 1, 3)
            v = (x @ vw.T + vb_).reshape(B, S, H, Dh).transpose(0, 2, 1, 3)
            scores = jnp.einsum('bhqd,bhkd->bhqk', q, k) * scale
            p = jax.nn.softmax(scores, axis=-1)
            o = jnp.einsum('bhqk,bhkd->bhqd', p, v)
            o = o.transpose(0, 2, 1, 3).reshape(B, S, E) @ ow.T + ob_
            return (acc + o * g[..., None], None)
        out, _ = jax.lax.scan(expert_step, jnp.zeros_like(x), (qW, qb, kW, kb, vW, vb, oW, ob, gates))
        return out

    def _L1_xattn_ref(Q, K, V, Wq, Wk, Wv, Wo, pre_g, pre_b, ln_g, ln_b):
        import jax, jax.numpy as jnp
        import numpy as np
        import math
        D = 256
        H = 8
        HD = D // H
        TEMP = math.sqrt(D)
        EPS = 1e-05

        def _layernorm(x, g, b):
            mu = jnp.mean(x, axis=-1, keepdims=True)
            var = jnp.var(x, axis=-1, keepdims=True)
            return (x - mu) * jax.lax.rsqrt(var + EPS) * g + b
        B, Lq, _ = Q.shape
        Lk = K.shape[1]
        Qn = _layernorm(Q, pre_g, pre_b)
        Kn = _layernorm(K, pre_g, pre_b)
        q = (Qn @ Wq).reshape(B, Lq, H, HD)
        k = (Kn @ Wk).reshape(B, Lk, H, HD)
        v = (V @ Wv).reshape(B, Lk, H, HD)
        scores = jnp.einsum('bqhd,bkhd->bhqk', q, k) / TEMP
        scores = jnp.clip(scores, -10000.0, 10000.0)
        A = jax.nn.softmax(scores, axis=-1)
        O = jnp.einsum('bhqk,bkhd->bqhd', A, v).reshape(B, Lq, D)
        O = _layernorm(O, ln_g, ln_b)
        O = O + jax.nn.gelu(O @ Wo, approximate=False)
        return O

    def _L1_ffn_ref(x, k0, k1, k2, s0, s1, s2):
        import jax, jax.numpy as jnp
        import numpy as np
        import math
        D_IN = 256
        FEATURES = (1024, 1024, 256)
        BATCH, SEQ = (8, 512)

        def _conn_dense(kernel_bool, x):
            w = jnp.where(kernel_bool, jnp.float32(1.0), jnp.float32(-1.0))
            return x @ w
        h = jnp.concatenate([x, -x], axis=-1)
        h = s0 * _conn_dense(k0, h)
        h = jax.nn.relu(h) * 2
        h = s1 * _conn_dense(k1, h)
        h = jax.nn.relu(h) * 2
        h = s2 * _conn_dense(k2, h)
        return h
    x = x + _L0_xattn_ref(_layernorm(x, axis=-1), ctx_1024, mask_BxS2_bf1, L0_xattn_Wq, L0_xattn_Wkv, L0_xattn_Wout)
    x = x + _L0_ffn_ref(_layernorm(x, axis=-1), L0_ffn_rW1, L0_ffn_rb1, L0_ffn_ln_g, L0_ffn_ln_b, L0_ffn_rW2, L0_ffn_rb2, L0_ffn_qW, L0_ffn_qb, L0_ffn_kW, L0_ffn_kb, L0_ffn_vW, L0_ffn_vb, L0_ffn_oW, L0_ffn_ob)
    x = x + _L1_xattn_ref(_layernorm(x, axis=-1), ctx_1024, ctx_1024, L1_xattn_Wq, L1_xattn_Wk, L1_xattn_Wv, L1_xattn_Wo, L1_xattn_pre_g, L1_xattn_pre_b, L1_xattn_ln_g, L1_xattn_ln_b)
    x = x + _L1_ffn_ref(_layernorm(x, axis=-1), L1_ffn_k0, L1_ffn_k1, L1_ffn_k2, L1_ffn_s0, L1_ffn_s1, L1_ffn_s2)
    return x

_drawn_inputs = setup_inputs


def setup_inputs(seed=0):
    import zlib

    import numpy as np

    out = dict(_drawn_inputs(seed))
    spreads = {'L0_ffn_rb1': (0.0, 0.348),
     'L0_ffn_ln_g': (1.0, 0.6),
     'L0_ffn_ln_b': (0.0, 0.545),
     'L0_ffn_rb2': (0.0, 0.1),
     'L0_ffn_qb': (0.0, 0.8),
     'L0_ffn_kb': (0.0, 0.8),
     'L0_ffn_vb': (0.0, 0.529),
     'L0_ffn_ob': (0.0, 0.1),
     'L1_xattn_pre_g': (1.0, 0.6),
     'L1_xattn_pre_b': (0.0, 0.8),
     'L1_xattn_ln_g': (1.0, 0.2),
     'L1_xattn_ln_b': (0.0, 0.1)}
    factors = {'L0_ffn_qW': 8.0,
     'L0_ffn_kW': 8.0,
     'L0_ffn_vW': 2.923,
     'L1_xattn_Wq': 5.134,
     'L1_xattn_Wk': 5.109}
    for name, (base, spread) in spreads.items():
        noise = np.random.default_rng([zlib.crc32(name.encode()), seed]).standard_normal(out[name].shape)
        drawn = base * np.exp(spread * noise) if base else spread * noise
        out[name] = jnp.asarray(drawn.astype(out[name].dtype))
    for name, factor in factors.items():
        out[name] = (out[name] * factor).astype(out[name].dtype)
    return out
```

```python
from contextlib import ExitStack

import numpy as np

import concourse.bass as bass
from concourse import mybir

F32 = mybir.dt.float32
BF16 = mybir.dt.bfloat16
U8 = mybir.dt.uint8
U32 = mybir.dt.uint32
ALU = mybir.AluOpType
ACT = mybir.ActivationFunctionType
AX = mybir.AxisListType

P = 128
B, S, D = 4, 512, 256
T = B * S // P
TB = S // P
KC = D // P
S2 = 64
NCTX = B * S2
H0, H1 = 16, 8
E, HE, DH = 8, 16, 16
R1 = D // 2
FF = 1024
OC = FF // P
EPS = 1e-5
LOWEST = -3.4028234663852886e38
HC = HE // KC
G4 = 4
RING = 8
Q_PARTS, K_PARTS = (0, 0, 0, 1, 1, 2), (0, 1, 2, 0, 1, 0)
SPLIT_ROWS = len(Q_PARTS) * DH
MAX_ROWS = SPLIT_ROWS + 2


def bcast(ap, axis, n):
    ap = ap.unsqueeze(axis)
    shape = list(ap.shape)
    shape[axis] = n
    return ap.broadcast_to(shape)


def by(ap, n):
    dims = " ".join("abcdef"[:len(ap.shape) - 1])
    return ap.rearrange(f"{dims} (g n) -> {dims} g n", n=n)


class Steps:

    def __init__(self, engine, semaphore):
        self.engine, self.semaphore, self.count = engine, semaphore, 0

    def did(self, instruction):
        instruction.then_inc(self.semaphore, 1)
        self.count += 1

    def wait(self):
        self.engine.wait_ge(self.semaphore, self.count)


CONST_WIDTHS = (("ident", P), ("heads16", H0 // KC), ("heads8", H1 // KC), ("first", E), ("eps", 1), ("one", 1))
CONST = {name: slice(sum(w for _, w in CONST_WIDTHS[:i]), sum(w for _, w in CONST_WIDTHS[:i + 1]))
         for i, (name, _) in enumerate(CONST_WIDTHS)}
NCONST = sum(w for _, w in CONST_WIDTHS)


class Scope:

    def __init__(self, nc, name, stack):
        self.nc, self.name, self.stack = nc, name, stack

    def sem(self, name):
        return self.stack.enter_context(self.nc.semaphore(f"{self.name}_{name}"))

    def sems(self, names):
        return [self.sem(n) for n in names.split()]

    def sb(self, name, shape, dt=F32):
        return self.stack.enter_context(self.nc.sbuf_tensor(f"{self.name}_{name}", shape, dt))


def context_stage(nc, t, io, name, more):
    with ExitStack() as stack:
        sc = Scope(nc, name, stack)
        loaded, own, var_ready, std_ready, normed, turned, evacuated = sc.sems(
            "loaded own var_ready std_ready normed turned evacuated")
        cx = sc.sb("cx", [P, NCTX // P, D])
        cn = sc.sb("cn", [P, NCTX // P, D])
        mask = sc.sb("mask", [P, NCTX], U8)
        loads = more + [(cx, io["ctx"]), (mask, io["mask"]), (t.pre, io["pre"])]
        block = stack.enter_context(nc.Block())

        @block.sync
        def _(sp):
            for out, src in loads:
                sp.dma_start(out[:], src).then_inc(loaded, 16)

        @block.vector
        def _(dve):
            dve.wait_ge(loaded, 16 * len(loads))
            steps = Steps(dve, own)
            for i in range(NCTX // P):
                steps.did(nc.vector.bn_stats(t.stats[:, i, :], cx[:, i, :]))
            steps.did(nc.vector.tensor_scalar(t.bound[:], mask[:], 0.5, -LOWEST, ALU.subtract, ALU.mult))
            steps.wait()
            steps.did(nc.vector.tensor_scalar(t.bound[:], t.bound[:], 2.0, None, ALU.mult))
            for i in range(NCTX // P):
                last = nc.vector.bn_aggr(t.mv[:, i, :], t.stats[:, i, :])
            last.then_inc(var_ready, 1)
            dve.wait_ge(std_ready, 1)
            steps.did(nc.vector.reciprocal(t.rstd[:, 0:2], t.std[:, 0:2]))
            steps.wait()
            for i in range(NCTX // P):
                last = nc.vector.tensor_scalar(cn[:, i, :], cx[:, i, :], t.mv[:, i, 0:1], t.rstd[:, i:i + 1],
                                               ALU.subtract, ALU.mult)
            last.then_inc(normed, 1)

        @block.scalar
        def _(act):
            act.wait_ge(var_ready, 1)
            nc.scalar.activation(t.std[:, 0:2], t.mv[:, 0:2, 1], ACT.Sqrt, bias=t.eps).then_inc(std_ready, 1)
            for c in range(KC):
                act.wait_ge(turned, c + 1)
                src = t.ps[:, c, 0:NCTX]
                nc.scalar.copy(t.ctxT[:, c, :], src)
                for a in range(2):
                    nc.scalar.copy(t.ctxT2[:, c, :, a, :], src.rearrange("p (b k) -> p b k", b=B))
            for c in range(KC):
                act.wait_ge(turned, KC + c + 1)
                nc.scalar.activation(t.ctxnT[:, c, :], t.ps[:, KC + c, 0:NCTX], ACT.Identity,
                                     bias=t.pre[:, 1, c:c + 1], scale=t.pre[:, 0, c:c + 1])

        @block.tensor
        def _(pe):
            pe.wait_ge(loaded, 16 * len(loads))
            for n, src in enumerate((cx, cn)):
                if n:
                    pe.wait_ge(normed, 1)
                for c in range(KC):
                    for i in range(NCTX // P):
                        last = nc.tensor.transpose(t.ps[:, n * KC + c, i * P:(i + 1) * P], src[:, i, c * P:(c + 1) * P],
                                                   t.ident)
                    last.then_inc(turned, 1)


def layernorm_stage(nc, t, name, affine=None, rounds=1):
    with ExitStack() as stack:
        sc = Scope(nc, name, stack)
        var_ready, std_ready, xn_ready, turned, evacuated, own = sc.sems(
            "var_ready std_ready xn_ready turned evacuated own")
        xn = sc.sb("xn", [P, T, D])
        block = stack.enter_context(nc.Block())

        @block.vector
        def _(dve):
            steps = Steps(dve, own)
            for r in range(rounds):
                src = t.x if r == 0 else xn
                for b in range(B):
                    if r:
                        dve.wait_ge(xn_ready, b + 1)
                    for k in range(b * TB, (b + 1) * TB):
                        steps.did(nc.vector.bn_stats(t.stats[:, k, :], src[:, k, :]))
                    steps.wait()
                    for k in range(b * TB, (b + 1) * TB):
                        last = nc.vector.bn_aggr(t.mv[:, k, :], t.stats[:, k, :])
                    last.then_inc(var_ready, 1)
                for b in range(B):
                    dve.wait_ge(std_ready, r * B + b + 1)
                    steps.did(nc.vector.reciprocal(t.rstd[:, b * TB:(b + 1) * TB], t.std[:, b * TB:(b + 1) * TB]))
                    steps.wait()
                    for k in range(b * TB, (b + 1) * TB):
                        last = nc.vector.tensor_scalar(xn[:, k, :], src[:, k, :], t.mv[:, k, 0:1], t.rstd[:, k:k + 1],
                                                       ALU.subtract, ALU.mult)
                    last.then_inc(xn_ready, 1)

        @block.scalar
        def _(act):
            for j in range(rounds * B):
                b = j % B
                act.wait_ge(var_ready, j + 1)
                nc.scalar.activation(t.std[:, b * TB:(b + 1) * TB], t.mv[:, b * TB:(b + 1) * TB, 1], ACT.Sqrt,
                                     bias=t.eps).then_inc(std_ready, 1)
            for b in range(B):
                for c in range(KC):
                    act.wait_ge(turned, b * KC + c + 1)
                    out, bank = t.xnT[:, c, b * S:(b + 1) * S], t.ps[:, b * KC + c, :]
                    if affine is None:
                        nc.scalar.copy(out, bank)
                    else:
                        nc.scalar.activation(out, bank, ACT.Identity, bias=affine[1][:, c:c + 1],
                                             scale=affine[0][:, c:c + 1])

        @block.tensor
        def _(pe):
            for b in range(B):
                pe.wait_ge(xn_ready, (rounds - 1) * B + b + 1)
                for c in range(KC):
                    for i in range(TB):
                        last = nc.tensor.transpose(t.ps[:, b * KC + c, i * P:(i + 1) * P],
                                                   xn[:, b * TB + i, c * P:(c + 1) * P], t.ident)
                    last.then_inc(turned, 1)


def context_attention(nc, t, name, heads, weights, order, scale, rotary, keys_in, limit, rows):
    dh, hc = D // heads, heads // KC
    NK = heads * S2
    NC = NK // KC
    NB = NK // P
    sin_cos = ("cos", "sin") if rotary else ("cos",)
    with ExitStack() as outer:
        so = Scope(nc, name, outer)
        W = so.sb("w", [P, KC, len(order), D])
        w = {n: W[:, :, j, :] for j, n in enumerate(order)}
        qT = so.sb("qT", [P, KC, B * S])
        kd = so.sb("kd", [P, B, KC, hc, S2])
        vd = so.sb("vd", [P, B, D])
        o = so.sb("o", [P, T, D])
        kT = so.sb("kT", [P, KC, NCTX])

        with ExitStack() as stack:
            sc = Scope(nc, f"{name}_qkv", stack)
            loaded, v_ready, v_taken, made, products, taken, zeroed, k_sum = sc.sems(
                "loaded v_ready v_taken made products taken zeroed k_sum")
            part = sc.sb("part", [P, 2, 2, S])
            jobs = [("k", None, c) for c in range(KC)] + [("q", b, c) for b in range(B) for c in range(KC)]

            def width(job):
                return NCTX if job[0] == "k" else S

            def target(job):
                kind, b, c = job
                return kT[:, c, :] if kind == "k" else qT[:, c, b * S:(b + 1) * S]

            block = stack.enter_context(nc.Block())

            @block.sync
            def _(sp):
                sp.dma_start(W[:], weights).then_inc(loaded, 16)

            @block.tensor
            def _(pe):
                pe.wait_ge(loaded, 16)
                for b in range(B):
                    for kc in range(KC):
                        last = nc.tensor.matmul(t.ps[:, b, 0:D], t.ctxT2[:, kc, b, :, :].rearrange("p a k -> p (a k)"),
                                                w["v"][:, kc, :], start=kc == 0, stop=kc == KC - 1)
                    last.then_inc(v_ready, 1)
                pe.wait_ge(v_taken, B)
                for j, job in enumerate(jobs):
                    kind, b, c = job
                    n = width(job)
                    if j >= 4:
                        pe.wait_ge(taken, j - 3)
                    for a in range(2 if rotary else 1):
                        src = keys_in if kind == "k" else t.xnT
                        for kc in range(KC):
                            rhs = src[:, kc, :] if kind == "k" else src[:, kc, b * S:(b + 1) * S]
                            last = nc.tensor.matmul(t.ps[:, 2 * (j % 4) + a, 0:n],
                                                    w[kind + ("rot" if a else "")][:, kc, c * P:(c + 1) * P], rhs,
                                                    start=kc == 0, stop=kc == KC - 1)
                    last.then_inc(made, 1)

            @block.vector
            def _(dve):
                nc.vector.memset(vd[:], 0.0).then_inc(zeroed, 1)
                dve.wait_ge(zeroed, 1)
                for b in range(B):
                    dve.wait_ge(v_ready, b + 1)
                    for half in range(2):
                        r = slice(half * 64, half * 64 + 64)
                        last = nc.vector.tensor_copy(by(by(vd[r, b, :], 2 * dh), dh)[:, :, half, :],
                                                     by(by(t.ps[r, b, 0:D], 2 * dh), dh)[:, :, half, :])
                    last.then_inc(v_taken, 1)
                if rotary:
                    for j, job in enumerate(jobs):
                        n = width(job)
                        dve.wait_ge(made, j + 1)
                        if j >= 2:
                            dve.wait_ge(k_sum, j - 1)
                        for a in range(2):
                            src, table = t.ps[:, 2 * (j % 4) + a, 0:n], t.rot[a]
                            out = part[:, j % 2, a, 0:n]
                            if job[0] == "k":
                                src, out, table = by(src, S2), by(out, S2), bcast(table[:, 0:S2], 1, B)
                            last = nc.vector.tensor_tensor(out, src, table, ALU.mult)
                        last.then_inc(taken, 1)
                dve.wait_ge(k_sum if rotary else taken, KC)
                for b in range(B):
                    for c in range(KC):
                        nc.vector.tensor_tensor(kd[:, b, c, :, :], bcast(kT[:, c, b * S2:(b + 1) * S2], 1, hc),
                                                bcast(t.heads[heads], 2, S2), ALU.mult)

            if rotary:
                @block.gpsimd
                def _(pool):
                    for j, job in enumerate(jobs):
                        pool.wait_ge(taken, j + 1)
                        n = width(job)
                        nc.gpsimd.tensor_tensor(target(job), part[:, j % 2, 0, 0:n], part[:, j % 2, 1, 0:n], ALU.add)\
                            .then_inc(k_sum, 1)
            else:
                @block.scalar
                def _(act):
                    for j, job in enumerate(jobs):
                        act.wait_ge(made, j + 1)
                        nc.scalar.copy(target(job), t.ps[:, 2 * (j % 4), 0:width(job)]).then_inc(taken, 1)

        with ExitStack() as stack:
            sc = Scope(nc, f"{name}_attend", stack)
            scores_ready, bounded, max_ready, centred, exp_ready, p_turned, p_evacuated, o_ready, o_taken, sum_ready, rsum_ready = \
                sc.sems("scores_ready bounded max_ready centred exp_ready p_turned p_evacuated o_ready o_taken "
                        "sum_ready rsum_ready")
            prob = sc.sb("prob", [P, 2, NK])
            probT = sc.sb("probT", [P, 2, NB * P])
            mx = sc.sb("mx", [P, 2, heads])
            total = sc.sb("total", [P, 2, heads])
            rsum = sc.sb("rsum", [P, 2, heads])
            LAG = 2
            block = stack.enter_context(nc.Block())

            @block.tensor
            def _(pe):
                for i in range(T + LAG):
                    if i < T:
                        b = i // TB
                        if i >= 2:
                            pe.wait_ge(bounded, i - 1)
                        for c in range(KC):
                            last = nc.tensor.matmul(t.ps[:, 2 * (i % 2) + c, 0:NC], qT[:, c, i * P:(i + 1) * P],
                                                    kd[:, b, c, :, :].rearrange("p h k -> p (h k)"), start=True, stop=True)
                        last.then_inc(scores_ready, 1)
                    if 1 <= i <= T:
                        j = i - 1
                        pe.wait_ge(exp_ready, j + 1)
                        if j:
                            pe.wait_ge(p_evacuated, j)
                        for n in range(NB):
                            last = nc.tensor.transpose(t.ps[:, 4 + n // 4, (n % 4) * P:(n % 4 + 1) * P],
                                                       prob[:, j % 2, n * P:(n + 1) * P], t.ident)
                        last.then_inc(p_turned, 1)
                    if i >= LAG:
                        j = i - LAG
                        pe.wait_ge(p_evacuated, j + 1)
                        if j >= 2:
                            pe.wait_ge(o_taken, j - 1)
                        for n in range(NB):
                            cols = slice(n * 2 * dh, (n + 1) * 2 * dh)
                            last = nc.tensor.matmul(t.ps[:, 6 + j % 2, cols], probT[:, j % 2, n * P:(n + 1) * P],
                                                    vd[:, j // TB, cols], start=True, stop=True)
                        last.then_inc(o_ready, 1)

            @block.vector
            def _(dve):
                for i in range(T + LAG):
                    if i < T:
                        dve.wait_ge(scores_ready, i + 1)
                        if i >= 2:
                            dve.wait_ge(p_turned, i - 1)
                        banks = t.ps[:, 2 * (i % 2):2 * (i % 2) + KC, 0:NC]
                        out = prob[:, i % 2, :].rearrange("p (c n) -> p c n", c=KC)
                        if limit is None:
                            b = i // TB
                            for c in range(KC):
                                ins = nc.vector.tensor_tensor(by(out[:, c, :], S2), by(banks[:, c, :], S2),
                                                              bcast(t.bound[:, b * S2:(b + 1) * S2], 1, hc), ALU.min)
                        else:
                            ins = nc.vector.tensor_scalar(out, banks, limit, -limit, ALU.min, ALU.max)
                        ins.then_inc(bounded, 1)
                        dve.wait_ge(bounded, i + 1)
                        nc.vector.tensor_reduce(mx[:, i % 2, :], by(prob[:, i % 2, :], S2), AX.X, ALU.max)\
                            .then_inc(max_ready, 1)
                    if 1 <= i <= T:
                        j = i - 1
                        dve.wait_ge(exp_ready, j + 1)
                        nc.vector.tensor_reduce(total[:, j % 2, :], by(prob[:, j % 2, :], S2), AX.X, ALU.add)\
                            .then_inc(sum_ready, 1)
                        dve.wait_ge(sum_ready, j + 1)
                        nc.vector.reciprocal(rsum[:, j % 2, :], total[:, j % 2, :]).then_inc(rsum_ready, 1)
                    if i >= LAG:
                        j = i - LAG
                        dve.wait_ge(o_ready, j + 1)
                        dve.wait_ge(rsum_ready, j + 1)
                        nc.vector.tensor_tensor(by(o[:, j, :], dh), by(t.ps[:, 6 + j % 2, 0:D], dh),
                                                bcast(rsum[:, j % 2, :], 2, dh), ALU.mult).then_inc(o_taken, 1)

            @block.gpsimd
            def _(pool):
                for i in range(T):
                    pool.wait_ge(max_ready, i + 1)
                    pr = by(prob[:, i % 2, :], S2)
                    nc.gpsimd.tensor_tensor(pr, pr, bcast(mx[:, i % 2, :], 2, S2), ALU.subtract).then_inc(centred, 1)

            @block.scalar
            def _(act):
                for i in range(T + 1):
                    if i < T:
                        act.wait_ge(centred, i + 1)
                        nc.scalar.activation(prob[:, i % 2, :], prob[:, i % 2, :], ACT.Exp, scale=scale)\
                            .then_inc(exp_ready, 1)
                    if i >= 1:
                        j = i - 1
                        act.wait_ge(p_turned, j + 1)
                        if j >= 2:
                            act.wait_ge(o_ready, j - 1)
                        n = NB * P // 512
                        nc.scalar.copy(probT[:, j % 2, :].rearrange("p (a n) -> p a n", a=n), t.ps[:, 4:4 + n, :])\
                            .then_inc(p_evacuated, 1)

        with ExitStack() as stack:
            sc = Scope(nc, f"{name}_out", stack)
            var_ready, std_ready, own, normed, turned, evacuated, y_ready, y_taken, gelu_ready, rows_in, stats_ready = sc.sems(
                "var_ready std_ready own normed turned evacuated y_ready y_taken gelu_ready rows_in stats_ready")
            oT = sc.sb("oT", [P, 2, KC * P])
            gl = sc.sb("gl", [P, 2, D])
            if rows is not None:
                gb = sc.sb("gb", [P, 2, D])
            block = stack.enter_context(nc.Block())

            @block.sync
            def _(sp):
                if rows is not None:
                    sp.dma_start(gb[:], rows).then_inc(rows_in, 16)

            @block.tensor
            def _(pe):
                for i in range(T + 1):
                    if i < T:
                        if rows is not None:
                            pe.wait_ge(normed, i + 1)
                        if i >= 2:
                            pe.wait_ge(evacuated, i - 1)
                        for c in range(KC):
                            last = nc.tensor.transpose(t.ps[:, i % 2, c * P:(c + 1) * P], o[:, i, c * P:(c + 1) * P], t.ident)
                        last.then_inc(turned, 1)
                    if i:
                        j = i - 1
                        pe.wait_ge(evacuated, j + 1)
                        if j >= 2:
                            pe.wait_ge(y_taken, j - 1)
                        for kc in range(KC):
                            last = nc.tensor.matmul(t.ps[:, 2 + j % 2, 0:D], oT[:, j % 2, kc * P:(kc + 1) * P],
                                                    w["o"][:, kc, :], start=kc == 0, stop=kc == KC - 1)
                        last.then_inc(y_ready, 1)

            @block.scalar
            def _(act):
                if rows is not None:
                    act.wait_ge(var_ready, 1)
                    nc.scalar.activation(t.std[:], t.mv[:, :, 1], ACT.Sqrt, bias=t.eps).then_inc(std_ready, 1)
                for i in range(T + 1):
                    if i < T:
                        act.wait_ge(turned, i + 1)
                        if i >= 2:
                            act.wait_ge(y_ready, i - 1)
                        nc.scalar.copy(oT[:, i % 2, :], t.ps[:, i % 2, 0:KC * P]).then_inc(evacuated, 1)
                    if i and rows is not None:
                        j = i - 1
                        act.wait_ge(y_ready, j + 1)
                        if j >= 2:
                            act.wait_ge(y_taken, j - 1)
                        nc.scalar.activation(gl[:, j % 2, :], t.ps[:, 2 + j % 2, 0:D], ACT.Gelu).then_inc(gelu_ready, 1)

            @block.vector
            def _(dve):
                steps = Steps(dve, own)
                if rows is not None:
                    for i in range(T):
                        steps.did(nc.vector.bn_stats(t.stats[:, i, :], o[:, i, :]))
                    steps.wait()
                    for i in range(T):
                        last = nc.vector.bn_aggr(t.mv[:, i, :], t.stats[:, i, :])
                    last.then_inc(var_ready, 1)
                    dve.wait_ge(rows_in, 16)
                    dve.wait_ge(std_ready, 1)
                    steps.did(nc.vector.reciprocal(t.rstd[:], t.std[:]))
                    steps.wait()
                for i in range(T + 1):
                    if i < T and rows is not None:
                        v = o[:, i, :]
                        steps.did(nc.vector.tensor_scalar(v, v, t.mv[:, i, 0:1], t.rstd[:, i:i + 1], ALU.subtract, ALU.mult))
                        steps.wait()
                        steps.did(nc.vector.tensor_tensor(v, v, gb[:, 0, :], ALU.mult))
                        steps.wait()
                        nc.vector.tensor_tensor(v, v, gb[:, 1, :], ALU.add).then_inc(normed, 1)
                        dve.wait_ge(normed, i + 1)
                        steps.did(nc.vector.tensor_tensor(t.x[:, i, :], t.x[:, i, :], v, ALU.add))
                    if i:
                        j = i - 1
                        if rows is None:
                            dve.wait_ge(y_ready, j + 1)
                            y = t.ps[:, 2 + j % 2, 0:D]
                        else:
                            dve.wait_ge(gelu_ready, j + 1)
                            steps.wait()
                            y = gl[:, j % 2, :]
                        nc.vector.tensor_tensor(t.x[:, j, :], t.x[:, j, :], y, ALU.add).then_inc(y_taken, 1)


def router_stage(nc, t, io):
    with ExitStack() as stack:
        sc = Scope(nc, "router", stack)
        loaded, own, h_ready, var_ready, std_ready, normed, turned, relu_ready, logits_ready, logits_in, exp_ready, \
            gates_ready, gt_turned, gt_ready, bias_ready, centred = sc.sems(
                "loaded own h_ready var_ready std_ready normed turned relu_ready logits_ready logits_in exp_ready "
                "gates_ready gt_turned gt_ready bias_ready centred")
        w1 = sc.sb("w1", [P, KC, R1])
        rows = sc.sb("rows", [P, R1 + E])
        cols = sc.sb("cols", [P, 2 + E])
        ob = sc.sb("ob", [E, D])
        h = sc.sb("h", [P, T, R1])
        hT = sc.sb("hT", [P, T * P])
        lg = sc.sb("lg", [P, T, E])
        pr = sc.sb("pr", [P, T, E])
        cand = sc.sb("cand", [P, T, E])
        pick = sc.sb("pick", [P, 2, T, E])
        one = sc.sb("one", [P, T])
        gT = sc.sb("gT", [E, T * P])
        loads = ((w1, io["rW1"]), (rows, io["r_rows"]), (cols, io["r_cols"]), (ob, io["ob"]))
        block = stack.enter_context(nc.Block())

        @block.sync
        def _(sp):
            for out, src in loads:
                sp.dma_start(out[:], src).then_inc(loaded, 16)

        @block.tensor
        def _(pe):
            pe.wait_ge(loaded, 16 * len(loads))
            for b in range(B):
                for i in range(TB):
                    k = b * TB + i
                    for kc in range(KC):
                        last = nc.tensor.matmul(t.ps[:, b, i * R1:(i + 1) * R1], t.xnT[:, kc, k * P:(k + 1) * P],
                                                w1[:, kc, :], start=kc == 0, stop=kc == KC - 1)
                last.then_inc(h_ready, 1)
            for b in range(B):
                pe.wait_ge(normed, b + 1)
                for i in range(TB):
                    last = nc.tensor.transpose(t.ps[:, b, i * P:(i + 1) * P], h[:, b * TB + i, :], t.ident)
                last.then_inc(turned, 1)
            for k in range(T):
                if k % TB == 0:
                    pe.wait_ge(relu_ready, k // TB + 1)
                last = nc.tensor.matmul(t.ps[:, 4, k * E:(k + 1) * E], hT[:, k * P:(k + 1) * P], cols[:, 2:2 + E],
                                        start=True, stop=True)
            last.then_inc(logits_ready, 1)
            pe.wait_ge(gates_ready, 1)
            for b in range(B):
                for i in range(TB):
                    last = nc.tensor.transpose(t.ps[0:E, b, i * P:(i + 1) * P], t.gates[:, :, b * TB + i], t.ident)
                last.then_inc(gt_turned, 1)
            for k in range(T):
                if k % TB == 0:
                    pe.wait_ge(gt_ready, k // TB + 1)
                if k >= 4:
                    pe.wait_ge(bias_ready, k - 3)
                nc.tensor.matmul(t.ps[:, 4 + k % 4, 0:D], gT[:, k * P:(k + 1) * P], ob[:],
                                 start=True, stop=True).then_inc(centred, 1)

        @block.scalar
        def _(act):
            for b in range(B):
                act.wait_ge(var_ready, b + 1)
                nc.scalar.activation(t.std[:, b * TB:(b + 1) * TB], t.mv[:, b * TB:(b + 1) * TB, 1], ACT.Sqrt,
                                     bias=t.eps).then_inc(std_ready, 1)
            for b in range(B):
                act.wait_ge(turned, b + 1)
                nc.scalar.activation(hT[:, b * S:(b + 1) * S], t.ps[:, b, :], ACT.Relu, bias=cols[:, 1:2],
                                     scale=cols[:, 0:1]).then_inc(relu_ready, 1)
            act.wait_ge(logits_in, 1)
            nc.scalar.activation(pr[:], lg[:], ACT.Exp).then_inc(exp_ready, 1)
            for b in range(B):
                act.wait_ge(gt_turned, b + 1)
                nc.scalar.copy(gT[:, b * S:(b + 1) * S], t.ps[0:E, b, :]).then_inc(gt_ready, 1)

        @block.vector
        def _(dve):
            steps = Steps(dve, own)

            def step(ins):
                steps.did(ins)
                steps.wait()

            dve.wait_ge(loaded, 16 * len(loads))
            for b in range(B):
                dve.wait_ge(h_ready, b + 1)
                ks = range(b * TB, (b + 1) * TB)
                step(nc.vector.tensor_tensor(h[:, b * TB:(b + 1) * TB, :], by(t.ps[:, b, :], R1),
                                             bcast(rows[:, 0:R1], 1, TB), ALU.add))
                for k in ks:
                    steps.did(nc.vector.bn_stats(t.stats[:, k, :], h[:, k, :]))
                steps.wait()
                for k in ks:
                    last = nc.vector.bn_aggr(t.mv[:, k, :], t.stats[:, k, :])
                last.then_inc(var_ready, 1)
            for b in range(B):
                dve.wait_ge(std_ready, b + 1)
                step(nc.vector.reciprocal(t.rstd[:, b * TB:(b + 1) * TB], t.std[:, b * TB:(b + 1) * TB]))
                for k in range(b * TB, (b + 1) * TB):
                    last = nc.vector.tensor_scalar(h[:, k, :], h[:, k, :], t.mv[:, k, 0:1], t.rstd[:, k:k + 1],
                                                   ALU.subtract, ALU.mult)
                last.then_inc(normed, 1)
            dve.wait_ge(logits_ready, 1)
            step(nc.vector.tensor_tensor(lg[:], by(t.ps[:, 4, 0:T * E], E), bcast(rows[:, R1:R1 + E], 1, T), ALU.add))
            step(nc.vector.tensor_reduce(one[:], lg[:], AX.X, ALU.max))
            nc.vector.tensor_tensor(lg[:], lg[:], bcast(one[:], 2, E), ALU.subtract).then_inc(logits_in, 1)
            dve.wait_ge(exp_ready, 1)
            step(nc.vector.tensor_reduce(one[:], pr[:], AX.X, ALU.add))
            step(nc.vector.reciprocal(one[:], one[:]))
            step(nc.vector.tensor_tensor(pr[:], pr[:], bcast(one[:], 2, E), ALU.mult))
            step(nc.vector.tensor_copy(lg[:], pr[:]))
            for n in range(2):
                step(nc.vector.tensor_reduce(one[:], lg[:], AX.X, ALU.max))
                step(nc.vector.tensor_tensor(cand[:], lg[:], bcast(one[:], 2, E), ALU.is_equal))
                step(nc.vector.tensor_tensor(cand[:], cand[:], bcast(t.const[:, CONST["first"]], 1, T), ALU.mult))
                step(nc.vector.tensor_reduce(one[:], cand[:], AX.X, ALU.max))
                step(nc.vector.tensor_tensor(pick[:, n, :, :], cand[:], bcast(one[:], 2, E), ALU.is_equal))
                if n == 0:
                    step(nc.vector.tensor_scalar(cand[:], pick[:, 0, :, :], -2.0, None, ALU.mult))
                    step(nc.vector.tensor_tensor(lg[:], lg[:], cand[:], ALU.add))
            step(nc.vector.tensor_tensor(cand[:], pick[:, 0, :, :], pick[:, 1, :, :], ALU.add))
            step(nc.vector.tensor_tensor(pr[:], pr[:], cand[:], ALU.mult))
            step(nc.vector.tensor_reduce(one[:], pr[:], AX.X, ALU.add))
            step(nc.vector.reciprocal(one[:], one[:]))
            nc.vector.tensor_tensor(t.gates[:].rearrange("p e k -> p k e"), pr[:], bcast(one[:], 2, E), ALU.mult)\
                .then_inc(gates_ready, 1)
            for k in range(T):
                dve.wait_ge(centred, k + 1)
                nc.vector.tensor_tensor(t.x[:, k, :], t.x[:, k, :],
                                        t.ps[:, 4 + k % 4, 0:D], ALU.add).then_inc(bias_ready, 1)


PAIRS = E * B


def round_steps(n):
    now, before, after, later = (0 <= m < PAIRS for m in (n, n - 1, n + 1, n + 2))
    at = {}

    def put(on, slot, place, *step):
        if on:
            at.setdefault((slot, place), []).append(step)

    for g in range(HE // G4):
        last = g == HE // G4 - 1
        for k in range(TB):
            put(before if last else now, (G4 * (g + 1)) % HE + k, 2, "values", n - last, g * TB + k)
    put(later, 0, 0, "project", n + 2, 0)
    put(later, 2, 0, "project", n + 2, 1)
    put(after, 4, 0, "project_v", n + 1, 0)
    put(later, 6, 0, "project", n + 2, 2)
    put(later, 8, 0, "project", n + 2, 3)
    put(before, 10, 0, "add", n - 1, 0)
    put(before, 12, 0, "add", n - 1, 1)
    put(after, 14, 0, "project_v", n + 1, 1)
    put(before, 1, 0, "turn_out", n - 1, 2)
    put(now, 3, 0, "row_max", n, 1)
    put(before, 5, 0, "turn_out", n - 1, 3)
    put(before, 7, 0, "turn_norm", n - 1, 1)
    put(now, 9, 0, "turn_out", n, 0)
    put(after, 11, 0, "row_max", n + 1, 0)
    put(now, 13, 0, "turn_out", n, 1)
    put(now, 15, 0, "turn_norm", n, 0)
    steps = []
    for h in range(HE):
        steps += at.get((h, 0), [])
        steps += [("maxima", n + 1, 2 * h)] * after
        steps += at.get((h, 1), [])
        steps += [("attend", n, 2 * h)] * now
        steps += [("maxima", n + 1, 2 * h + 1)] * after
        steps += at.get((h, 2), [])
        steps += [("attend", n, 2 * h + 1)] * now
    return steps


ROUNDS = range(-2, PAIRS + 1)
MISC = ("turn_out", "row_max", "turn_norm", "project", "add", "project_v")
MISC_LIST = [s for n in ROUNDS for s in round_steps(n) if s[0] in MISC]
MISC_AT = {step: i for i, step in enumerate(MISC_LIST)}


def ring_slot(n, h):
    return h % RING


def values_before(n, h):
    k = n * HE + h
    for j in range(k - 1, k - HE - RING, -1):
        if j >= 0 and ring_slot(*divmod(j, HE)) == ring_slot(n, h):
            return j // G4 + 1
    return 0


class Rounds:

    def __init__(self, engine, nc, steps):
        self.engine, self.expert = engine, None
        self.n = 0
        for self.n in range(-2, B):
            self.walk(steps)
        with engine.Fori(1, E - 1) as self.expert:
            for self.n in range(B, 2 * B):
                self.walk(steps)
        self.expert = None
        for self.n in range((E - 1) * B, PAIRS + 1):
            self.walk(steps)

    def walk(self, steps):
        start = steps.get("start")
        if start:
            start(self, self.n)
        for kind, m, arg in round_steps(self.n):
            if kind in steps:
                steps[kind](self, m, arg)
        end = steps.get("end")
        if end:
            end(self, self.n)

    def value(self, count, *args):
        m, rest = args[0], args[1:]
        v = count(m, *rest)
        if self.expert is None:
            return v
        step = count(m + B, *rest) - v
        assert v > 0 and step >= 0 and count(m + 2 * B, *rest) - v == 2 * step
        return self.expert * step + (v - step) if step else v

    def wait(self, semaphore, count, *args):
        v = self.value(count, *args)
        if self.expert is not None or v > 0:
            self.engine.wait_ge(semaphore, v)

    def expert_of(self, m):
        return m // B if self.expert is None else self.expert + (m // B - 1)


def expert_stage(nc, t, io):
    with ExitStack() as stack:
        sc = Scope(nc, "experts", stack)
        wqk_in, wv_in, wo_in = sc.sems("wqk_in wv_in wo_in")
        qk_moved, max_moved = sc.sems("qk_moved0 qk_moved1"), sc.sems("max_moved0 max_moved1")
        max_scores, maxed, scores, exped, summed, out_taken = sc.sems("max_scores maxed scores exped summed out_taken")
        misc_made, added, high_ready, rest_ready, mid_ready, low_ready, max_high, max_split, inverse, normed, \
            gate_ready, ones_ready, v_taken, turned_taken, sum_clear = sc.sems(
                "misc_made added high_ready rest_ready mid_ready low_ready max_high max_split inverse normed "
                "gate_ready ones_ready v_taken turned_taken sum_clear")
        QW = 4 * KC * P + 4
        VW = KC * D + D
        wqk = sc.sb("wqk", [P, QW])
        wv = sc.sb("wv", [P, VW])
        wo = sc.sb("wo", [P, KC * D])
        qs = [sc.sb(f"qs{i}", [MAX_ROWS, HE, S], BF16) for i in range(2)]
        ks = [sc.sb(f"ks{i}", [MAX_ROWS, HE, S], BF16) for i in range(2)]
        parts = sc.sb("parts", [P, 4, 3, S], BF16)
        rest = sc.sb("rest", [P, 2, S])
        vs = [sc.sb(f"vs{i}", [P, TB, HE, DH + 1]) for i in range(2)]
        prob = sc.sb("prob", [P, RING, TB, S])
        out_sb = sc.sb("out_sb", [P, S])
        rinv = sc.sb("rinv", [P, TB, G4])
        on = sc.sb("on", [P, TB, D])
        onT = sc.sb("onT", [P, KC, S])
        nmx = sc.sb("nmx", [P, TB, HE])
        nm = sc.sb("nm", [HC, 2, S], BF16)
        gate = sc.sb("gate", [P, TB])
        MX = t.ps[:, 0:4, :]
        EX = t.ps[:, 4:6, :]
        OUT = t.ps[:, 6, :]
        SH = t.ps[:, 7, :]

        max_count = lambda m, h, half: m * 2 * HE + 2 * h + half + 1
        score_count = lambda m, h, k: m * HE * TB + h * TB + k + 1
        sum_count = lambda m, g: m * HE // G4 + g + 1
        moved_count = lambda m: 16 * 2 * len(Q_PARTS) * (m + 1)
        max_moved_count = lambda m: 16 * 2 * (m + 1)
        row_count = lambda m, c: m * KC + c + 1
        value_count = lambda m, half: 2 * m + half + 1
        misc_count = lambda m, kind, a: MISC_AT[kind, m, a] + 1
        project_count = lambda m, a: 4 * m + a + 1
        freed = {"turn_out": (normed, sum_count), "row_max": (max_split, row_count), "turn_norm": (turned_taken, row_count),
                 "project": (rest_ready, project_count), "project_v": (v_taken, value_count), "add": (added, value_count)}
        block = stack.enter_context(nc.Block())

        @block.sync
        def _(sp):
            def load_qk(e):
                sp.dma_start(wqk[:], io["e_qk"][e]).then_inc(wqk_in, 16)

            def load_v(e):
                sp.dma_start(wv[:], io["e_v"][e]).then_inc(wv_in, 16)

            def load_o(e):
                sp.dma_start(wo[:], io["e_o"][e]).then_inc(wo_in, 16)

            def move_split(r, m, c):
                r.wait(low_ready, project_count, m, 2 * c + 1)
                for a, (dst, order) in enumerate(((qs[m % 2], Q_PARTS), (ks[m % 2], K_PARTS))):
                    for g, part in enumerate(order):
                        sp.dma_start(dst[g * DH:(g + 1) * DH, c * HC:(c + 1) * HC, :], parts[:, 2 * c + a, part, :])\
                            .then_inc(qk_moved[c], 16)

            def move_max(r, m, c):
                r.wait(max_split, row_count, m, c)
                for a in range(2):
                    sp.dma_start(qs[m % 2][SPLIT_ROWS + a:SPLIT_ROWS + a + 1, c * HC:(c + 1) * HC, :], nm[:, a, :])\
                        .then_inc(max_moved[c], 16)

            def start(r, n):
                if 0 <= n + 1 < PAIRS:
                    move_split(r, n + 1, 1)

            def step(r, m, a):
                move_max(r, m, a)

            def projected(r, m, a):
                if a == 3:
                    move_split(r, m, 0)

            def end(r, n):
                for m, semaphore, count, last, load in ((n + 2, rest_ready, project_count, 3, load_qk),
                                                        (n + 1, v_taken, value_count, 1, load_v),
                                                        (n - 1, misc_made, lambda m, a: misc_count(m, "add", a), 1, load_o)):
                    if m % B == B - 1 and B - 1 <= m < PAIRS - 1:
                        r.wait(semaphore, count, m, last)
                        if r.expert is not None:
                            sp.wait_ge(semaphore, 1)
                        load(r.expert_of(m + 1))

            load_qk(0)
            load_v(0)
            load_o(0)
            Rounds(sp, nc, {"start": start, "row_max": step, "project": projected, "end": end})

        @block.tensor
        def _(pe):
            def shared(r, kind, m, a):
                at = MISC_AT[kind, m, a]
                if at:
                    kind, m, a = MISC_LIST[at - 1]
                    r.wait(*freed[kind], m, a)

            def maxima(r, m, a):
                h, half = divmod(a, 2)
                if h % HC == 0 and half == 0:
                    r.wait(qk_moved[h // HC], moved_count, m)
                r.wait(maxed, lambda m: max_count(m, h, half) - 2, m)
                for q in range(2 * half, 2 * half + 2):
                    last = nc.tensor.matmul(MX[:, q, :], qs[m % 2][0:SPLIT_ROWS, h, q * P:(q + 1) * P],
                                            ks[m % 2][0:SPLIT_ROWS, h, :], start=True, stop=True)
                last.then_inc(max_scores, 1)

            def attend(r, m, a):
                h, half = divmod(a, 2)
                if h % HC == 0 and half == 0:
                    r.wait(max_moved[h // HC], max_moved_count, m)
                if m == 0 and a == 0:
                    pe.wait_ge(ones_ready, 4)
                for k in (2 * half, 2 * half + 1):
                    r.wait(exped, lambda m: score_count(m, h, k) - 2, m)
                    nc.tensor.matmul(EX[:, k % 2, :], ks[m % 2][:, h, k * P:(k + 1) * P], qs[m % 2][:, h, :],
                                     start=True, stop=True).then_inc(scores, 1)

            def values(r, m, a):
                g, k = divmod(a, TB)
                if k == 0:
                    r.wait(exped, score_count, m, G4 * g + G4 - 1, TB - 1)
                    r.wait(out_taken, lambda m: sum_count(m, g) - 1, m)
                if m == 0 and a == 0:
                    pe.wait_ge(sum_clear, 1)
                if a == 0:
                    r.wait(v_taken, value_count, m, 1)
                for j in range(G4):
                    h = G4 * g + j
                    last = nc.tensor.matmul(OUT[32 * j:32 * j + DH + 1, :], vs[m % 2][:, k, h, :],
                                            prob[:, ring_slot(m, h), k, :], start=k == 0, stop=k == TB - 1)
                if k == TB - 1:
                    last.then_inc(summed, 1)

            def turn_out(r, m, g):
                shared(r, "turn_out", m, g)
                r.wait(out_taken, sum_count, m, g)
                for q in range(TB):
                    last = nc.tensor.transpose(SH[:, q * P:(q + 1) * P], out_sb[:, q * P:(q + 1) * P], t.ident)
                last.then_inc(misc_made, 1)

            def row_max(r, m, c):
                shared(r, "row_max", m, c)
                r.wait(maxed, max_count, m, HC * (c + 1) - 1, 1)
                for q in range(TB):
                    last = nc.tensor.transpose(SH[0:HC, q * P:(q + 1) * P], nmx[:, q, c * HC:(c + 1) * HC], t.ident)
                last.then_inc(misc_made, 1)

            def turn_norm(r, m, c):
                shared(r, "turn_norm", m, c)
                r.wait(normed, lambda m: sum_count(m, 2 * c + 1), m)
                for q in range(TB):
                    last = nc.tensor.transpose(SH[:, q * P:(q + 1) * P], on[:, q, c * P:(c + 1) * P], t.ident)
                last.then_inc(misc_made, 1)

            def project(r, m, a):
                shared(r, "project", m, a)
                c, w = divmod(a, 2)
                if m % B == 0 and a == 0:
                    r.wait(wqk_in, lambda m: 16 * (m // B + 1), m)
                for kc in range(KC):
                    col = ((w * KC + c) * KC + kc) * P
                    last = nc.tensor.matmul(SH, wqk[:, col:col + P], t.xnT[:, kc, (m % B) * S:(m % B + 1) * S],
                                            start=kc == 0, stop=kc == KC - 1)
                last.then_inc(misc_made, 1)

            def project_v(r, m, half):
                shared(r, "project_v", m, half)
                if m % B == 0 and half == 0:
                    r.wait(wv_in, lambda m: 16 * (m // B + 1), m)
                for i in range(2):
                    tok = (m % B) * S + (2 * half + i) * P
                    for kc in range(KC):
                        last = nc.tensor.matmul(SH[:, i * D:(i + 1) * D], t.xnT[:, kc, tok:tok + P],
                                                wv[:, kc * D:(kc + 1) * D], start=kc == 0, stop=kc == KC - 1)
                last.then_inc(misc_made, 1)

            def add(r, m, half):
                shared(r, "add", m, half)
                if half == 0:
                    r.wait(turned_taken, row_count, m, KC - 1)
                    if m % B == 0:
                        r.wait(wo_in, lambda m: 16 * (m // B + 1), m)
                for i in range(2):
                    q = 2 * half + i
                    for kc in range(KC):
                        last = nc.tensor.matmul(SH[:, i * D:(i + 1) * D], onT[:, kc, q * P:(q + 1) * P],
                                                wo[:, kc * D:(kc + 1) * D], start=kc == 0, stop=kc == KC - 1)
                last.then_inc(misc_made, 1)

            Rounds(pe, nc, {"maxima": maxima, "attend": attend, "values": values, "turn_out": turn_out,
                            "row_max": row_max, "turn_norm": turn_norm, "project": project, "project_v": project_v,
                            "add": add})

        @block.scalar
        def _(act):
            def attend(r, m, a):
                h, half = divmod(a, 2)
                if half == 0:
                    r.wait(summed, lambda m: values_before(m, h), m)
                for k in (2 * half, 2 * half + 1):
                    r.wait(scores, score_count, m, h, k)
                    nc.scalar.activation(prob[:, ring_slot(m, h), k, :], EX[:, k % 2, :], ACT.Exp, scale=DH ** -0.5)\
                        .then_inc(exped, 1)

            def project(r, m, a):
                r.wait(misc_made, misc_count, m, "project", a)
                if m >= 1:
                    r.wait(qk_moved[a // 2], moved_count, m - 1)
                w = a % 2
                bias = wqk[:, 4 * KC * P + w * KC + a // 2:4 * KC * P + w * KC + a // 2 + 1]
                nc.scalar.activation(parts[:, a, 0, :], SH, ACT.Identity, bias=bias).then_inc(high_ready, 1)

            def values(r, m, a):
                g, k = divmod(a, TB)
                if k < TB - 1:
                    return
                r.wait(summed, sum_count, m, g)
                if m * (HE // G4) + g >= 1:
                    pm, pg = divmod(m * (HE // G4) + g - 1, HE // G4)
                    r.wait(misc_made, lambda x: misc_count(x, "turn_out", pg), pm)
                nc.scalar.copy(out_sb[:], OUT).then_inc(out_taken, 1)

            def turn_norm(r, m, c):
                r.wait(misc_made, misc_count, m, "turn_norm", c)
                nc.scalar.copy(onT[:, c, :], SH).then_inc(turned_taken, 1)

            Rounds(act, nc, {"attend": attend, "project": project, "values": values, "turn_norm": turn_norm})

        @block.vector
        def _(dve):
            def maxima(r, m, a):
                h, half = divmod(a, 2)
                two = slice(2 * half, 2 * half + 2)
                r.wait(max_scores, max_count, m, h, half)
                nc.vector.tensor_reduce(nmx[:, two, h], MX[:, two, :], AX.X, ALU.max, negate=True).then_inc(maxed, 1)

            def project(r, m, a):
                r.wait(high_ready, project_count, m, a)
                k = 4 * m + a
                if k >= 2:
                    r.wait(low_ready, lambda m: project_count(m, a) - 2, m)
                w = a % 2
                bias = wqk[:, 4 * KC * P + w * KC + a // 2:4 * KC * P + w * KC + a // 2 + 1]
                nc.vector.scalar_tensor_tensor(rest[:, a % 2, :], SH, bias, parts[:, a, 0, :], ALU.add, ALU.subtract)\
                    .then_inc(rest_ready, 1)

            def project_v(r, m, half):
                r.wait(misc_made, misc_count, m, "project_v", half)
                if m >= 2:
                    r.wait(summed, sum_count, m - 2, HE // G4 - 1)
                for i in range(2):
                    last = nc.vector.tensor_tensor(vs[m % 2][:, 2 * half + i, :, 0:DH], by(SH[:, i * D:(i + 1) * D], DH),
                                                   by(wv[:, KC * D:VW], DH), ALU.add)
                last.then_inc(v_taken, 1)

            def row_max(r, m, c):
                r.wait(misc_made, misc_count, m, "row_max", c)
                if c:
                    r.wait(max_moved[0], max_moved_count, m)
                elif m >= 1:
                    r.wait(max_moved[1], max_moved_count, m - 1)
                nc.vector.tensor_copy(nm[:, 0, :], SH[0:HC, :]).then_inc(max_high, 1)
                r.wait(max_high, row_count, m, c)
                if m >= 2:
                    r.wait(scores, score_count, m - 2, HC * (c + 1) - 1, TB - 1)
                nc.vector.tensor_tensor(nm[:, 1, :], SH[0:HC, :], nm[:, 0, :], ALU.subtract).then_inc(max_split, 1)

            def turn_out(r, m, g):
                r.wait(misc_made, misc_count, m, "turn_out", g)
                heads = SH.rearrange("p (q j d) -> p q j d", q=TB, j=G4)
                nc.vector.reciprocal(rinv[:], heads[:, :, :, DH]).then_inc(inverse, 1)
                r.wait(inverse, sum_count, m, g)
                for q in range(TB):
                    last = nc.vector.tensor_tensor(by(on[:, q, g * G4 * DH:(g + 1) * G4 * DH], DH), heads[:, q, :, 0:DH],
                                                   bcast(rinv[:, q, :], 2, DH), ALU.mult)
                last.then_inc(normed, 1)

            def add(r, m, half):
                if half == 0:
                    nc.vector.tensor_copy(gate[:], t.gates[:, r.expert_of(m), (m % B) * TB:(m % B + 1) * TB])\
                        .then_inc(gate_ready, 1)
                r.wait(misc_made, misc_count, m, "add", half)
                r.wait(gate_ready, lambda m: m + 1, m)
                for i in range(2):
                    q = 2 * half + i
                    x = t.x[:, (m % B) * TB + q, :]
                    last = nc.vector.scalar_tensor_tensor(x, SH[:, i * D:(i + 1) * D], gate[:, q:q + 1], x, ALU.mult, ALU.add)
                last.then_inc(added, 1)

            nc.vector.memset(OUT, 0.0).then_inc(sum_clear, 1)
            for i in range(2):
                nc.vector.memset(ks[i][SPLIT_ROWS:MAX_ROWS, :, :], 1.0).then_inc(ones_ready, 1)
                nc.vector.memset(vs[i][:, :, :, DH:DH + 1], 1.0).then_inc(ones_ready, 1)
            Rounds(dve, nc, {"maxima": maxima, "project": project, "project_v": project_v, "row_max": row_max,
                             "turn_out": turn_out, "add": add})

        @block.gpsimd
        def _(pool):
            def project(r, m, a):
                r.wait(rest_ready, project_count, m, a)
                if m >= 1:
                    r.wait(qk_moved[a // 2], moved_count, m - 1)
                nc.gpsimd.tensor_tensor(parts[:, a, 1, :], rest[:, a % 2, :], t.one.broadcast_to([P, S]), ALU.mult)\
                    .then_inc(mid_ready, 1)
                r.wait(mid_ready, project_count, m, a)
                if m >= 2 and a % 2:
                    r.wait(scores, score_count, m - 2, HC * (a // 2 + 1) - 1, TB - 1)
                nc.gpsimd.tensor_tensor(parts[:, a, 2, :], rest[:, a % 2, :], parts[:, a, 1, :], ALU.subtract)\
                    .then_inc(low_ready, 1)

            Rounds(pool, nc, {"project": project})


def sign_stage(nc, t, io):
    with ExitStack() as stack:
        sc = Scope(nc, "sign", stack)
        loaded, w_ready, x_high, x_rest, x_mid, x_low = sc.sems("loaded w_ready x_high x_rest x_mid x_low")
        made, kept, high, left, mid, low, y_ready, y_added, stored = sc.sems("made kept high left mid low y_ready y_added stored")
        words = [sc.sb(f"words{i}", [P, rows, width // 4], U32)
                 for i, (rows, width) in enumerate(((2 * KC, FF), (OC, FF), (OC, D)))]
        signs = [w[:].bitcast(U8) for w in words]
        w0 = sc.sb("w0", [P, KC, FF], BF16)
        w1 = sc.sb("w1", [P, OC, FF], BF16)
        w2 = sc.sb("w2", [P, OC, D], BF16)
        sv = sc.sb("sv", [P, 3])
        sv4 = sc.sb("sv4", [P, 3])
        xp = sc.sb("xp", [P, 2, 3, KC, S], BF16)
        xr = sc.sb("xr", [P, 2, KC * S])
        hp = [sc.sb(f"hp{i}", [P, 3, OC, S], BF16) for i in range(2)]
        hf = sc.sb("hf", [P, 2, S])
        hr = sc.sb("hr", [P, 2, S])
        loads = list(zip(words, (io["k0"], io["k1"], io["k2"]))) + [(sv, io["sv"])]
        block = stack.enter_context(nc.Block())

        @block.sync
        def _(sp):
            for out, src in loads:
                sp.dma_start(out[:], src).then_inc(loaded, 16)
            for b in range(B):
                sp.wait_ge(y_added, (b + 1) * TB)
                sp.dma_start(io["out"][:, b * TB:(b + 1) * TB, :], t.x[:, b * TB:(b + 1) * TB, :]).then_inc(stored, 16)
            sp.wait_ge(stored, 16 * B)

        @block.gpsimd
        def _(pool):
            for b in range(B):
                xv = xr[:, b % 2, :].rearrange("p (c s) -> p c s", c=KC)
                if b >= 2:
                    pool.wait_ge(made, (2 * (b - 2) + 1) * OC)
                pool.wait_ge(x_rest, b + 1)
                nc.gpsimd.tensor_copy(xp[:, b % 2, 1, :, :], xv).then_inc(x_mid, 1)
                pool.wait_ge(x_mid, b + 1)
                nc.gpsimd.tensor_tensor(xp[:, b % 2, 2, :, :], xv, xp[:, b % 2, 1, :, :], ALU.subtract).then_inc(x_low, 1)

        @block.tensor
        def _(pe):
            pe.wait_ge(w_ready, 3)
            for b in range(B):
                for layer, (w, src, n) in enumerate(((w0, xp[:, b % 2, :, :, :], KC), (w1, hp[0], OC))):
                    if layer == 0:
                        pe.wait_ge(x_low, b + 1)
                    else:
                        pe.wait_ge(low, (2 * b + 1) * OC)
                    for c in range(OC):
                        u = (2 * b + layer) * OC + c
                        if u >= 4:
                            pe.wait_ge(kept, u - 3)
                        for k in range(n):
                            for part in range(3):
                                last = nc.tensor.matmul(t.ps[:, u % 4, :], w[:, k, c * P:(c + 1) * P], src[:, part, k, :],
                                                        start=k == 0 and part == 0, stop=k == n - 1 and part == 2)
                        last.then_inc(made, 1)
                pe.wait_ge(low, (2 * b + 2) * OC)
                for i in range(TB):
                    j = b * TB + i
                    if j >= 4:
                        pe.wait_ge(y_added, j - 3)
                    for k in range(OC):
                        for part in range(3):
                            last = nc.tensor.matmul(t.ps[:, 4 + j % 4, 0:D], hp[1][:, part, k, i * P:(i + 1) * P], w2[:, k, :],
                                                    start=k == 0 and part == 0, stop=k == OC - 1 and part == 2)
                    last.then_inc(y_ready, 1)

        @block.scalar
        def _(act):
            act.wait_ge(w_ready, 3)

            def x_parts(b):
                if b >= 2:
                    act.wait_ge(made, (2 * (b - 2) + 1) * OC)
                nc.scalar.copy(xp[:, b % 2, 0, :, :], t.xnT[:, :, b * S:(b + 1) * S]).then_inc(x_high, 1)

            x_parts(0)
            for b in range(B):
                for layer in range(2):
                    if layer == 0 and b + 1 < B:
                        x_parts(b + 1)
                    for c in range(OC):
                        u = (2 * b + layer) * OC + c
                        act.wait_ge(made, u + 1)
                        if u >= 2:
                            act.wait_ge(left, u - 1)
                        nc.scalar.activation(hf[:, u % 2, :], t.ps[:, u % 4, :], ACT.Relu, scale=sv4[:, layer:layer + 1])\
                            .then_inc(kept, 1)
                        act.wait_ge(kept, u + 1)
                        if c == 0 and b:
                            if layer == 0:
                                act.wait_ge(made, 2 * b * OC)
                            else:
                                act.wait_ge(y_ready, b * TB)
                        nc.scalar.copy(hp[layer][:, 0, c, :], hf[:, u % 2, :]).then_inc(high, 1)

        @block.vector
        def _(dve):
            dve.wait_ge(loaded, 16 * len(loads))
            nc.vector.tensor_tensor(w0[:], signs[0][:, 0:KC, :], signs[0][:, KC:2 * KC, :], ALU.subtract)
            nc.vector.tensor_scalar(w1[:], signs[1], 2.0, -1.0, ALU.mult, ALU.add).then_inc(w_ready, 1)
            nc.vector.tensor_scalar(w2[:], signs[2], 2.0, -1.0, ALU.mult, ALU.add).then_inc(w_ready, 1)
            nc.vector.tensor_scalar(sv4[:, 0:1], sv[:, 0:1], 4.0, None, ALU.mult)
            nc.vector.tensor_scalar(sv4[:, 1:2], sv[:, 1:2], 2.0, None, ALU.mult).then_inc(w_ready, 1)

            def x_parts(b):
                xv = xr[:, b % 2, :].rearrange("p (c s) -> p c s", c=KC)
                dve.wait_ge(x_high, b + 1)
                if b >= 2:
                    dve.wait_ge(x_low, b - 1)
                nc.vector.tensor_tensor(xv, t.xnT[:, :, b * S:(b + 1) * S], xp[:, b % 2, 0, :, :], ALU.subtract)\
                    .then_inc(x_rest, 1)

            x_parts(0)
            for b in range(B):
                for layer in range(2):
                    if layer == 0 and b + 1 < B:
                        x_parts(b + 1)
                    for c in range(OC):
                        u = (2 * b + layer) * OC + c
                        dve.wait_ge(high, u + 1)
                        nc.vector.tensor_tensor(hr[:, u % 2, :], hf[:, u % 2, :], hp[layer][:, 0, c, :], ALU.subtract)\
                            .then_inc(left, 1)
                        dve.wait_ge(left, u + 1)
                        nc.vector.tensor_copy(hp[layer][:, 1, c, :], hr[:, u % 2, :]).then_inc(mid, 1)
                        dve.wait_ge(mid, u + 1)
                        nc.vector.tensor_tensor(hp[layer][:, 2, c, :], hr[:, u % 2, :], hp[layer][:, 1, c, :], ALU.subtract)\
                            .then_inc(low, 1)
                for i in range(TB):
                    j = b * TB + i
                    dve.wait_ge(y_ready, j + 1)
                    nc.vector.scalar_tensor_tensor(t.x[:, j, :], t.ps[:, 4 + j % 4, 0:D], sv[:, 2:3], t.x[:, j, :],
                                                   ALU.mult, ALU.add).then_inc(y_added, 1)


class State:
    pass


STAGES = 5


def build(nc, io):
    with ExitStack() as stack:
        sc = Scope(nc, "main", stack)
        t = State()
        t.ps = stack.enter_context(nc.psum_tensor("ps", [P, 8, 512], F32))
        t.const = sc.sb("const", [P, NCONST])
        t.x = sc.sb("x", [P, T, D])
        t.xnT = sc.sb("xnT", [P, KC, B * S])
        t.gates = sc.sb("gates", [P, E, T])
        t.stats = sc.sb("stats", [P, T, 6])
        t.mv = sc.sb("mv", [P, T, 2])
        t.std = sc.sb("std", [P, T])
        t.rstd = sc.sb("rstd", [P, T])
        t.ident = t.const[:, CONST["ident"]]
        t.eps = t.const[:, CONST["eps"]]
        t.one = t.const[:, CONST["one"]]
        t.heads = {16: t.const[:, CONST["heads16"]], 8: t.const[:, CONST["heads8"]]}

        for layer in range(2):
            with ExitStack() as inner:
                si = Scope(nc, f"context{layer}", inner)
                t.ctxT = si.sb("ctxT", [P, KC, NCTX])
                t.ctxT2 = si.sb("ctxT2", [P, KC, B, 2, S2])
                t.ctxnT = si.sb("ctxnT", [P, KC, NCTX])
                t.bound = si.sb("bound", [P, NCTX])
                t.pre = si.sb("pre", [P, 2, KC])
                if layer == 0:
                    rot = si.sb("rot", [P, 2, S])
                    t.rot = [rot[:, 0, :], rot[:, 1, :]]
                    context_stage(nc, t, io, "load0", [(t.const, io["const"]), (t.x, io["x"]), (rot, io["rot"])])
                    layernorm_stage(nc, t, "ln0")
                    context_attention(nc, t, "attn0", H0, io["a0"], ("q", "qrot", "k", "krot", "v", "o"),
                                      (D // H0) ** -0.5, True, t.ctxT, None, None)
                elif STAGES >= 3:
                    context_stage(nc, t, io, "load1", [])
                    layernorm_stage(nc, t, "ln2", (t.pre[:, 0, :], t.pre[:, 1, :]), 2)
                    context_attention(nc, t, "attn1", H1, io["a1"], ("q", "k", "v", "o"), D ** -0.5, False, t.ctxnT,
                                      1e4 * D ** 0.5, io["a1_rows"])
            if layer == 0 and STAGES >= 2:
                layernorm_stage(nc, t, "ln1")
                router_stage(nc, t, io)
                expert_stage(nc, t, io)
        if STAGES >= 4:
            layernorm_stage(nc, t, "ln3")
            sign_stage(nc, t, io)
        else:
            done = sc.sem("done")
            with nc.Block() as block:
                @block.sync
                def _(sp):
                    sp.dma_start(io["out"], t.x[:]).then_inc(done, 16)
                    sp.wait_ge(done, 16)


def constants():
    const = np.zeros((P, NCONST), np.float32)
    rows = np.arange(P)
    const[:, CONST["ident"]] = np.eye(P)
    for heads in (H0, H1):
        const[:, CONST[f"heads{heads}"]] = rows[:, None] // (D // heads) == np.arange(heads // KC)[None]
    const[:, CONST["first"]] = np.arange(E, 0, -1)
    const[:, CONST["eps"]] = EPS
    const[:, CONST["one"]] = 1
    dh = D // H0
    div = np.exp(np.arange(0, dh, 2, dtype=np.float32) * np.float32(-np.log(10000.0) / dh))
    angle = (np.arange(S, dtype=np.float32)[:, None] * div).T
    which = rows % dh
    sign = np.where(which < dh // 2, -1, 1).astype(np.float32)[:, None]
    rot = np.stack([np.cos(angle)[which % (dh // 2)], np.sin(angle)[which % (dh // 2)] * sign], 1)
    return const, rot.astype(np.float32)


def lay_out(i):
    f = lambda name: np.asarray(i[name])
    chunks = lambda w: w.reshape(w.shape[0] // P, P, -1).transpose(1, 0, 2)
    rep = lambda row: np.broadcast_to(row, (P,) + row.shape)
    cols = lambda v: v.reshape(-1, P).T
    a = {}
    a["const"], a["rot"] = constants()
    a["x"] = f("x").reshape(T, P, D).transpose(1, 0, 2)
    a["ctx"] = f("ctx_1024").reshape(NCTX // P, P, D).transpose(1, 0, 2)
    a["mask"] = rep(f("mask_BxS2_bf1").view(np.uint8).reshape(NCTX))
    a["pre"] = np.stack([cols(f("L1_xattn_pre_g")), cols(f("L1_xattn_pre_b"))], 1)
    dh = D // H0
    turn = (np.arange(D) // dh) * dh + (np.arange(D) + dh // 2) % dh
    wq, wkv, wo = f("L0_xattn_Wq"), f("L0_xattn_Wkv"), f("L0_xattn_Wout")
    a["a0"] = np.stack([chunks(w) for w in (wq, wq[:, turn], wkv[:, :D], wkv[:, :D][:, turn], wkv[:, D:], wo)], 2)
    a["a1"] = np.stack([chunks(f(f"L1_xattn_W{n}")) for n in "qkvo"], 2)
    a["a1_rows"] = np.stack([rep(f("L1_xattn_ln_g")), rep(f("L1_xattn_ln_b"))], 1)
    a["rW1"] = chunks(f("L0_ffn_rW1").T)
    a["r_rows"] = np.concatenate([rep(f("L0_ffn_rb1")), rep(f("L0_ffn_rb2"))], 1)
    a["r_cols"] = np.concatenate([f("L0_ffn_ln_g")[:, None], f("L0_ffn_ln_b")[:, None], f("L0_ffn_rW2").T], 1)
    a["ob"] = f("L0_ffn_ob")
    order = np.arange(D).reshape(KC, HC, DH).transpose(0, 2, 1).reshape(KC, P)
    qk, biases = [], []
    for n in "qk":
        w = f(f"L0_ffn_{n}W").transpose(0, 2, 1)
        w = w.reshape(E, KC, P, D)[:, :, :, order]
        qk.append(w.transpose(0, 2, 3, 1, 4).reshape(E, P, -1))
        biases.append(f(f"L0_ffn_{n}b")[:, order].transpose(0, 2, 1))
    a["e_qk"] = np.concatenate(qk + biases, 2)
    wide = lambda w: w.transpose(0, 2, 1).reshape(E, KC, P, D).transpose(0, 2, 1, 3).reshape(E, P, KC * D)
    a["e_v"] = np.concatenate([wide(f("L0_ffn_vW")), np.broadcast_to(f("L0_ffn_vb")[:, None], (E, P, D))], 2)
    a["e_o"] = wide(f("L0_ffn_oW"))
    for n in range(3):
        a[f"k{n}"] = np.ascontiguousarray(chunks(f(f"L1_ffn_k{n}").view(np.uint8))).view(np.uint32)
    a["sv"] = np.stack([np.broadcast_to(f(f"L1_ffn_s{n}").reshape(()), (P,)) for n in range(3)], 1)
    return {n: np.ascontiguousarray(v) for n, v in a.items()}


def kernel(**inputs):
    import concourse.bacc as bacc
    from concourse.bass_utils import run_bass_kernel_spmd

    arrays = lay_out(inputs)
    nc = bacc.Bacc("TRN2", target_bir_lowering=False, num_devices=1)
    io = {n: nc.dram_tensor(f"in_{n}", v.shape, mybir.dt.from_np(v.dtype), kind="ExternalInput").ap()
          for n, v in arrays.items()}
    io["out"] = nc.dram_tensor("out_x", (P, T, D), F32, kind="ExternalOutput").ap()
    build(nc, io)
    r = run_bass_kernel_spmd(nc, [{f"in_{n}": v for n, v in arrays.items()}], core_ids=[0])
    out = r.results[0]["out_x"]
    return np.ascontiguousarray(out.transpose(1, 0, 2)).reshape(B, S, D)
```

```python
from contextlib import ExitStack

import numpy as np

import concourse.bass as bass
from concourse import mybir

F32 = mybir.dt.float32
BF16 = mybir.dt.bfloat16
U8 = mybir.dt.uint8
U32 = mybir.dt.uint32
ALU = mybir.AluOpType
ACT = mybir.ActivationFunctionType
AX = mybir.AxisListType

P = 128
B, S, D = 4, 512, 256
T = B * S // P
TB = S // P
KC = D // P
S2 = 64
NCTX = B * S2
H0, H1 = 16, 8
E, HE, DH = 8, 16, 16
R1 = D // 2
FF = 1024
OC = FF // P
EPS = 1e-5
LOWEST = -3.4028234663852886e38
HC = HE // KC
G4 = 4
RING = 8
Q_PARTS, K_PARTS = (0, 0, 0, 1, 1, 2), (0, 1, 2, 0, 1, 0)
SPLIT_ROWS = len(Q_PARTS) * DH
MAX_ROWS = SPLIT_ROWS + 2


def bcast(ap, axis, n):
    ap = ap.unsqueeze(axis)
    shape = list(ap.shape)
    shape[axis] = n
    return ap.broadcast_to(shape)


def by(ap, n):
    dims = " ".join("abcdef"[:len(ap.shape) - 1])
    return ap.rearrange(f"{dims} (g n) -> {dims} g n", n=n)


class Steps:

    def __init__(self, engine, semaphore):
        self.engine, self.semaphore, self.count = engine, semaphore, 0

    def did(self, instruction):
        instruction.then_inc(self.semaphore, 1)
        self.count += 1

    def wait(self):
        self.engine.wait_ge(self.semaphore, self.count)


CONST_WIDTHS = (("ident", P), ("heads16", H0 // KC), ("heads8", H1 // KC), ("first", E), ("eps", 1), ("one", 1))
CONST = {name: slice(sum(w for _, w in CONST_WIDTHS[:i]), sum(w for _, w in CONST_WIDTHS[:i + 1]))
         for i, (name, _) in enumerate(CONST_WIDTHS)}
NCONST = sum(w for _, w in CONST_WIDTHS)


class Scope:

    def __init__(self, nc, name, stack):
        self.nc, self.name, self.stack = nc, name, stack

    def sem(self, name):
        return self.stack.enter_context(self.nc.semaphore(f"{self.name}_{name}"))

    def sems(self, names):
        return [self.sem(n) for n in names.split()]

    def sb(self, name, shape, dt=F32):
        return self.stack.enter_context(self.nc.sbuf_tensor(f"{self.name}_{name}", shape, dt))


def context_stage(nc, t, io, name, more, ahead):
    with ExitStack() as stack:
        sc = Scope(nc, name, stack)
        loaded, own, var_ready, std_ready, normed, turned, evacuated = sc.sems(
            "loaded own var_ready std_ready normed turned evacuated")
        cx = sc.sb("cx", [P, NCTX // P, D])
        cn = sc.sb("cn", [P, NCTX // P, D])
        mask = sc.sb("mask", [P, NCTX], U8)
        loads = more + [(cx, io["ctx"]), (mask, io["mask"]), (t.pre, io["pre"])]
        block = stack.enter_context(nc.Block())

        @block.sync
        def _(sp):
            for out, src in loads:
                sp.dma_start(out[:], src).then_inc(loaded, 16)
            for out, src, semaphore in ahead:
                sp.dma_start(out[:], src).then_inc(semaphore, 16)

        @block.vector
        def _(dve):
            dve.wait_ge(loaded, 16 * len(loads))
            steps = Steps(dve, own)
            for i in range(NCTX // P):
                steps.did(nc.vector.bn_stats(t.stats[:, i, :], cx[:, i, :]))
            steps.did(nc.vector.tensor_scalar(t.bound[:], mask[:], 0.5, -LOWEST, ALU.subtract, ALU.mult))
            steps.wait()
            steps.did(nc.vector.tensor_scalar(t.bound[:], t.bound[:], 2.0, None, ALU.mult))
            for i in range(NCTX // P):
                last = nc.vector.bn_aggr(t.mv[:, i, :], t.stats[:, i, :])
            last.then_inc(var_ready, 1)
            dve.wait_ge(std_ready, 1)
            steps.did(nc.vector.reciprocal(t.rstd[:, 0:2], t.std[:, 0:2]))
            steps.wait()
            for i in range(NCTX // P):
                last = nc.vector.tensor_scalar(cn[:, i, :], cx[:, i, :], t.mv[:, i, 0:1], t.rstd[:, i:i + 1],
                                               ALU.subtract, ALU.mult)
            last.then_inc(normed, 1)

        @block.scalar
        def _(act):
            act.wait_ge(var_ready, 1)
            nc.scalar.activation(t.std[:, 0:2], t.mv[:, 0:2, 1], ACT.Sqrt, bias=t.eps).then_inc(std_ready, 1)
            for c in range(KC):
                act.wait_ge(turned, c + 1)
                src = t.ps[:, c, 0:NCTX]
                nc.scalar.copy(t.ctxT[:, c, :], src)
                for a in range(2):
                    nc.scalar.copy(t.ctxT2[:, c, :, a, :], src.rearrange("p (b k) -> p b k", b=B))
            for c in range(KC):
                act.wait_ge(turned, KC + c + 1)
                nc.scalar.activation(t.ctxnT[:, c, :], t.ps[:, KC + c, 0:NCTX], ACT.Identity,
                                     bias=t.pre[:, 1, c:c + 1], scale=t.pre[:, 0, c:c + 1])

        @block.tensor
        def _(pe):
            pe.wait_ge(loaded, 16 * len(loads))
            for n, src in enumerate((cx, cn)):
                if n:
                    pe.wait_ge(normed, 1)
                for c in range(KC):
                    for i in range(NCTX // P):
                        last = nc.tensor.transpose(t.ps[:, n * KC + c, i * P:(i + 1) * P], src[:, i, c * P:(c + 1) * P],
                                                   t.ident)
                    last.then_inc(turned, 1)


def layernorm_stage(nc, t, name, affine=None, rounds=1):
    with ExitStack() as stack:
        sc = Scope(nc, name, stack)
        var_ready, std_ready, xn_ready, turned, evacuated, own = sc.sems(
            "var_ready std_ready xn_ready turned evacuated own")
        xn = sc.sb("xn", [P, T, D])
        block = stack.enter_context(nc.Block())

        @block.vector
        def _(dve):
            steps = Steps(dve, own)
            for r in range(rounds):
                src = t.x if r == 0 else xn
                for b in range(B):
                    if r:
                        dve.wait_ge(xn_ready, b + 1)
                    for k in range(b * TB, (b + 1) * TB):
                        steps.did(nc.vector.bn_stats(t.stats[:, k, :], src[:, k, :]))
                    steps.wait()
                    for k in range(b * TB, (b + 1) * TB):
                        last = nc.vector.bn_aggr(t.mv[:, k, :], t.stats[:, k, :])
                    last.then_inc(var_ready, 1)
                for b in range(B):
                    dve.wait_ge(std_ready, r * B + b + 1)
                    steps.did(nc.vector.reciprocal(t.rstd[:, b * TB:(b + 1) * TB], t.std[:, b * TB:(b + 1) * TB]))
                    steps.wait()
                    for k in range(b * TB, (b + 1) * TB):
                        last = nc.vector.tensor_scalar(xn[:, k, :], src[:, k, :], t.mv[:, k, 0:1], t.rstd[:, k:k + 1],
                                                       ALU.subtract, ALU.mult)
                    last.then_inc(xn_ready, 1)

        @block.scalar
        def _(act):
            for j in range(rounds * B):
                b = j % B
                act.wait_ge(var_ready, j + 1)
                nc.scalar.activation(t.std[:, b * TB:(b + 1) * TB], t.mv[:, b * TB:(b + 1) * TB, 1], ACT.Sqrt,
                                     bias=t.eps).then_inc(std_ready, 1)
            for b in range(B):
                for c in range(KC):
                    act.wait_ge(turned, b * KC + c + 1)
                    out, bank = t.xnT[:, c, b * S:(b + 1) * S], t.ps[:, b * KC + c, :]
                    if affine is None:
                        nc.scalar.copy(out, bank)
                    else:
                        nc.scalar.activation(out, bank, ACT.Identity, bias=affine[1][:, c:c + 1],
                                             scale=affine[0][:, c:c + 1])

        @block.tensor
        def _(pe):
            for b in range(B):
                pe.wait_ge(xn_ready, (rounds - 1) * B + b + 1)
                for c in range(KC):
                    for i in range(TB):
                        last = nc.tensor.transpose(t.ps[:, b * KC + c, i * P:(i + 1) * P],
                                                   xn[:, b * TB + i, c * P:(c + 1) * P], t.ident)
                    last.then_inc(turned, 1)


def context_attention(nc, t, name, heads, W, W_in, order, scale, rotary, keys_in, limit, rows, beside=None):
    dh, hc = D // heads, heads // KC
    NK = heads * S2
    NC = NK // KC
    NB = NK // P
    sin_cos = ("cos", "sin") if rotary else ("cos",)
    with ExitStack() as outer:
        so = Scope(nc, name, outer)
        w = {n: W[:, :, j, :] for j, n in enumerate(order)}
        qT = so.sb("qT", [P, KC, B * S])
        kd = so.sb("kd", [P, B, KC, hc, S2])
        vd = so.sb("vd", [P, B, D])
        o = so.sb("o", [P, T, D])
        kT = so.sb("kT", [P, KC, NCTX])

        with ExitStack() as stack:
            sc = Scope(nc, f"{name}_qkv", stack)
            v_ready, v_taken, made, taken, zeroed, k_sum = sc.sems("v_ready v_taken made taken zeroed k_sum")
            part = sc.sb("part", [P, 2, 2, S])
            jobs = [("k", None, c) for c in range(KC)] + [("q", b, c) for b in range(B) for c in range(KC)]

            def width(job):
                return NCTX if job[0] == "k" else S

            def target(job):
                kind, b, c = job
                return kT[:, c, :] if kind == "k" else qT[:, c, b * S:(b + 1) * S]

            block = stack.enter_context(nc.Block())

            @block.tensor
            def _(pe):
                pe.wait_ge(W_in, 32 if rotary else 16)
                for b in range(B):
                    for kc in range(KC):
                        last = nc.tensor.matmul(t.ps[:, b, 0:D], t.ctxT2[:, kc, b, :, :].rearrange("p a k -> p (a k)"),
                                                w["v"][:, kc, :], start=kc == 0, stop=kc == KC - 1)
                    last.then_inc(v_ready, 1)
                pe.wait_ge(v_taken, B)
                for j, job in enumerate(jobs):
                    kind, b, c = job
                    n = width(job)
                    if j >= 4:
                        pe.wait_ge(taken, j - 3)
                    for a in range(2 if rotary else 1):
                        src = keys_in if kind == "k" else t.xnT
                        for kc in range(KC):
                            rhs = src[:, kc, :] if kind == "k" else src[:, kc, b * S:(b + 1) * S]
                            last = nc.tensor.matmul(t.ps[:, 2 * (j % 4) + a, 0:n],
                                                    w[kind + ("rot" if a else "")][:, kc, c * P:(c + 1) * P], rhs,
                                                    start=kc == 0, stop=kc == KC - 1)
                    last.then_inc(made, 1)

            @block.vector
            def _(dve):
                nc.vector.memset(vd[:], 0.0).then_inc(zeroed, 1)
                dve.wait_ge(zeroed, 1)
                for b in range(B):
                    dve.wait_ge(v_ready, b + 1)
                    for half in range(2):
                        r = slice(half * 64, half * 64 + 64)
                        last = nc.vector.tensor_copy(by(by(vd[r, b, :], 2 * dh), dh)[:, :, half, :],
                                                     by(by(t.ps[r, b, 0:D], 2 * dh), dh)[:, :, half, :])
                    last.then_inc(v_taken, 1)
                if rotary:
                    dve.wait_ge(W_in, 32)
                    for j, job in enumerate(jobs):
                        n = width(job)
                        dve.wait_ge(made, j + 1)
                        if j >= 2:
                            dve.wait_ge(k_sum, j - 1)
                        for a in range(2):
                            src, table = t.ps[:, 2 * (j % 4) + a, 0:n], t.rot[a]
                            out = part[:, j % 2, a, 0:n]
                            if job[0] == "k":
                                src, out, table = by(src, S2), by(out, S2), bcast(table[:, 0:S2], 1, B)
                            last = nc.vector.tensor_tensor(out, src, table, ALU.mult)
                        last.then_inc(taken, 1)
                if beside:
                    beside(dve)
                dve.wait_ge(k_sum if rotary else taken, KC)
                for b in range(B):
                    for c in range(KC):
                        nc.vector.tensor_tensor(kd[:, b, c, :, :], bcast(kT[:, c, b * S2:(b + 1) * S2], 1, hc),
                                                bcast(t.heads[heads], 2, S2), ALU.mult)

            if rotary:
                @block.gpsimd
                def _(pool):
                    for j, job in enumerate(jobs):
                        pool.wait_ge(taken, j + 1)
                        n = width(job)
                        nc.gpsimd.tensor_tensor(target(job), part[:, j % 2, 0, 0:n], part[:, j % 2, 1, 0:n], ALU.add)\
                            .then_inc(k_sum, 1)
            else:
                @block.scalar
                def _(act):
                    for j, job in enumerate(jobs):
                        act.wait_ge(made, j + 1)
                        nc.scalar.copy(target(job), t.ps[:, 2 * (j % 4), 0:width(job)]).then_inc(taken, 1)

        TURN, LAG, DEEP = 2, 3, 4
        with ExitStack() as stack:
            sc = Scope(nc, f"{name}_attend", stack)
            scores_ready, bounded, max_ready, centred, exp_ready, p_turned, p_evacuated, o_ready, o_taken, sum_ready, rsum_ready = \
                sc.sems("scores_ready bounded max_ready centred exp_ready p_turned p_evacuated o_ready o_taken "
                        "sum_ready rsum_ready")
            prob = sc.sb("prob", [P, DEEP, NK])
            probT = sc.sb("probT", [P, 2, NB * P])
            mx = sc.sb("mx", [P, DEEP, heads])
            total = sc.sb("total", [P, DEEP, heads])
            rsum = sc.sb("rsum", [P, DEEP, heads])
            block = stack.enter_context(nc.Block())

            @block.tensor
            def _(pe):
                for i in range(T + LAG):
                    if i < T:
                        b = i // TB
                        if i >= 2:
                            pe.wait_ge(bounded, i - 1)
                        for c in range(KC):
                            last = nc.tensor.matmul(t.ps[:, 2 * (i % 2) + c, 0:NC], qT[:, c, i * P:(i + 1) * P],
                                                    kd[:, b, c, :, :].rearrange("p h k -> p (h k)"), start=True, stop=True)
                        last.then_inc(scores_ready, 1)
                    if TURN <= i < T + TURN:
                        j = i - TURN
                        pe.wait_ge(exp_ready, j + 1)
                        if j:
                            pe.wait_ge(p_evacuated, j)
                        for n in range(NB):
                            last = nc.tensor.transpose(t.ps[:, 4 + n // 4, (n % 4) * P:(n % 4 + 1) * P],
                                                       prob[:, j % DEEP, n * P:(n + 1) * P], t.ident)
                        last.then_inc(p_turned, 1)
                    if i >= LAG:
                        j = i - LAG
                        pe.wait_ge(p_evacuated, j + 1)
                        if j >= 2:
                            pe.wait_ge(o_taken, j - 1)
                        for n in range(NB):
                            cols = slice(n * 2 * dh, (n + 1) * 2 * dh)
                            last = nc.tensor.matmul(t.ps[:, 6 + j % 2, cols], probT[:, j % 2, n * P:(n + 1) * P],
                                                    vd[:, j // TB, cols], start=True, stop=True)
                        last.then_inc(o_ready, 1)

            @block.vector
            def _(dve):
                for i in range(T + LAG):
                    if i < T:
                        dve.wait_ge(scores_ready, i + 1)
                        if i >= DEEP:
                            dve.wait_ge(p_turned, i - DEEP + 1)
                        banks = t.ps[:, 2 * (i % 2):2 * (i % 2) + KC, 0:NC]
                        out = prob[:, i % DEEP, :].rearrange("p (c n) -> p c n", c=KC)
                        if limit is None:
                            b = i // TB
                            for c in range(KC):
                                ins = nc.vector.tensor_tensor(by(out[:, c, :], S2), by(banks[:, c, :], S2),
                                                              bcast(t.bound[:, b * S2:(b + 1) * S2], 1, hc), ALU.min)
                        else:
                            ins = nc.vector.tensor_scalar(out, banks, limit, -limit, ALU.min, ALU.max)
                        ins.then_inc(bounded, 1)
                        dve.wait_ge(bounded, i + 1)
                        nc.vector.tensor_reduce(mx[:, i % DEEP, :], by(prob[:, i % DEEP, :], S2), AX.X, ALU.max)\
                            .then_inc(max_ready, 1)
                    if TURN <= i < T + TURN:
                        j = i - TURN
                        dve.wait_ge(exp_ready, j + 1)
                        nc.vector.tensor_reduce(total[:, j % DEEP, :], by(prob[:, j % DEEP, :], S2), AX.X, ALU.add)\
                            .then_inc(sum_ready, 1)
                        dve.wait_ge(sum_ready, j + 1)
                        nc.vector.reciprocal(rsum[:, j % DEEP, :], total[:, j % DEEP, :]).then_inc(rsum_ready, 1)
                    if i >= LAG:
                        j = i - LAG
                        dve.wait_ge(o_ready, j + 1)
                        dve.wait_ge(rsum_ready, j + 1)
                        nc.vector.tensor_tensor(by(o[:, j, :], dh), by(t.ps[:, 6 + j % 2, 0:D], dh),
                                                bcast(rsum[:, j % DEEP, :], 2, dh), ALU.mult).then_inc(o_taken, 1)

            @block.gpsimd
            def _(pool):
                for i in range(T):
                    pool.wait_ge(max_ready, i + 1)
                    pr = by(prob[:, i % DEEP, :], S2)
                    nc.gpsimd.tensor_tensor(pr, pr, bcast(mx[:, i % DEEP, :], 2, S2), ALU.subtract).then_inc(centred, 1)

            @block.scalar
            def _(act):
                for i in range(T + TURN):
                    if i >= TURN:
                        j = i - TURN
                        act.wait_ge(p_turned, j + 1)
                        if j >= 2:
                            act.wait_ge(o_ready, j - 1)
                        n = NB * P // 512
                        nc.scalar.copy(probT[:, j % 2, :].rearrange("p (a n) -> p a n", a=n), t.ps[:, 4:4 + n, :])\
                            .then_inc(p_evacuated, 1)
                    if i < T:
                        act.wait_ge(centred, i + 1)
                        nc.scalar.activation(prob[:, i % DEEP, :], prob[:, i % DEEP, :], ACT.Exp, scale=scale)\
                            .then_inc(exp_ready, 1)

        with ExitStack() as stack:
            sc = Scope(nc, f"{name}_out", stack)
            var_ready, std_ready, own, normed, turned, evacuated, y_ready, y_taken, gelu_ready, rows_in, x_added = sc.sems(
                "var_ready std_ready own normed turned evacuated y_ready y_taken gelu_ready rows_in x_added")
            DEEP_OUT = 6
            oT = sc.sb("oT", [P, 2, KC * P])
            gl = sc.sb("gl", [P, DEEP_OUT, D])
            if rows is not None:
                gb = sc.sb("gb", [P, 2, D])
            block = stack.enter_context(nc.Block())

            @block.sync
            def _(sp):
                if rows is not None:
                    sp.dma_start(gb[:], rows).then_inc(rows_in, 16)

            @block.tensor
            def _(pe):
                for i in range(T + 1):
                    if i < T:
                        if rows is not None:
                            pe.wait_ge(normed, i // TB + 1)
                        if i >= 2:
                            pe.wait_ge(evacuated, i - 1)
                        for c in range(KC):
                            last = nc.tensor.transpose(t.ps[:, i % 2, c * P:(c + 1) * P], o[:, i, c * P:(c + 1) * P], t.ident)
                        last.then_inc(turned, 1)
                    if i:
                        j = i - 1
                        pe.wait_ge(evacuated, j + 1)
                        if j >= 2:
                            pe.wait_ge(y_taken if rows is None else gelu_ready, j - 1)
                        for kc in range(KC):
                            last = nc.tensor.matmul(t.ps[:, 2 + j % 2, 0:D], oT[:, j % 2, kc * P:(kc + 1) * P],
                                                    w["o"][:, kc, :], start=kc == 0, stop=kc == KC - 1)
                        last.then_inc(y_ready, 1)

            @block.scalar
            def _(act):
                if rows is not None:
                    act.wait_ge(var_ready, 1)
                    nc.scalar.activation(t.std[:], t.mv[:, :, 1], ACT.Sqrt, bias=t.eps).then_inc(std_ready, 1)
                for i in range(T + 1):
                    if i < T:
                        act.wait_ge(turned, i + 1)
                        if i >= 2:
                            act.wait_ge(y_ready, i - 1)
                        nc.scalar.copy(oT[:, i % 2, :], t.ps[:, i % 2, 0:KC * P]).then_inc(evacuated, 1)
                    if i and rows is not None:
                        j = i - 1
                        act.wait_ge(y_ready, j + 1)
                        if j >= DEEP_OUT:
                            act.wait_ge(y_taken, j - DEEP_OUT + 1)
                        nc.scalar.activation(gl[:, j % DEEP_OUT, :], t.ps[:, 2 + j % 2, 0:D], ACT.Gelu).then_inc(gelu_ready, 1)

            @block.vector
            def _(dve):
                steps = Steps(dve, own)
                if rows is not None:
                    for i in range(T):
                        steps.did(nc.vector.bn_stats(t.stats[:, i, :], o[:, i, :]))
                    steps.wait()
                    for i in range(T):
                        last = nc.vector.bn_aggr(t.mv[:, i, :], t.stats[:, i, :])
                    last.then_inc(var_ready, 1)
                    dve.wait_ge(rows_in, 16)
                    dve.wait_ge(std_ready, 1)
                    steps.did(nc.vector.reciprocal(t.rstd[:], t.std[:]))
                    steps.wait()

                def add(j, y):
                    nc.vector.tensor_tensor(t.x[:, j, :], t.x[:, j, :], y, ALU.add).then_inc(y_taken, 1)

                if rows is None:
                    for j in range(T):
                        dve.wait_ge(y_ready, j + 1)
                        add(j, t.ps[:, 2 + j % 2, 0:D])
                    return

                for b in range(B + 1):
                    if b < B:
                        v = o[:, b * TB:(b + 1) * TB, :]
                        for i in range(b * TB, (b + 1) * TB):
                            steps.did(nc.vector.tensor_scalar(o[:, i, :], o[:, i, :], t.mv[:, i, 0:1], t.rstd[:, i:i + 1],
                                                              ALU.subtract, ALU.mult))
                        steps.wait()
                        steps.did(nc.vector.tensor_tensor(v, v, bcast(gb[:, 0, :], 1, TB), ALU.mult))
                        steps.wait()
                        nc.vector.tensor_tensor(v, v, bcast(gb[:, 1, :], 1, TB), ALU.add).then_inc(normed, 1)
                    if b:
                        dve.wait_ge(x_added, b)
                        for j in range((b - 1) * TB, b * TB):
                            dve.wait_ge(gelu_ready, j + 1)
                            add(j, gl[:, j % DEEP_OUT, :])

            if rows is not None:
                @block.gpsimd
                def _(pool):
                    for b in range(B):
                        xs = slice(b * TB, (b + 1) * TB)
                        pool.wait_ge(normed, b + 1)
                        nc.gpsimd.tensor_tensor(t.x[:, xs, :], t.x[:, xs, :], o[:, xs, :], ALU.add).then_inc(x_added, 1)


def router_stage(nc, t, io):
    with ExitStack() as stack:
        sc = Scope(nc, "router", stack)
        loaded, own, h_ready, var_ready, std_ready, normed, turned, relu_ready, logits_ready, logits_in, exp_ready, \
            gates_ready, gt_turned, gt_ready, bias_ready, centred = sc.sems(
                "loaded own h_ready var_ready std_ready normed turned relu_ready logits_ready logits_in exp_ready "
                "gates_ready gt_turned gt_ready bias_ready centred")
        w1 = sc.sb("w1", [P, KC, R1])
        rows = sc.sb("rows", [P, R1 + E])
        cols = sc.sb("cols", [P, 2 + E])
        ob = sc.sb("ob", [E, D])
        h = sc.sb("h", [P, T, R1])
        hT = sc.sb("hT", [P, T * P])
        lg = sc.sb("lg", [P, T, E])
        pr = sc.sb("pr", [P, T, E])
        cand = sc.sb("cand", [P, T, E])
        pick = sc.sb("pick", [P, 2, T, E])
        one = sc.sb("one", [P, T])
        gT = sc.sb("gT", [E, T * P])
        loads = ((w1, io["rW1"]), (rows, io["r_rows"]), (cols, io["r_cols"]), (ob, io["ob"]))
        block = stack.enter_context(nc.Block())

        @block.sync
        def _(sp):
            for out, src in loads:
                sp.dma_start(out[:], src).then_inc(loaded, 16)

        @block.tensor
        def _(pe):
            pe.wait_ge(loaded, 16 * len(loads))
            for b in range(B):
                for i in range(TB):
                    k = b * TB + i
                    for kc in range(KC):
                        last = nc.tensor.matmul(t.ps[:, b, i * R1:(i + 1) * R1], t.xnT[:, kc, k * P:(k + 1) * P],
                                                w1[:, kc, :], start=kc == 0, stop=kc == KC - 1)
                last.then_inc(h_ready, 1)
            for b in range(B):
                pe.wait_ge(normed, b + 1)
                for i in range(TB):
                    last = nc.tensor.transpose(t.ps[:, b, i * P:(i + 1) * P], h[:, b * TB + i, :], t.ident)
                last.then_inc(turned, 1)
            for k in range(T):
                if k % TB == 0:
                    pe.wait_ge(relu_ready, k // TB + 1)
                last = nc.tensor.matmul(t.ps[:, 4, k * E:(k + 1) * E], hT[:, k * P:(k + 1) * P], cols[:, 2:2 + E],
                                        start=True, stop=True)
            last.then_inc(logits_ready, 1)
            pe.wait_ge(gates_ready, 1)
            for b in range(B):
                for i in range(TB):
                    last = nc.tensor.transpose(t.ps[0:E, b, i * P:(i + 1) * P], t.gates[:, :, b * TB + i], t.ident)
                last.then_inc(gt_turned, 1)
            for k in range(T):
                if k % TB == 0:
                    pe.wait_ge(gt_ready, k // TB + 1)
                if k >= 4:
                    pe.wait_ge(bias_ready, k - 3)
                nc.tensor.matmul(t.ps[:, 4 + k % 4, 0:D], gT[:, k * P:(k + 1) * P], ob[:],
                                 start=True, stop=True).then_inc(centred, 1)

        @block.scalar
        def _(act):
            for b in range(B):
                act.wait_ge(var_ready, b + 1)
                nc.scalar.activation(t.std[:, b * TB:(b + 1) * TB], t.mv[:, b * TB:(b + 1) * TB, 1], ACT.Sqrt,
                                     bias=t.eps).then_inc(std_ready, 1)
            for b in range(B):
                act.wait_ge(turned, b + 1)
                nc.scalar.activation(hT[:, b * S:(b + 1) * S], t.ps[:, b, :], ACT.Relu, bias=cols[:, 1:2],
                                     scale=cols[:, 0:1]).then_inc(relu_ready, 1)
            act.wait_ge(logits_in, 1)
            nc.scalar.activation(pr[:], lg[:], ACT.Exp).then_inc(exp_ready, 1)
            for b in range(B):
                act.wait_ge(gt_turned, b + 1)
                nc.scalar.copy(gT[:, b * S:(b + 1) * S], t.ps[0:E, b, :]).then_inc(gt_ready, 1)

        @block.vector
        def _(dve):
            steps = Steps(dve, own)

            def step(ins):
                steps.did(ins)
                steps.wait()

            dve.wait_ge(loaded, 16 * len(loads))
            for b in range(B):
                dve.wait_ge(h_ready, b + 1)
                ks = range(b * TB, (b + 1) * TB)
                step(nc.vector.tensor_tensor(h[:, b * TB:(b + 1) * TB, :], by(t.ps[:, b, :], R1),
                                             bcast(rows[:, 0:R1], 1, TB), ALU.add))
                for k in ks:
                    steps.did(nc.vector.bn_stats(t.stats[:, k, :], h[:, k, :]))
                steps.wait()
                for k in ks:
                    last = nc.vector.bn_aggr(t.mv[:, k, :], t.stats[:, k, :])
                last.then_inc(var_ready, 1)
            for b in range(B):
                dve.wait_ge(std_ready, b + 1)
                step(nc.vector.reciprocal(t.rstd[:, b * TB:(b + 1) * TB], t.std[:, b * TB:(b + 1) * TB]))
                for k in range(b * TB, (b + 1) * TB):
                    last = nc.vector.tensor_scalar(h[:, k, :], h[:, k, :], t.mv[:, k, 0:1], t.rstd[:, k:k + 1],
                                                   ALU.subtract, ALU.mult)
                last.then_inc(normed, 1)
            dve.wait_ge(logits_ready, 1)
            step(nc.vector.tensor_tensor(lg[:], by(t.ps[:, 4, 0:T * E], E), bcast(rows[:, R1:R1 + E], 1, T), ALU.add))
            step(nc.vector.tensor_reduce(one[:], lg[:], AX.X, ALU.max))
            nc.vector.tensor_tensor(lg[:], lg[:], bcast(one[:], 2, E), ALU.subtract).then_inc(logits_in, 1)
            dve.wait_ge(exp_ready, 1)
            step(nc.vector.tensor_reduce(one[:], pr[:], AX.X, ALU.add))
            step(nc.vector.reciprocal(one[:], one[:]))
            step(nc.vector.tensor_tensor(pr[:], pr[:], bcast(one[:], 2, E), ALU.mult))
            step(nc.vector.tensor_copy(lg[:], pr[:]))
            for n in range(2):
                step(nc.vector.tensor_reduce(one[:], lg[:], AX.X, ALU.max))
                step(nc.vector.tensor_tensor(cand[:], lg[:], bcast(one[:], 2, E), ALU.is_equal))
                step(nc.vector.tensor_tensor(cand[:], cand[:], bcast(t.const[:, CONST["first"]], 1, T), ALU.mult))
                step(nc.vector.tensor_reduce(one[:], cand[:], AX.X, ALU.max))
                step(nc.vector.tensor_tensor(pick[:, n, :, :], cand[:], bcast(one[:], 2, E), ALU.is_equal))
                if n == 0:
                    step(nc.vector.tensor_scalar(cand[:], pick[:, 0, :, :], -2.0, None, ALU.mult))
                    step(nc.vector.tensor_tensor(lg[:], lg[:], cand[:], ALU.add))
            step(nc.vector.tensor_tensor(cand[:], pick[:, 0, :, :], pick[:, 1, :, :], ALU.add))
            step(nc.vector.tensor_tensor(pr[:], pr[:], cand[:], ALU.mult))
            step(nc.vector.tensor_reduce(one[:], pr[:], AX.X, ALU.add))
            step(nc.vector.reciprocal(one[:], one[:]))
            nc.vector.tensor_tensor(t.gates[:].rearrange("p e k -> p k e"), pr[:], bcast(one[:], 2, E), ALU.mult)\
                .then_inc(gates_ready, 1)
            for k in range(T):
                dve.wait_ge(centred, k + 1)
                nc.vector.tensor_tensor(t.x[:, k, :], t.x[:, k, :],
                                        t.ps[:, 4 + k % 4, 0:D], ALU.add).then_inc(bias_ready, 1)


PAIRS = E * B


def round_steps(n):
    now, before, after, later = (0 <= m < PAIRS for m in (n, n - 1, n + 1, n + 2))
    at = {}

    def put(on, slot, place, *step):
        if on:
            at.setdefault((slot, place), []).append(step)

    for g in range(HE // G4):
        last = g == HE // G4 - 1
        for k in range(TB):
            put(before if last else now, (G4 * (g + 1)) % HE + k, 2, "values", n - last, g * TB + k)
    put(later, 0, 0, "project", n + 2, 0)
    put(later, 2, 0, "project", n + 2, 1)
    put(after, 4, 0, "project_v", n + 1, 0)
    put(later, 6, 0, "project", n + 2, 2)
    put(later, 8, 0, "project", n + 2, 3)
    put(before, 10, 0, "add", n - 1, 0)
    put(before, 12, 0, "add", n - 1, 1)
    put(after, 14, 0, "project_v", n + 1, 1)
    put(before, 1, 0, "turn_out", n - 1, 2)
    put(now, 3, 0, "row_max", n, 1)
    put(before, 5, 0, "turn_out", n - 1, 3)
    put(before, 7, 0, "turn_norm", n - 1, 1)
    put(now, 9, 0, "turn_out", n, 0)
    put(after, 11, 0, "row_max", n + 1, 0)
    put(now, 13, 0, "turn_out", n, 1)
    put(now, 15, 0, "turn_norm", n, 0)
    steps = []
    for h in range(HE):
        steps += at.get((h, 0), [])
        steps += [("maxima", n + 1, 2 * h)] * after
        steps += at.get((h, 1), [])
        steps += [("attend", n, 2 * h)] * now
        steps += [("maxima", n + 1, 2 * h + 1)] * after
        steps += at.get((h, 2), [])
        steps += [("attend", n, 2 * h + 1)] * now
    return steps


ROUNDS = range(-2, PAIRS + 1)
MISC = ("turn_out", "row_max", "turn_norm", "project", "add", "project_v")
MISC_LIST = [s for n in ROUNDS for s in round_steps(n) if s[0] in MISC]
MISC_AT = {step: i for i, step in enumerate(MISC_LIST)}


def ring_slot(n, h):
    return h % RING


def values_before(n, h):
    k = n * HE + h
    for j in range(k - 1, k - HE - RING, -1):
        if j >= 0 and ring_slot(*divmod(j, HE)) == ring_slot(n, h):
            return j // G4 + 1
    return 0


class Rounds:

    def __init__(self, engine, nc, steps):
        self.engine, self.expert = engine, None
        self.n = 0
        for self.n in range(-2, B):
            self.walk(steps)
        with engine.Fori(1, E - 1) as self.expert:
            for self.n in range(B, 2 * B):
                self.walk(steps)
        self.expert = None
        for self.n in range((E - 1) * B, PAIRS + 1):
            self.walk(steps)

    def walk(self, steps):
        start = steps.get("start")
        if start:
            start(self, self.n)
        for kind, m, arg in round_steps(self.n):
            if kind in steps:
                steps[kind](self, m, arg)
        end = steps.get("end")
        if end:
            end(self, self.n)

    def value(self, count, *args):
        m, rest = args[0], args[1:]
        v = count(m, *rest)
        if self.expert is None:
            return v
        step = count(m + B, *rest) - v
        assert v > 0 and step >= 0 and count(m + 2 * B, *rest) - v == 2 * step
        return self.expert * step + (v - step) if step else v

    def wait(self, semaphore, count, *args):
        v = self.value(count, *args)
        if self.expert is not None or v > 0:
            self.engine.wait_ge(semaphore, v)

    def expert_of(self, m):
        return m // B if self.expert is None else self.expert + (m // B - 1)


def expert_stage(nc, t, io):
    with ExitStack() as stack:
        sc = Scope(nc, "experts", stack)
        wqk_in, wv_in, wo_in = sc.sems("wqk_in wv_in wo_in")
        qk_moved, max_moved = sc.sems("qk_moved0 qk_moved1"), sc.sems("max_moved0 max_moved1")
        max_scores, maxed, scores, exped, summed, out_taken = sc.sems("max_scores maxed scores exped summed out_taken")
        misc_made, added, high_ready, rest_ready, mid_ready, low_ready, max_high, max_split, inverse, normed, \
            gate_ready, ones_ready, v_taken, turned_taken, sum_clear = sc.sems(
                "misc_made added high_ready rest_ready mid_ready low_ready max_high max_split inverse normed "
                "gate_ready ones_ready v_taken turned_taken sum_clear")
        QW = 4 * KC * P + 4
        VW = KC * D + D
        wqk = sc.sb("wqk", [P, QW])
        wv = sc.sb("wv", [P, VW])
        wo = sc.sb("wo", [P, KC * D])
        qs = [sc.sb(f"qs{i}", [MAX_ROWS, HE, S], BF16) for i in range(2)]
        ks = [sc.sb(f"ks{i}", [MAX_ROWS, HE, S], BF16) for i in range(2)]
        parts = sc.sb("parts", [P, 4, 3, S], BF16)
        rest = sc.sb("rest", [P, 2, S])
        vs = [sc.sb(f"vs{i}", [P, TB, HE, DH + 1]) for i in range(2)]
        prob = sc.sb("prob", [P, RING, TB, S])
        out_sb = sc.sb("out_sb", [P, S])
        rinv = sc.sb("rinv", [P, TB, G4])
        on = sc.sb("on", [P, TB, D])
        onT = sc.sb("onT", [P, KC, S])
        nmx = sc.sb("nmx", [P, TB, HE])
        nm = sc.sb("nm", [HC, 2, S], BF16)
        gate = sc.sb("gate", [P, TB])
        MX = t.ps[:, 0:4, :]
        EX = t.ps[:, 4:6, :]
        OUT = t.ps[:, 6, :]
        SH = t.ps[:, 7, :]

        max_count = lambda m, h, half: m * 2 * HE + 2 * h + half + 1
        score_count = lambda m, h, k: m * HE * TB + h * TB + k + 1
        sum_count = lambda m, g: m * HE // G4 + g + 1
        moved_count = lambda m: 16 * 2 * len(Q_PARTS) * (m + 1)
        max_moved_count = lambda m: 16 * 2 * (m + 1)
        row_count = lambda m, c: m * KC + c + 1
        value_count = lambda m, half: 2 * m + half + 1
        misc_count = lambda m, kind, a: MISC_AT[kind, m, a] + 1
        project_count = lambda m, a: 4 * m + a + 1
        freed = {"turn_out": (normed, sum_count), "row_max": (max_split, row_count), "turn_norm": (turned_taken, row_count),
                 "project": (rest_ready, project_count), "project_v": (v_taken, value_count), "add": (added, value_count)}
        block = stack.enter_context(nc.Block())

        @block.sync
        def _(sp):
            def load_qk(e):
                sp.dma_start(wqk[:], io["e_qk"][e]).then_inc(wqk_in, 16)

            def load_v(e):
                sp.dma_start(wv[:], io["e_v"][e]).then_inc(wv_in, 16)

            def load_o(e):
                sp.dma_start(wo[:], io["e_o"][e]).then_inc(wo_in, 16)

            def move_split(r, m, c):
                r.wait(low_ready, project_count, m, 2 * c + 1)
                for a, (dst, order) in enumerate(((qs[m % 2], Q_PARTS), (ks[m % 2], K_PARTS))):
                    for g, part in enumerate(order):
                        sp.dma_start(dst[g * DH:(g + 1) * DH, c * HC:(c + 1) * HC, :], parts[:, 2 * c + a, part, :])\
                            .then_inc(qk_moved[c], 16)

            def move_max(r, m, c):
                r.wait(max_split, row_count, m, c)
                for a in range(2):
                    sp.dma_start(qs[m % 2][SPLIT_ROWS + a:SPLIT_ROWS + a + 1, c * HC:(c + 1) * HC, :], nm[:, a, :])\
                        .then_inc(max_moved[c], 16)

            def start(r, n):
                if 0 <= n + 1 < PAIRS:
                    move_split(r, n + 1, 1)

            def step(r, m, a):
                move_max(r, m, a)

            def projected(r, m, a):
                if a == 3:
                    move_split(r, m, 0)

            def end(r, n):
                for m, semaphore, count, last, load in ((n + 2, rest_ready, project_count, 3, load_qk),
                                                        (n + 1, v_taken, value_count, 1, load_v),
                                                        (n - 1, misc_made, lambda m, a: misc_count(m, "add", a), 1, load_o)):
                    if m % B == B - 1 and B - 1 <= m < PAIRS - 1:
                        r.wait(semaphore, count, m, last)
                        if r.expert is not None:
                            sp.wait_ge(semaphore, 1)
                        load(r.expert_of(m + 1))

            load_qk(0)
            load_v(0)
            load_o(0)
            Rounds(sp, nc, {"start": start, "row_max": step, "project": projected, "end": end})

        @block.tensor
        def _(pe):
            def shared(r, kind, m, a):
                at = MISC_AT[kind, m, a]
                if at:
                    kind, m, a = MISC_LIST[at - 1]
                    r.wait(*freed[kind], m, a)

            def maxima(r, m, a):
                h, half = divmod(a, 2)
                if h % HC == 0 and half == 0:
                    r.wait(qk_moved[h // HC], moved_count, m)
                r.wait(maxed, lambda m: max_count(m, h, half) - 2, m)
                for q in range(2 * half, 2 * half + 2):
                    last = nc.tensor.matmul(MX[:, q, :], qs[m % 2][0:SPLIT_ROWS, h, q * P:(q + 1) * P],
                                            ks[m % 2][0:SPLIT_ROWS, h, :], start=True, stop=True)
                last.then_inc(max_scores, 1)

            def attend(r, m, a):
                h, half = divmod(a, 2)
                if h % HC == 0 and half == 0:
                    r.wait(max_moved[h // HC], max_moved_count, m)
                if m == 0 and a == 0:
                    pe.wait_ge(ones_ready, 4)
                for k in (2 * half, 2 * half + 1):
                    r.wait(exped, lambda m: score_count(m, h, k) - 2, m)
                    nc.tensor.matmul(EX[:, k % 2, :], ks[m % 2][:, h, k * P:(k + 1) * P], qs[m % 2][:, h, :],
                                     start=True, stop=True).then_inc(scores, 1)

            def values(r, m, a):
                g, k = divmod(a, TB)
                if k == 0:
                    r.wait(exped, score_count, m, G4 * g + G4 - 1, TB - 1)
                    r.wait(out_taken, lambda m: sum_count(m, g) - 1, m)
                if m == 0 and a == 0:
                    pe.wait_ge(sum_clear, 1)
                if a == 0:
                    r.wait(v_taken, value_count, m, 1)
                for j in range(G4):
                    h = G4 * g + j
                    last = nc.tensor.matmul(OUT[32 * j:32 * j + DH + 1, :], vs[m % 2][:, k, h, :],
                                            prob[:, ring_slot(m, h), k, :], start=k == 0, stop=k == TB - 1)
                if k == TB - 1:
                    last.then_inc(summed, 1)

            def turn_out(r, m, g):
                shared(r, "turn_out", m, g)
                r.wait(out_taken, sum_count, m, g)
                for q in range(TB):
                    last = nc.tensor.transpose(SH[:, q * P:(q + 1) * P], out_sb[:, q * P:(q + 1) * P], t.ident)
                last.then_inc(misc_made, 1)

            def row_max(r, m, c):
                shared(r, "row_max", m, c)
                r.wait(maxed, max_count, m, HC * (c + 1) - 1, 1)
                for q in range(TB):
                    last = nc.tensor.transpose(SH[0:HC, q * P:(q + 1) * P], nmx[:, q, c * HC:(c + 1) * HC], t.ident)
                last.then_inc(misc_made, 1)

            def turn_norm(r, m, c):
                shared(r, "turn_norm", m, c)
                r.wait(normed, lambda m: sum_count(m, 2 * c + 1), m)
                for q in range(TB):
                    last = nc.tensor.transpose(SH[:, q * P:(q + 1) * P], on[:, q, c * P:(c + 1) * P], t.ident)
                last.then_inc(misc_made, 1)

            def project(r, m, a):
                shared(r, "project", m, a)
                c, w = divmod(a, 2)
                if m % B == 0 and a == 0:
                    r.wait(wqk_in, lambda m: 16 * (m // B + 1), m)
                for kc in range(KC):
                    col = ((w * KC + c) * KC + kc) * P
                    last = nc.tensor.matmul(SH, wqk[:, col:col + P], t.xnT[:, kc, (m % B) * S:(m % B + 1) * S],
                                            start=kc == 0, stop=kc == KC - 1)
                last.then_inc(misc_made, 1)

            def project_v(r, m, half):
                shared(r, "project_v", m, half)
                if m % B == 0 and half == 0:
                    r.wait(wv_in, lambda m: 16 * (m // B + 1), m)
                for i in range(2):
                    tok = (m % B) * S + (2 * half + i) * P
                    for kc in range(KC):
                        last = nc.tensor.matmul(SH[:, i * D:(i + 1) * D], t.xnT[:, kc, tok:tok + P],
                                                wv[:, kc * D:(kc + 1) * D], start=kc == 0, stop=kc == KC - 1)
                last.then_inc(misc_made, 1)

            def add(r, m, half):
                shared(r, "add", m, half)
                if half == 0:
                    r.wait(turned_taken, row_count, m, KC - 1)
                    if m % B == 0:
                        r.wait(wo_in, lambda m: 16 * (m // B + 1), m)
                for i in range(2):
                    q = 2 * half + i
                    for kc in range(KC):
                        last = nc.tensor.matmul(SH[:, i * D:(i + 1) * D], onT[:, kc, q * P:(q + 1) * P],
                                                wo[:, kc * D:(kc + 1) * D], start=kc == 0, stop=kc == KC - 1)
                last.then_inc(misc_made, 1)

            Rounds(pe, nc, {"maxima": maxima, "attend": attend, "values": values, "turn_out": turn_out,
                            "row_max": row_max, "turn_norm": turn_norm, "project": project, "project_v": project_v,
                            "add": add})

        @block.scalar
        def _(act):
            def attend(r, m, a):
                h, half = divmod(a, 2)
                if half == 0:
                    r.wait(summed, lambda m: values_before(m, h), m)
                for k in (2 * half, 2 * half + 1):
                    r.wait(scores, score_count, m, h, k)
                    nc.scalar.activation(prob[:, ring_slot(m, h), k, :], EX[:, k % 2, :], ACT.Exp, scale=DH ** -0.5)\
                        .then_inc(exped, 1)

            def project(r, m, a):
                r.wait(misc_made, misc_count, m, "project", a)
                if m >= 1:
                    r.wait(qk_moved[a // 2], moved_count, m - 1)
                w = a % 2
                bias = wqk[:, 4 * KC * P + w * KC + a // 2:4 * KC * P + w * KC + a // 2 + 1]
                nc.scalar.activation(parts[:, a, 0, :], SH, ACT.Identity, bias=bias).then_inc(high_ready, 1)

            def values(r, m, a):
                g, k = divmod(a, TB)
                if k < TB - 1:
                    return
                r.wait(summed, sum_count, m, g)
                if m * (HE // G4) + g >= 1:
                    pm, pg = divmod(m * (HE // G4) + g - 1, HE // G4)
                    r.wait(misc_made, lambda x: misc_count(x, "turn_out", pg), pm)
                nc.scalar.copy(out_sb[:], OUT).then_inc(out_taken, 1)

            def turn_norm(r, m, c):
                r.wait(misc_made, misc_count, m, "turn_norm", c)
                nc.scalar.copy(onT[:, c, :], SH).then_inc(turned_taken, 1)

            Rounds(act, nc, {"attend": attend, "project": project, "values": values, "turn_norm": turn_norm})

        @block.vector
        def _(dve):
            def maxima(r, m, a):
                h, half = divmod(a, 2)
                two = slice(2 * half, 2 * half + 2)
                r.wait(max_scores, max_count, m, h, half)
                nc.vector.tensor_reduce(nmx[:, two, h], MX[:, two, :], AX.X, ALU.max, negate=True).then_inc(maxed, 1)

            def project(r, m, a):
                r.wait(high_ready, project_count, m, a)
                k = 4 * m + a
                if k >= 2:
                    r.wait(low_ready, lambda m: project_count(m, a) - 2, m)
                w = a % 2
                bias = wqk[:, 4 * KC * P + w * KC + a // 2:4 * KC * P + w * KC + a // 2 + 1]
                nc.vector.scalar_tensor_tensor(rest[:, a % 2, :], SH, bias, parts[:, a, 0, :], ALU.add, ALU.subtract)\
                    .then_inc(rest_ready, 1)

            def project_v(r, m, half):
                r.wait(misc_made, misc_count, m, "project_v", half)
                if m >= 2:
                    r.wait(summed, sum_count, m - 2, HE // G4 - 1)
                for i in range(2):
                    last = nc.vector.tensor_tensor(vs[m % 2][:, 2 * half + i, :, 0:DH], by(SH[:, i * D:(i + 1) * D], DH),
                                                   by(wv[:, KC * D:VW], DH), ALU.add)
                last.then_inc(v_taken, 1)

            def row_max(r, m, c):
                r.wait(misc_made, misc_count, m, "row_max", c)
                if c:
                    r.wait(max_moved[0], max_moved_count, m)
                elif m >= 1:
                    r.wait(max_moved[1], max_moved_count, m - 1)
                nc.vector.tensor_copy(nm[:, 0, :], SH[0:HC, :]).then_inc(max_high, 1)
                r.wait(max_high, row_count, m, c)
                if m >= 2:
                    r.wait(scores, score_count, m - 2, HC * (c + 1) - 1, TB - 1)
                nc.vector.tensor_tensor(nm[:, 1, :], SH[0:HC, :], nm[:, 0, :], ALU.subtract).then_inc(max_split, 1)

            def turn_out(r, m, g):
                r.wait(misc_made, misc_count, m, "turn_out", g)
                heads = SH.rearrange("p (q j d) -> p q j d", q=TB, j=G4)
                nc.vector.reciprocal(rinv[:], heads[:, :, :, DH]).then_inc(inverse, 1)
                r.wait(inverse, sum_count, m, g)
                for q in range(TB):
                    last = nc.vector.tensor_tensor(by(on[:, q, g * G4 * DH:(g + 1) * G4 * DH], DH), heads[:, q, :, 0:DH],
                                                   bcast(rinv[:, q, :], 2, DH), ALU.mult)
                last.then_inc(normed, 1)

            def add(r, m, half):
                if half == 0:
                    nc.vector.tensor_copy(gate[:], t.gates[:, r.expert_of(m), (m % B) * TB:(m % B + 1) * TB])\
                        .then_inc(gate_ready, 1)
                r.wait(misc_made, misc_count, m, "add", half)
                r.wait(gate_ready, lambda m: m + 1, m)
                for i in range(2):
                    q = 2 * half + i
                    x = t.x[:, (m % B) * TB + q, :]
                    last = nc.vector.scalar_tensor_tensor(x, SH[:, i * D:(i + 1) * D], gate[:, q:q + 1], x, ALU.mult, ALU.add)
                last.then_inc(added, 1)

            nc.vector.memset(OUT, 0.0).then_inc(sum_clear, 1)
            for i in range(2):
                nc.vector.memset(ks[i][SPLIT_ROWS:MAX_ROWS, :, :], 1.0).then_inc(ones_ready, 1)
                nc.vector.memset(vs[i][:, :, :, DH:DH + 1], 1.0).then_inc(ones_ready, 1)
            Rounds(dve, nc, {"maxima": maxima, "project": project, "project_v": project_v, "row_max": row_max,
                             "turn_out": turn_out, "add": add})

        @block.gpsimd
        def _(pool):
            def project(r, m, a):
                r.wait(rest_ready, project_count, m, a)
                if m >= 1:
                    r.wait(qk_moved[a // 2], moved_count, m - 1)
                nc.gpsimd.tensor_tensor(parts[:, a, 1, :], rest[:, a % 2, :], t.one.broadcast_to([P, S]), ALU.mult)\
                    .then_inc(mid_ready, 1)
                r.wait(mid_ready, project_count, m, a)
                if m >= 2 and a % 2:
                    r.wait(scores, score_count, m - 2, HC * (a // 2 + 1) - 1, TB - 1)
                nc.gpsimd.tensor_tensor(parts[:, a, 2, :], rest[:, a % 2, :], parts[:, a, 1, :], ALU.subtract)\
                    .then_inc(low_ready, 1)

            Rounds(pool, nc, {"project": project})


def sign_steps():
    steps = [("turn", 0, None), ("turn", 1, None)] + [("layer0", 0, c) for c in range(OC)]
    for b in range(B):
        for c in range(OC):
            steps.append(("layer1", b, c))
            if b + 1 < B:
                steps.append(("layer0", b + 1, c))
            if b and c < TB:
                steps.append(("output", b - 1, c))
            if c == OC // 2 and b + 2 < B:
                steps.append(("turn", b + 2, None))
    return steps + [("output", B - 1, i) for i in range(TB)]


def sign_stage(nc, t, io):
    steps = sign_steps()
    unit = {s: i for i, s in enumerate(s for s in steps if s[0] in ("layer0", "layer1"))}
    with ExitStack() as stack:
        sc = Scope(nc, "sign", stack)
        x_high, x_rest, x_mid, x_low = sc.sems("x_high x_rest x_mid x_low")
        var_ready, std_ready, own, xn_ready, turned = sc.sems("var_ready std_ready own xn_ready turned")
        made, kept, high, left, mid, low, y_ready, y_added, stored = sc.sems("made kept high left mid low y_ready y_added stored")
        xn = sc.sb("xn", [P, 2, TB, D])
        xp = sc.sb("xp", [P, 2, 3, KC, S], BF16)
        xr = sc.sb("xr", [P, 2, KC * S])
        hp = [[sc.sb(f"hp{layer}_{i}", [P, 3, OC, S], BF16) for i in range(2)] for layer in range(2)]
        hf = sc.sb("hf", [P, 2, S])
        hr = sc.sb("hr", [P, 2, S])
        block = stack.enter_context(nc.Block())

        def layer_of(kind):
            return 0 if kind == "layer0" else 1

        @block.sync
        def _(sp):
            for b in range(B):
                sp.wait_ge(y_added, (b + 1) * TB)
                sp.dma_start(io["out"][:, b * TB:(b + 1) * TB, :], t.x[:, b * TB:(b + 1) * TB, :]).then_inc(stored, 16)
            sp.wait_ge(stored, 16 * B)

        @block.gpsimd
        def _(pool):
            for b in range(B):
                xv = xr[:, b % 2, :].rearrange("p (c s) -> p c s", c=KC)
                pool.wait_ge(x_rest, b + 1)
                nc.gpsimd.tensor_copy(xp[:, b % 2, 1, :, :], xv).then_inc(x_mid, 1)
                pool.wait_ge(x_mid, b + 1)
                nc.gpsimd.tensor_tensor(xp[:, b % 2, 2, :, :], xv, xp[:, b % 2, 1, :, :], ALU.subtract).then_inc(x_low, 1)

        @block.tensor
        def _(pe):
            pe.wait_ge(t.signs_ready, 3)

            def products(kind, b, c):
                u = unit[kind, b, c]
                w, src, n = (t.w0, xp[:, b % 2, :, :, :], KC) if kind == "layer0" else (t.w1, hp[0][b % 2], OC)
                if kind == "layer0":
                    pe.wait_ge(x_low, b + 1)
                if u >= 4:
                    pe.wait_ge(kept, u - 3)
                for k in range(n):
                    if kind == "layer1" and c == 0:
                        pe.wait_ge(low, unit["layer0", b, k] + 1)
                    for part in range(3):
                        last = nc.tensor.matmul(t.ps[:, u % 4, :], w[:, k, c * P:(c + 1) * P], src[:, part, k, :],
                                                start=k == 0 and part == 0, stop=k == n - 1 and part == 2)
                last.then_inc(made, 1)

            def output(b, i):
                j = b * TB + i
                if j >= 2:
                    pe.wait_ge(y_added, j - 1)
                for k in range(OC):
                    if i == 0:
                        pe.wait_ge(low, unit["layer1", b, k] + 1)
                    for part in range(3):
                        last = nc.tensor.matmul(t.ps[:, 4 + j % 2, 0:D], hp[1][b % 2][:, part, k, i * P:(i + 1) * P],
                                                t.w2[:, k, :], start=k == 0 and part == 0, stop=k == OC - 1 and part == 2)
                last.then_inc(y_ready, 1)

            for kind, b, a in steps:
                if kind == "turn":
                    pe.wait_ge(xn_ready, b + 1)
                    if b:
                        pe.wait_ge(x_rest, b)
                    for c in range(KC):
                        for i in range(TB):
                            last = nc.tensor.transpose(t.ps[:, 6 + c, i * P:(i + 1) * P],
                                                       xn[:, b % 2, i, c * P:(c + 1) * P], t.ident)
                    last.then_inc(turned, 1)
                elif kind == "output":
                    output(b, a)
                else:
                    products(kind, b, a)

        @block.scalar
        def _(act):
            def root(b):
                act.wait_ge(var_ready, b + 1)
                nc.scalar.activation(t.std[:, b * TB:(b + 1) * TB], t.mv[:, b * TB:(b + 1) * TB, 1], ACT.Sqrt,
                                     bias=t.eps).then_inc(std_ready, 1)

            def x_part(b):
                if b >= 2:
                    act.wait_ge(made, unit["layer0", b - 2, OC - 1] + 1)
                act.wait_ge(turned, b + 1)
                nc.scalar.copy(xp[:, b % 2, 0, :, :], t.ps[:, 6:6 + KC, :]).then_inc(x_high, 1)

            for b in range(B):
                root(b)
            for kind, b, c in steps:
                if kind == "turn":
                    x_part(b)
                if kind not in ("layer0", "layer1"):
                    continue
                u, layer = unit[kind, b, c], layer_of(kind)
                act.wait_ge(made, u + 1)
                if u >= 2:
                    act.wait_ge(left, u - 1)
                nc.scalar.activation(hf[:, u % 2, :], t.ps[:, u % 4, :], ACT.Relu, scale=t.sv4[:, layer:layer + 1])\
                    .then_inc(kept, 1)
                act.wait_ge(kept, u + 1)
                if c == 0 and b >= 2:
                    if layer == 0:
                        act.wait_ge(made, unit["layer1", b - 2, OC - 1] + 1)
                    else:
                        act.wait_ge(y_ready, (b - 1) * TB)
                nc.scalar.copy(hp[layer][b % 2][:, 0, c, :], hf[:, u % 2, :]).then_inc(high, 1)

        @block.vector
        def _(dve):
            own_steps = Steps(dve, own)

            def moments(b):
                ks = range(b * TB, (b + 1) * TB)
                for k in ks:
                    own_steps.did(nc.vector.bn_stats(t.stats[:, k, :], t.x[:, k, :]))
                own_steps.wait()
                for k in ks:
                    last = nc.vector.bn_aggr(t.mv[:, k, :], t.stats[:, k, :])
                last.then_inc(var_ready, 1)

            def normalise(b):
                dve.wait_ge(std_ready, b + 1)
                own_steps.did(nc.vector.reciprocal(t.rstd[:, b * TB:(b + 1) * TB], t.std[:, b * TB:(b + 1) * TB]))
                if b >= 2:
                    dve.wait_ge(turned, b - 1)
                own_steps.wait()
                for i in range(TB):
                    k = b * TB + i
                    last = nc.vector.tensor_scalar(xn[:, b % 2, i, :], t.x[:, k, :], t.mv[:, k, 0:1], t.rstd[:, k:k + 1],
                                                   ALU.subtract, ALU.mult)
                last.then_inc(xn_ready, 1)

            def x_part(b):
                dve.wait_ge(x_high, b + 1)
                if b >= 2:
                    dve.wait_ge(x_low, b - 1)
                nc.vector.tensor_tensor(xr[:, b % 2, :].rearrange("p (c s) -> p c s", c=KC), t.ps[:, 6:6 + KC, :],
                                        xp[:, b % 2, 0, :, :], ALU.subtract).then_inc(x_rest, 1)

            moments(0)
            moments(1)
            normalise(0)
            normalise(1)
            moments(2)
            moments(3)
            for kind, b, a in steps:
                if kind == "turn":
                    if b >= 2:
                        normalise(b)
                    x_part(b)
                elif kind == "output":
                    j = b * TB + a
                    dve.wait_ge(y_ready, j + 1)
                    nc.vector.scalar_tensor_tensor(t.x[:, j, :], t.ps[:, 4 + j % 2, 0:D], t.sv[:, 2:3], t.x[:, j, :],
                                                   ALU.mult, ALU.add).then_inc(y_added, 1)
                else:
                    u, parts = unit[kind, b, a], hp[layer_of(kind)][b % 2]
                    dve.wait_ge(high, u + 1)
                    nc.vector.tensor_tensor(hr[:, u % 2, :], hf[:, u % 2, :], parts[:, 0, a, :], ALU.subtract)\
                        .then_inc(left, 1)
                    dve.wait_ge(left, u + 1)
                    nc.vector.tensor_copy(parts[:, 1, a, :], hr[:, u % 2, :]).then_inc(mid, 1)
                    dve.wait_ge(mid, u + 1)
                    nc.vector.tensor_tensor(parts[:, 2, a, :], hr[:, u % 2, :], parts[:, 1, a, :], ALU.subtract)\
                        .then_inc(low, 1)


class State:
    pass


STAGES = 5


def build(nc, io):
    with ExitStack() as stack:
        sc = Scope(nc, "main", stack)
        t = State()
        t.ps = stack.enter_context(nc.psum_tensor("ps", [P, 8, 512], F32))
        t.const = sc.sb("const", [P, NCONST])
        t.x = sc.sb("x", [P, T, D])
        t.xnT = sc.sb("xnT", [P, KC, B * S])
        t.gates = sc.sb("gates", [P, E, T])
        t.stats = sc.sb("stats", [P, T, 6])
        t.mv = sc.sb("mv", [P, T, 2])
        t.std = sc.sb("std", [P, T])
        t.rstd = sc.sb("rstd", [P, T])
        t.ident = t.const[:, CONST["ident"]]
        t.eps = t.const[:, CONST["eps"]]
        t.one = t.const[:, CONST["one"]]
        t.heads = {16: t.const[:, CONST["heads16"]], 8: t.const[:, CONST["heads8"]]}

        def context_buffers(si):
            t.ctxT = si.sb("ctxT", [P, KC, NCTX])
            t.ctxT2 = si.sb("ctxT2", [P, KC, B, 2, S2])
            t.ctxnT = si.sb("ctxnT", [P, KC, NCTX])
            t.bound = si.sb("bound", [P, NCTX])
            t.pre = si.sb("pre", [P, 2, KC])

        with ExitStack() as inner:
            si = Scope(nc, "first", inner)
            context_buffers(si)
            rot = si.sb("rot", [P, 2, S])
            t.rot = [rot[:, 0, :], rot[:, 1, :]]
            order = ("q", "qrot", "k", "krot", "v", "o")
            W, W_in = si.sb("w", [P, KC, len(order), D]), si.sem("w_in")
            context_stage(nc, t, io, "load0", [(t.const, io["const"]), (t.x, io["x"])],
                          [(rot, io["rot"], W_in), (W, io["a0"], W_in)])
            layernorm_stage(nc, t, "ln0")
            context_attention(nc, t, "attn0", H0, W, W_in, order, (D // H0) ** -0.5, True, t.ctxT, None, None)

        if STAGES >= 2:
            layernorm_stage(nc, t, "ln1")
            router_stage(nc, t, io)
            expert_stage(nc, t, io)

        if STAGES < 3:
            done = sc.sem("done")
            with nc.Block() as block:
                @block.sync
                def _(sp):
                    sp.dma_start(io["out"], t.x[:]).then_inc(done, 16)
                    sp.wait_ge(done, 16)
            return

        t.w0 = sc.sb("w0", [P, KC, FF], BF16)
        t.w1 = sc.sb("w1", [P, OC, FF], BF16)
        t.w2 = sc.sb("w2", [P, OC, D], BF16)
        t.sv = sc.sb("sv", [P, 3])
        t.sv4 = sc.sb("sv4", [P, 3])
        t.signs_ready = sc.sem("signs_ready")
        with ExitStack() as inner:
            si = Scope(nc, "second", inner)
            context_buffers(si)
            order = ("q", "k", "v", "o")
            W, W_in, signs_in = si.sb("w", [P, KC, len(order), D]), si.sem("w_in"), si.sem("signs_in")
            words = [si.sb(f"words{i}", [P, rows, width // 4], U32)
                     for i, (rows, width) in enumerate(((2 * KC, FF), (OC, FF), (OC, D)))]

            def make_signs(dve):
                signs = [w[:].bitcast(U8) for w in words]
                dve.wait_ge(signs_in, 16 * 4)
                nc.vector.tensor_tensor(t.w0[:], signs[0][:, 0:KC, :], signs[0][:, KC:2 * KC, :], ALU.subtract)
                nc.vector.tensor_scalar(t.w1[:], signs[1], 2.0, -1.0, ALU.mult, ALU.add).then_inc(t.signs_ready, 1)
                nc.vector.tensor_scalar(t.w2[:], signs[2], 2.0, -1.0, ALU.mult, ALU.add).then_inc(t.signs_ready, 1)
                nc.vector.tensor_scalar(t.sv4[:, 0:1], t.sv[:, 0:1], 4.0, None, ALU.mult)
                nc.vector.tensor_scalar(t.sv4[:, 1:2], t.sv[:, 1:2], 2.0, None, ALU.mult).then_inc(t.signs_ready, 1)

            context_stage(nc, t, io, "load1", [], [(W, io["a1"], W_in)] + [
                (out, io[n], signs_in) for out, n in zip(words + [t.sv], ("k0", "k1", "k2", "sv"))])
            layernorm_stage(nc, t, "ln2", (t.pre[:, 0, :], t.pre[:, 1, :]), 2)
            context_attention(nc, t, "attn1", H1, W, W_in, order, D ** -0.5, False, t.ctxnT, 1e4 * D ** 0.5,
                              io["a1_rows"], make_signs)
        sign_stage(nc, t, io)


def constants():
    const = np.zeros((P, NCONST), np.float32)
    rows = np.arange(P)
    const[:, CONST["ident"]] = np.eye(P)
    for heads in (H0, H1):
        const[:, CONST[f"heads{heads}"]] = rows[:, None] // (D // heads) == np.arange(heads // KC)[None]
    const[:, CONST["first"]] = np.arange(E, 0, -1)
    const[:, CONST["eps"]] = EPS
    const[:, CONST["one"]] = 1
    dh = D // H0
    div = np.exp(np.arange(0, dh, 2, dtype=np.float32) * np.float32(-np.log(10000.0) / dh))
    angle = (np.arange(S, dtype=np.float32)[:, None] * div).T
    which = rows % dh
    sign = np.where(which < dh // 2, -1, 1).astype(np.float32)[:, None]
    rot = np.stack([np.cos(angle)[which % (dh // 2)], np.sin(angle)[which % (dh // 2)] * sign], 1)
    return const, rot.astype(np.float32)


def lay_out(i):
    f = lambda name: np.asarray(i[name])
    chunks = lambda w: w.reshape(w.shape[0] // P, P, -1).transpose(1, 0, 2)
    rep = lambda row: np.broadcast_to(row, (P,) + row.shape)
    cols = lambda v: v.reshape(-1, P).T
    a = {}
    a["const"], a["rot"] = constants()
    a["x"] = f("x").reshape(T, P, D).transpose(1, 0, 2)
    a["ctx"] = f("ctx_1024").reshape(NCTX // P, P, D).transpose(1, 0, 2)
    a["mask"] = rep(f("mask_BxS2_bf1").view(np.uint8).reshape(NCTX))
    a["pre"] = np.stack([cols(f("L1_xattn_pre_g")), cols(f("L1_xattn_pre_b"))], 1)
    dh = D // H0
    turn = (np.arange(D) // dh) * dh + (np.arange(D) + dh // 2) % dh
    wq, wkv, wo = f("L0_xattn_Wq"), f("L0_xattn_Wkv"), f("L0_xattn_Wout")
    a["a0"] = np.stack([chunks(w) for w in (wq, wq[:, turn], wkv[:, :D], wkv[:, :D][:, turn], wkv[:, D:], wo)], 2)
    a["a1"] = np.stack([chunks(f(f"L1_xattn_W{n}")) for n in "qkvo"], 2)
    a["a1_rows"] = np.stack([rep(f("L1_xattn_ln_g")), rep(f("L1_xattn_ln_b"))], 1)
    a["rW1"] = chunks(f("L0_ffn_rW1").T)
    a["r_rows"] = np.concatenate([rep(f("L0_ffn_rb1")), rep(f("L0_ffn_rb2"))], 1)
    a["r_cols"] = np.concatenate([f("L0_ffn_ln_g")[:, None], f("L0_ffn_ln_b")[:, None], f("L0_ffn_rW2").T], 1)
    a["ob"] = f("L0_ffn_ob")
    order = np.arange(D).reshape(KC, HC, DH).transpose(0, 2, 1).reshape(KC, P)
    qk, biases = [], []
    for n in "qk":
        w = f(f"L0_ffn_{n}W").transpose(0, 2, 1)
        w = w.reshape(E, KC, P, D)[:, :, :, order]
        qk.append(w.transpose(0, 2, 3, 1, 4).reshape(E, P, -1))
        biases.append(f(f"L0_ffn_{n}b")[:, order].transpose(0, 2, 1))
    a["e_qk"] = np.concatenate(qk + biases, 2)
    wide = lambda w: w.transpose(0, 2, 1).reshape(E, KC, P, D).transpose(0, 2, 1, 3).reshape(E, P, KC * D)
    a["e_v"] = np.concatenate([wide(f("L0_ffn_vW")), np.broadcast_to(f("L0_ffn_vb")[:, None], (E, P, D))], 2)
    a["e_o"] = wide(f("L0_ffn_oW"))
    for n in range(3):
        a[f"k{n}"] = np.ascontiguousarray(chunks(f(f"L1_ffn_k{n}").view(np.uint8))).view(np.uint32)
    a["sv"] = np.stack([np.broadcast_to(f(f"L1_ffn_s{n}").reshape(()), (P,)) for n in range(3)], 1)
    return {n: np.ascontiguousarray(v) for n, v in a.items()}


def kernel(**inputs):
    import concourse.bacc as bacc
    from concourse.bass_utils import run_bass_kernel_spmd

    arrays = lay_out(inputs)
    nc = bacc.Bacc("TRN2", target_bir_lowering=False, num_devices=1)
    io = {n: nc.dram_tensor(f"in_{n}", v.shape, mybir.dt.from_np(v.dtype), kind="ExternalInput").ap()
          for n, v in arrays.items()}
    io["out"] = nc.dram_tensor("out_x", (P, T, D), F32, kind="ExternalOutput").ap()
    build(nc, io)
    r = run_bass_kernel_spmd(nc, [{f"in_{n}": v for n, v in arrays.items()}], core_ids=[0])
    out = r.results[0]["out_x"]
    return np.ascontiguousarray(out.transpose(1, 0, 2)).reshape(B, S, D)
```

```python
from contextlib import ExitStack

import numpy as np

import concourse.bass as bass
from concourse import mybir

F32 = mybir.dt.float32
BF16 = mybir.dt.bfloat16
U8 = mybir.dt.uint8
U32 = mybir.dt.uint32
ALU = mybir.AluOpType
ACT = mybir.ActivationFunctionType
AX = mybir.AxisListType

P = 128
B, S, D = 4, 512, 256
T = B * S // P
TB = S // P
KC = D // P
S2 = 64
NCTX = B * S2
H0, H1 = 16, 8
E, HE, DH = 8, 16, 16
R1 = D // 2
FF = 1024
OC = FF // P
EPS = 1e-5
LOWEST = -3.4028234663852886e38
HC = HE // KC
G4 = 4
RING = 8
Q_PARTS, K_PARTS = (0, 0, 0, 1, 1, 2), (0, 1, 2, 0, 1, 0)
SPLIT_ROWS = len(Q_PARTS) * DH
MAX_ROWS = SPLIT_ROWS + 2


def bcast(ap, axis, n):
    ap = ap.unsqueeze(axis)
    shape = list(ap.shape)
    shape[axis] = n
    return ap.broadcast_to(shape)


def by(ap, n):
    dims = " ".join("abcdef"[:len(ap.shape) - 1])
    return ap.rearrange(f"{dims} (g n) -> {dims} g n", n=n)


class Steps:

    def __init__(self, engine, semaphore):
        self.engine, self.semaphore, self.count = engine, semaphore, 0

    def did(self, instruction):
        instruction.then_inc(self.semaphore, 1)
        self.count += 1

    def wait(self):
        self.engine.wait_ge(self.semaphore, self.count)


CONST_WIDTHS = (("ident", P), ("heads16", H0 // KC), ("heads8", H1 // KC), ("first", E), ("eps", 1), ("one", 1))
CONST = {name: slice(sum(w for _, w in CONST_WIDTHS[:i]), sum(w for _, w in CONST_WIDTHS[:i + 1]))
         for i, (name, _) in enumerate(CONST_WIDTHS)}
NCONST = sum(w for _, w in CONST_WIDTHS)


class Scope:

    def __init__(self, nc, name, stack):
        self.nc, self.name, self.stack = nc, name, stack

    def sem(self, name):
        return self.stack.enter_context(self.nc.semaphore(f"{self.name}_{name}"))

    def sems(self, names):
        return [self.sem(n) for n in names.split()]

    def sb(self, name, shape, dt=F32):
        return self.stack.enter_context(self.nc.sbuf_tensor(f"{self.name}_{name}", shape, dt))


def x_moments(nc, t, steps, b, done=None):
    for k in range(b * TB, (b + 1) * TB):
        steps.did(nc.vector.bn_stats(t.stats[:, k, :], t.x[:, k, :]))
    steps.wait()
    for k in range(b * TB, (b + 1) * TB):
        last = nc.vector.bn_aggr(t.x_mv[:, k, :], t.stats[:, k, :])
    if done:
        last.then_inc(done, 1)


def normalise(nc, t, b, out, src, mv):
    for i in range(TB):
        k = b * TB + i
        last = nc.vector.tensor_scalar(out[:, k, :], src[:, k, :], mv[:, k, 0:1], t.rstd[:, k:k + 1],
                                       ALU.subtract, ALU.mult)
    return last


def prepare_stage(nc, t, io, name, more, x_in, ahead, affine, rounds):
    with ExitStack() as stack:
        sc = Scope(nc, name, stack)
        loaded, own, c_var, c_std, c_normed, c_turned, c_taken = sc.sems(
            "loaded own c_var c_std c_normed c_turned c_taken")
        var_ready, std_ready, xn_ready, turned = sc.sems("var_ready std_ready xn_ready turned")
        xn = sc.sb("xn", [P, T, D])
        cx = sc.sb("cx", [P, NCTX // P, D])
        cn = sc.sb("cn", [P, NCTX // P, D])
        c_stats = sc.sb("c_stats", [P, NCTX // P, 6])
        c_mv = sc.sb("c_mv", [P, NCTX // P, 2])
        c_dev = sc.sb("c_dev", [P, 2, NCTX // P])
        mask = sc.sb("mask", [P, NCTX], U8)
        loads = more + [(cx, io["ctx"]), (mask, io["mask"]), (t.pre, io["pre"])]
        block = stack.enter_context(nc.Block())

        @block.sync
        def _(sp):
            for out, src in loads:
                sp.dma_start(out[:], src).then_inc(loaded, 16)
            for b, semaphore in enumerate(x_in or ()):
                sp.dma_start(t.x[:, b * TB:(b + 1) * TB, :], io["x"][:, b * TB:(b + 1) * TB, :]).then_inc(semaphore, 16)
            for out, src, semaphore in ahead:
                sp.dma_start(out[:], src).then_inc(semaphore, 16)

        @block.vector
        def _(dve):
            steps = Steps(dve, own)

            def normalised(j, src, mv):
                b = j % B
                dve.wait_ge(std_ready, j + 1)
                steps.did(nc.vector.reciprocal(t.rstd[:, b * TB:(b + 1) * TB], t.std[:, b * TB:(b + 1) * TB]))
                steps.wait()
                normalise(nc, t, b, xn, src, mv).then_inc(xn_ready, 1)

            if rounds == 2:
                for b in range(B):
                    normalised(b, t.x, t.x_mv)
            dve.wait_ge(loaded, 16 * len(loads))
            for i in range(NCTX // P):
                steps.did(nc.vector.bn_stats(c_stats[:, i, :], cx[:, i, :]))
            steps.did(nc.vector.tensor_scalar(t.bound[:], mask[:], 0.5, -LOWEST, ALU.subtract, ALU.mult))
            steps.wait()
            steps.did(nc.vector.tensor_scalar(t.bound[:], t.bound[:], 2.0, None, ALU.mult))
            for i in range(NCTX // P):
                last = nc.vector.bn_aggr(c_mv[:, i, :], c_stats[:, i, :])
            last.then_inc(c_var, 1)
            for b in range(B):
                if x_in is not None:
                    dve.wait_ge(x_in[b], 16)
                    x_moments(nc, t, steps, b, var_ready)
                else:
                    dve.wait_ge(xn_ready, b + 1)
                    for k in range(b * TB, (b + 1) * TB):
                        steps.did(nc.vector.bn_stats(t.stats[:, k, :], xn[:, k, :]))
                    steps.wait()
                    for k in range(b * TB, (b + 1) * TB):
                        last = nc.vector.bn_aggr(t.mv[:, k, :], t.stats[:, k, :])
                    last.then_inc(var_ready, 1)
                if b == 0:
                    dve.wait_ge(c_std, 1)
                    steps.did(nc.vector.reciprocal(c_dev[:, 1, :], c_dev[:, 0, :]))
                    steps.wait()
                    for i in range(NCTX // P):
                        last = nc.vector.tensor_scalar(cn[:, i, :], cx[:, i, :], c_mv[:, i, 0:1], c_dev[:, 1, i:i + 1],
                                                       ALU.subtract, ALU.mult)
                    last.then_inc(c_normed, 1)
            for b in range(B):
                if rounds == 2:
                    normalised(B + b, xn, t.mv)
                else:
                    normalised(b, t.x, t.x_mv)

        @block.scalar
        def _(act):
            def root(b, mv):
                nc.scalar.activation(t.std[:, b * TB:(b + 1) * TB], mv[:, b * TB:(b + 1) * TB, 1], ACT.Sqrt,
                                     bias=t.eps).then_inc(std_ready, 1)

            if rounds == 2:
                for b in range(B):
                    root(b, t.x_mv)
            act.wait_ge(c_var, 1)
            nc.scalar.activation(c_dev[:, 0, :], c_mv[:, :, 1], ACT.Sqrt, bias=t.eps).then_inc(c_std, 1)
            for b in range(B):
                act.wait_ge(var_ready, b + 1)
                if rounds == 2:
                    act.wait_ge(xn_ready, b + 1)
                root(b, t.mv if rounds == 2 else t.x_mv)
            for c in range(KC):
                act.wait_ge(c_turned, c + 1)
                src = t.ps[:, c, 0:NCTX]
                nc.scalar.copy(t.ctxT[:, c, :], src)
                for a in range(2):
                    last = nc.scalar.copy(t.ctxT2[:, c, :, a, :], src.rearrange("p (b k) -> p b k", b=B))
                last.then_inc(c_taken, 1)
            for c in range(KC):
                act.wait_ge(c_turned, KC + c + 1)
                nc.scalar.activation(t.ctxnT[:, c, :], t.ps[:, KC + c, 0:NCTX], ACT.Identity,
                                     bias=t.pre[:, 1, c:c + 1], scale=t.pre[:, 0, c:c + 1]).then_inc(c_taken, 1)
            for b in range(B):
                for c in range(KC):
                    act.wait_ge(turned, b * KC + c + 1)
                    out, bank = t.xnT[:, c, b * S:(b + 1) * S], t.ps[:, (b * KC + c + 4) % 8, :]
                    if affine is None:
                        nc.scalar.copy(out, bank)
                    else:
                        nc.scalar.activation(out, bank, ACT.Identity, bias=affine[1][:, c:c + 1],
                                             scale=affine[0][:, c:c + 1])

        @block.tensor
        def _(pe):
            pe.wait_ge(loaded, 16 * len(loads))
            for n, src in enumerate((cx, cn)):
                if n:
                    pe.wait_ge(c_normed, 1)
                for c in range(KC):
                    for i in range(NCTX // P):
                        last = nc.tensor.transpose(t.ps[:, n * KC + c, i * P:(i + 1) * P], src[:, i, c * P:(c + 1) * P],
                                                   t.ident)
                    last.then_inc(c_turned, 1)
            for b in range(B):
                pe.wait_ge(xn_ready, (rounds - 1) * B + b + 1)
                if b == 2:
                    pe.wait_ge(c_taken, 2 * KC)
                for c in range(KC):
                    for i in range(TB):
                        last = nc.tensor.transpose(t.ps[:, (b * KC + c + 4) % 8, i * P:(i + 1) * P],
                                                   xn[:, b * TB + i, c * P:(c + 1) * P], t.ident)
                    last.then_inc(turned, 1)


def layernorm_stage(nc, t, name, load):
    with ExitStack() as stack:
        sc = Scope(nc, name, stack)
        std_ready, xn_ready, turned, inverse = sc.sems("std_ready xn_ready turned inverse")
        xn = sc.sb("xn", [P, T, D])
        block = stack.enter_context(nc.Block())

        @block.sync
        def _(sp):
            load(sp)

        @block.vector
        def _(dve):
            dve.wait_ge(std_ready, 1)
            nc.vector.reciprocal(t.rstd[:], t.std[:]).then_inc(inverse, 1)
            dve.wait_ge(inverse, 1)
            for b in range(B):
                normalise(nc, t, b, xn, t.x, t.x_mv).then_inc(xn_ready, 1)

        @block.scalar
        def _(act):
            nc.scalar.activation(t.std[:], t.x_mv[:, :, 1], ACT.Sqrt, bias=t.eps).then_inc(std_ready, 1)
            for b in range(B):
                for c in range(KC):
                    act.wait_ge(turned, b * KC + c + 1)
                    nc.scalar.copy(t.xnT[:, c, b * S:(b + 1) * S], t.ps[:, b * KC + c, :])

        @block.tensor
        def _(pe):
            for b in range(B):
                pe.wait_ge(xn_ready, b + 1)
                for c in range(KC):
                    for i in range(TB):
                        last = nc.tensor.transpose(t.ps[:, b * KC + c, i * P:(i + 1) * P],
                                                   xn[:, b * TB + i, c * P:(c + 1) * P], t.ident)
                    last.then_inc(turned, 1)


def context_attention(nc, t, io, name, heads, W, W_in, order, scale, rotary, keys_in, limit, gelu, beside=None):
    dh, hc = D // heads, heads // KC
    NK = heads * S2
    NC = NK // KC
    NB = NK // P
    with ExitStack() as outer:
        so = Scope(nc, name, outer)
        w = {n: W[:, :, j, :] for j, n in enumerate(order)}
        qT = so.sb("qT", [P, KC, B * S])
        kd = so.sb("kd", [P, B, KC, hc, S2])
        vd = so.sb("vd", [P, B, NB, 2, dh + 1])
        o = so.sb("o", [P, T, D])
        kT = so.sb("kT", [P, KC, NCTX])

        with ExitStack() as stack:
            sc = Scope(nc, f"{name}_qkv", stack)
            v_ready, v_taken, made, taken, zeroed, k_sum, raw_ready, exchanged = sc.sems(
                "v_ready v_taken made taken zeroed k_sum raw_ready exchanged")
            if rotary:
                raw = sc.sb("raw", [P, 2, S])
                part = sc.sb("part", [P, 2, 2, S])
            jobs = [("k", None, c) for c in range(KC)] + [("q", b, c) for b in range(B) for c in range(KC)]

            def width(job):
                return NCTX if job[0] == "k" else S

            def target(job):
                kind, b, c = job
                return kT[:, c, :] if kind == "k" else qT[:, c, b * S:(b + 1) * S]

            block = stack.enter_context(nc.Block())

            @block.tensor
            def _(pe):
                pe.wait_ge(W_in, 32 if rotary else 16)
                for b in range(B):
                    for kc in range(KC):
                        last = nc.tensor.matmul(t.ps[:, b, 0:D], t.ctxT2[:, kc, b, :, :].rearrange("p a k -> p (a k)"),
                                                w["v"][:, kc, :], start=kc == 0, stop=kc == KC - 1)
                    last.then_inc(v_ready, 1)
                pe.wait_ge(v_taken, B)
                for j in range(len(jobs) + rotary):
                    if j < len(jobs):
                        kind, b, c = jobs[j]
                        if j >= 4:
                            pe.wait_ge(taken, j - 3)
                        src = keys_in if kind == "k" else t.xnT
                        for kc in range(KC):
                            rhs = src[:, kc, :] if kind == "k" else src[:, kc, b * S:(b + 1) * S]
                            last = nc.tensor.matmul(t.ps[:, 2 * (j % 4), 0:width(jobs[j])],
                                                    w[kind][:, kc, c * P:(c + 1) * P], rhs, start=kc == 0, stop=kc == KC - 1)
                        last.then_inc(made, 1)
                    if rotary and j:
                        i = j - 1
                        pe.wait_ge(raw_ready, i + 1)
                        n = width(jobs[i])
                        nc.tensor.matmul(t.ps[:, 2 * (i % 4) + 1, 0:n], t.exchange, raw[:, i % 2, 0:n],
                                         start=True, stop=True).then_inc(exchanged, 1)

            @block.vector
            def _(dve):
                nc.vector.memset(vd[:], 0.0).then_inc(zeroed, 1)
                dve.wait_ge(zeroed, 1)
                for half in range(2):
                    nc.vector.memset(vd[half * 64:half * 64 + 64, :, :, half, dh:dh + 1], 1.0)
                for b in range(B):
                    dve.wait_ge(v_ready, b + 1)
                    for half in range(2):
                        r = slice(half * 64, half * 64 + 64)
                        last = nc.vector.tensor_copy(vd[r, b, :, half, 0:dh],
                                                     by(by(t.ps[r, b, 0:D], 2 * dh), dh)[:, :, half, :])
                    last.then_inc(v_taken, 1)
                if rotary:
                    dve.wait_ge(W_in, 32)
                    for j, job in enumerate(jobs):
                        n = width(job)
                        dve.wait_ge(raw_ready, j + 1)
                        if j >= 2:
                            dve.wait_ge(k_sum, j - 1)
                        for a in range(2):
                            if a:
                                dve.wait_ge(exchanged, j + 1)
                            src, table = (raw[:, j % 2, 0:n], t.ps[:, 2 * (j % 4) + 1, 0:n])[a], t.rot[a]
                            out = part[:, j % 2, a, 0:n]
                            if job[0] == "k":
                                src, out, table = by(src, S2), by(out, S2), bcast(table[:, 0:S2], 1, B)
                            last = nc.vector.tensor_tensor(out, src, table, ALU.mult)
                        last.then_inc(taken, 1)
                if beside:
                    beside(dve)
                dve.wait_ge(k_sum if rotary else taken, KC)
                for b in range(B):
                    for c in range(KC):
                        nc.vector.tensor_tensor(kd[:, b, c, :, :], bcast(kT[:, c, b * S2:(b + 1) * S2], 1, hc),
                                                bcast(t.heads[heads], 2, S2), ALU.mult)

            if rotary:
                @block.gpsimd
                def _(pool):
                    for j, job in enumerate(jobs):
                        pool.wait_ge(taken, j + 1)
                        n = width(job)
                        nc.gpsimd.tensor_tensor(target(job), part[:, j % 2, 0, 0:n], part[:, j % 2, 1, 0:n], ALU.add)\
                            .then_inc(k_sum, 1)

            @block.scalar
            def _(act):
                for j, job in enumerate(jobs):
                    act.wait_ge(made, j + 1)
                    n = width(job)
                    if rotary and j >= 2:
                        act.wait_ge(taken, j - 1)
                    out, done = (raw[:, j % 2, 0:n], raw_ready) if rotary else (target(job), taken)
                    nc.scalar.copy(out, t.ps[:, 2 * (j % 4), 0:n]).then_inc(done, 1)

        TURN, LAG, DEEP = 2, 3, 4
        with ExitStack() as stack:
            sc = Scope(nc, f"{name}_attend", stack)
            scores_ready, bounded, max_ready, centred, exp_ready, p_turned, p_evacuated, o_ready, o_taken, \
                rsum_ready, stats_ready = sc.sems("scores_ready bounded max_ready centred exp_ready p_turned p_evacuated o_ready o_taken "
                        "rsum_ready stats_ready")
            prob = sc.sb("prob", [P, DEEP, NK])
            probT = sc.sb("probT", [P, 2, NB * P])
            mx = sc.sb("mx", [P, DEEP, heads])
            rsum = sc.sb("rsum", [P, 2, heads])
            block = stack.enter_context(nc.Block())

            @block.tensor
            def _(pe):
                for i in range(T + LAG):
                    if i < T:
                        b = i // TB
                        if i >= 2:
                            pe.wait_ge(bounded, i - 1)
                        for c in range(KC):
                            last = nc.tensor.matmul(t.ps[:, 2 * (i % 2) + c, 0:NC], qT[:, c, i * P:(i + 1) * P],
                                                    kd[:, b, c, :, :].rearrange("p h k -> p (h k)"), start=True, stop=True)
                        last.then_inc(scores_ready, 1)
                    if TURN <= i < T + TURN:
                        j = i - TURN
                        pe.wait_ge(exp_ready, j + 1)
                        if j:
                            pe.wait_ge(p_evacuated, j)
                        for n in range(NB):
                            last = nc.tensor.transpose(t.ps[:, 4 + n // 4, (n % 4) * P:(n % 4 + 1) * P],
                                                       prob[:, j % DEEP, n * P:(n + 1) * P], t.ident)
                        last.then_inc(p_turned, 1)
                    if i >= LAG:
                        j = i - LAG
                        pe.wait_ge(p_evacuated, j + 1)
                        if j >= 2:
                            pe.wait_ge(o_taken, j - 1)
                        for n in range(NB):
                            cols = slice(n * 2 * (dh + 1), (n + 1) * 2 * (dh + 1))
                            last = nc.tensor.matmul(t.ps[:, 6 + j % 2, cols], probT[:, j % 2, n * P:(n + 1) * P],
                                                    vd[:, j // TB, n, :, :].rearrange("p a d -> p (a d)"),
                                                    start=True, stop=True)
                        last.then_inc(o_ready, 1)

            @block.vector
            def _(dve):
                for i in range(T + LAG + gelu):
                    if i < T:
                        dve.wait_ge(scores_ready, i + 1)
                        if i >= DEEP:
                            dve.wait_ge(p_turned, i - DEEP + 1)
                        banks = t.ps[:, 2 * (i % 2):2 * (i % 2) + KC, 0:NC]
                        out = prob[:, i % DEEP, :].rearrange("p (c n) -> p c n", c=KC)
                        if limit is None:
                            b = i // TB
                            for c in range(KC):
                                ins = nc.vector.tensor_tensor(by(out[:, c, :], S2), by(banks[:, c, :], S2),
                                                              bcast(t.bound[:, b * S2:(b + 1) * S2], 1, hc), ALU.min)
                        else:
                            ins = nc.vector.tensor_scalar(out, banks, limit, -limit, ALU.min, ALU.max)
                        ins.then_inc(bounded, 1)
                        dve.wait_ge(bounded, i + 1)
                        nc.vector.tensor_reduce(mx[:, i % DEEP, :], by(prob[:, i % DEEP, :], S2), AX.X, ALU.max)\
                            .then_inc(max_ready, 1)
                    if LAG <= i < T + LAG:
                        j = i - LAG
                        dve.wait_ge(o_ready, j + 1)
                        sums = by(t.ps[:, 6 + j % 2, 0:heads * (dh + 1)], dh + 1)
                        if j >= 2:
                            dve.wait_ge(o_taken, j - 1)
                        nc.vector.reciprocal(rsum[:, j % 2, :], sums[:, :, dh]).then_inc(rsum_ready, 1)
                        dve.wait_ge(rsum_ready, j + 1)
                        nc.vector.tensor_tensor(by(o[:, j, :], dh), sums[:, :, 0:dh], bcast(rsum[:, j % 2, :], 2, dh),
                                                ALU.mult).then_inc(o_taken, 1)
                    if gelu and i > LAG and (i - LAG) % TB == 0:
                        b = (i - LAG) // TB - 1
                        dve.wait_ge(o_taken, (b + 1) * TB)
                        for j in range(b * TB, (b + 1) * TB):
                            last = nc.vector.bn_stats(t.stats[:, j, :], o[:, j, :])
                        last.then_inc(stats_ready, 1)
                        dve.wait_ge(stats_ready, b + 1)
                        for j in range(b * TB, (b + 1) * TB):
                            nc.vector.bn_aggr(t.mv[:, j, :], t.stats[:, j, :])

            @block.gpsimd
            def _(pool):
                for i in range(T):
                    pool.wait_ge(max_ready, i + 1)
                    pr = by(prob[:, i % DEEP, :], S2)
                    nc.gpsimd.tensor_tensor(pr, pr, bcast(mx[:, i % DEEP, :], 2, S2), ALU.subtract).then_inc(centred, 1)

            @block.scalar
            def _(act):
                for i in range(T + TURN):
                    if i >= TURN:
                        j = i - TURN
                        act.wait_ge(p_turned, j + 1)
                        if j >= 2:
                            act.wait_ge(o_ready, j - 1)
                        n = NB * P // 512
                        nc.scalar.copy(probT[:, j % 2, :].rearrange("p (a n) -> p a n", a=n), t.ps[:, 4:4 + n, :])\
                            .then_inc(p_evacuated, 1)
                    if i < T:
                        act.wait_ge(centred, i + 1)
                        nc.scalar.activation(prob[:, i % DEEP, :], prob[:, i % DEEP, :], ACT.Exp, scale=scale)\
                            .then_inc(exp_ready, 1)

        (gelu_stage if gelu else project_stage)(nc, t, io, f"{name}_out", o, w["o"])


def project_stage(nc, t, io, name, o, w_out):
    with ExitStack() as stack:
        sc = Scope(nc, name, stack)
        own, turned, evacuated, y_ready, y_added = sc.sems("own turned evacuated y_ready y_added")
        oT = sc.sb("oT", [P, 2, KC * P])
        block = stack.enter_context(nc.Block())

        @block.tensor
        def _(pe):
            for i in range(T + 1):
                if i < T:
                    if i >= 2:
                        pe.wait_ge(evacuated, i - 1)
                    for c in range(KC):
                        last = nc.tensor.transpose(t.ps[:, i % 2, c * P:(c + 1) * P], o[:, i, c * P:(c + 1) * P], t.ident)
                    last.then_inc(turned, 1)
                if i:
                    j = i - 1
                    pe.wait_ge(evacuated, j + 1)
                    if j >= 2:
                        pe.wait_ge(y_added, j - 1)
                    for kc in range(KC):
                        last = nc.tensor.matmul(t.ps[:, 2 + j % 2, 0:D], oT[:, j % 2, kc * P:(kc + 1) * P],
                                                w_out[:, kc, :], start=kc == 0, stop=kc == KC - 1)
                    last.then_inc(y_ready, 1)

        @block.scalar
        def _(act):
            for i in range(T):
                act.wait_ge(turned, i + 1)
                if i >= 2:
                    act.wait_ge(y_ready, i - 1)
                nc.scalar.copy(oT[:, i % 2, :], t.ps[:, i % 2, 0:KC * P]).then_inc(evacuated, 1)

        @block.vector
        def _(dve):
            steps = Steps(dve, own)
            for j in range(T):
                dve.wait_ge(y_ready, j + 1)
                nc.vector.tensor_tensor(t.x[:, j, :], t.x[:, j, :], t.ps[:, 2 + j % 2, 0:D], ALU.add).then_inc(y_added, 1)
                if j % TB == TB - 1:
                    dve.wait_ge(y_added, j + 1)
                    x_moments(nc, t, steps, j // TB)


def gelu_stage(nc, t, io, name, o, w_out):
    HELD = 6
    with ExitStack() as stack:
        sc = Scope(nc, name, stack)
        cols_in, own, std_ready, inverse, normed, turned, evacuated, returned, v_added, y_ready, gelu_ready, \
            x_added = sc.sems("cols_in own std_ready inverse normed turned evacuated returned v_added y_ready gelu_ready x_added")
        cols = sc.sb("cols", [P, 2, KC])
        vT = sc.sb("vT", [P, 2, KC, P])
        gl = sc.sb("gl", [P, HELD, D])
        block = stack.enter_context(nc.Block())

        @block.sync
        def _(sp):
            sp.dma_start(cols[:], io["a1_cols"]).then_inc(cols_in, 16)

        @block.tensor
        def _(pe):
            for i in range(T + 1):
                if i < T:
                    pe.wait_ge(normed, i // TB + 1)
                    if i >= 2:
                        pe.wait_ge(evacuated, i - 1)
                    for c in range(KC):
                        last = nc.tensor.transpose(t.ps[:, i % 2, c * P:(c + 1) * P], o[:, i, c * P:(c + 1) * P], t.ident)
                    last.then_inc(turned, 1)
                if i:
                    j = i - 1
                    pe.wait_ge(evacuated, j + 1)
                    if j >= 2:
                        pe.wait_ge(v_added, j - 1)
                    for c in range(KC):
                        last = nc.tensor.transpose(t.ps[:, 4 + j % 2, c * P:(c + 1) * P], vT[:, j % 2, c, :], t.ident)
                    last.then_inc(returned, 1)
                    if j >= 2:
                        pe.wait_ge(gelu_ready, j - 1)
                    for kc in range(KC):
                        last = nc.tensor.matmul(t.ps[:, 2 + j % 2, 0:D], vT[:, j % 2, kc, :], w_out[:, kc, :],
                                                start=kc == 0, stop=kc == KC - 1)
                    last.then_inc(y_ready, 1)

        @block.scalar
        def _(act):
            nc.scalar.activation(t.std[:], t.mv[:, :, 1], ACT.Sqrt, bias=t.eps).then_inc(std_ready, 1)
            act.wait_ge(cols_in, 16)
            for i in range(T + 1):
                if i < T:
                    act.wait_ge(turned, i + 1)
                    if i >= 2:
                        act.wait_ge(y_ready, i - 1)
                    for c in range(KC):
                        last = nc.scalar.activation(vT[:, i % 2, c, :], t.ps[:, i % 2, c * P:(c + 1) * P], ACT.Identity,
                                                    bias=cols[:, 1, c:c + 1], scale=cols[:, 0, c:c + 1])
                    last.then_inc(evacuated, 1)
                if i:
                    j = i - 1
                    act.wait_ge(y_ready, j + 1)
                    if j >= HELD:
                        act.wait_ge(x_added, j - HELD + 1)
                    nc.scalar.activation(gl[:, j % HELD, :], t.ps[:, 2 + j % 2, 0:D], ACT.Gelu).then_inc(gelu_ready, 1)

        @block.gpsimd
        def _(pool):
            for j in range(T):
                pool.wait_ge(v_added, j + 1)
                pool.wait_ge(gelu_ready, j + 1)
                nc.gpsimd.tensor_tensor(t.x[:, j, :], t.x[:, j, :], gl[:, j % HELD, :], ALU.add).then_inc(x_added, 1)

        @block.vector
        def _(dve):
            steps = Steps(dve, own)
            dve.wait_ge(std_ready, 1)
            nc.vector.reciprocal(t.rstd[:], t.std[:]).then_inc(inverse, 1)
            dve.wait_ge(inverse, 1)
            for b in range(B):
                normalise(nc, t, b, o, o, t.mv).then_inc(normed, 1)
            for b in range(B + 1):
                if b < B:
                    for j in range(b * TB, (b + 1) * TB):
                        dve.wait_ge(returned, j + 1)
                        nc.vector.tensor_tensor(t.x[:, j, :], t.x[:, j, :], t.ps[:, 4 + j % 2, 0:D], ALU.add)\
                            .then_inc(v_added, 1)
                if b:
                    dve.wait_ge(x_added, b * TB)
                    x_moments(nc, t, steps, b - 1)


PAIRS = E * B
PICKS = 6


def round_steps(n):
    now, before, after, later = (0 <= m < PAIRS for m in (n, n - 1, n + 1, n + 2))
    at = {}

    def put(on, slot, place, *step):
        if on:
            at.setdefault((slot, place), []).append(step)

    for g in range(HE // G4):
        last = g == HE // G4 - 1
        for k in range(TB):
            put(before if last else now, (G4 * (g + 1)) % HE + k, 2, "values", n - last, g * TB + k)
    put(later, 0, 0, "project", n + 2, 0)
    put(later, 2, 0, "project", n + 2, 1)
    put(after, 4, 0, "project_v", n + 1, 0)
    put(later, 6, 0, "project", n + 2, 2)
    put(later, 8, 0, "project", n + 2, 3)
    put(before, 10, 0, "add", n - 1, 0)
    put(before, 12, 0, "add", n - 1, 1)
    put(after, 14, 0, "project_v", n + 1, 1)
    put(before, 1, 0, "turn_out", n - 1, 2)
    put(now, 3, 0, "row_max", n, 1)
    put(before, 5, 0, "turn_out", n - 1, 3)
    put(before, 7, 0, "turn_norm", n - 1, 1)
    put(now, 9, 0, "turn_out", n, 0)
    put(after, 11, 0, "row_max", n + 1, 0)
    put(now, 13, 0, "turn_out", n, 1)
    put(now, 15, 0, "turn_norm", n, 0)
    if n == -2:
        for b, slot in enumerate((1, 3, 4, 7)):
            put(True, slot, 0, "route_hidden", None, b)
        put(True, 9, 0, "route_norm", None, None)
    if n == -1:
        for b, slot in enumerate((0, 1, 2, 3)):
            put(True, slot, 1, "route_turn", None, b)
        put(True, 4, 1, "route_logits", None, None)
        for i in range(PICKS):
            put(True, 5 + i, 1, "route_pick", None, i)
        for b in range(B):
            put(True, 10 + b // 2, 2, "route_gates", None, b)
        for j in range(T // 2):
            put(True, 12 + j // 2, 1 + j % 2, "route_bias", None, j)
    steps = []
    for h in range(HE):
        steps += at.get((h, 0), [])
        steps += [("maxima", n + 1, 2 * h)] * after
        steps += at.get((h, 1), [])
        steps += [("attend", n, 2 * h)] * now
        steps += [("maxima", n + 1, 2 * h + 1)] * after
        steps += at.get((h, 2), [])
        steps += [("attend", n, 2 * h + 1)] * now
    return steps


ROUNDS = range(-2, PAIRS + 1)
MISC = ("turn_out", "row_max", "turn_norm", "project", "add", "project_v")
MISC_LIST = [s for n in ROUNDS for s in round_steps(n) if s[0] in MISC]
MISC_AT = {step: i for i, step in enumerate(MISC_LIST)}


ROUTE_LIST = [s for n in (-2, -1) for s in round_steps(n)
              if s[0] in ("route_hidden", "route_turn", "route_logits", "route_gates", "route_bias")]
ROUTE_AT = {(kind, a): i for i, (kind, _, a) in enumerate(ROUTE_LIST)}


def ring_slot(n, h):
    return h % RING


def values_before(n, h):
    k = n * HE + h
    for j in range(k - 1, k - HE - RING, -1):
        if j >= 0 and ring_slot(*divmod(j, HE)) == ring_slot(n, h):
            return j // G4 + 1
    return 0


class Rounds:

    def __init__(self, engine, nc, steps):
        self.engine, self.expert = engine, None
        self.n = 0
        for self.n in range(-2, B):
            self.walk(steps)
        with engine.Fori(1, E - 1) as self.expert:
            for self.n in range(B, 2 * B):
                self.walk(steps)
        self.expert = None
        for self.n in range((E - 1) * B, PAIRS + 1):
            self.walk(steps)

    def walk(self, steps):
        start = steps.get("start")
        if start:
            start(self, self.n)
        for kind, m, arg in round_steps(self.n):
            if kind in steps:
                steps[kind](self, m, arg)
        end = steps.get("end")
        if end:
            end(self, self.n)

    def value(self, count, *args):
        m, rest = args[0], args[1:]
        v = count(m, *rest)
        if self.expert is None:
            return v
        step = count(m + B, *rest) - v
        assert v > 0 and step >= 0 and count(m + 2 * B, *rest) - v == 2 * step
        return self.expert * step + (v - step) if step else v

    def wait(self, semaphore, count, *args):
        v = self.value(count, *args)
        if self.expert is not None or v > 0:
            self.engine.wait_ge(semaphore, v)

    def expert_of(self, m):
        return m // B if self.expert is None else self.expert + (m // B - 1)


QW = 4 * KC * P + 4
VW = KC * D + D


class ExpertWeights:

    def __init__(self, sc, io):
        self.buffers = [sc.sb(n, [P, w]) for n, w in (("wqk", QW), ("wv", VW), ("wo", KC * D))]
        self.semaphores = sc.sems("wqk_in wv_in wo_in")
        self.sources = [io[n] for n in ("e_qk", "e_v", "e_o")]

    def load_first(self, sp):
        for buffer, src, semaphore in zip(self.buffers, self.sources, self.semaphores):
            sp.dma_start(buffer[:], src[0]).then_inc(semaphore, 16)


def expert_stage(nc, t, io, weights):
    with ExitStack() as stack:
        sc = Scope(nc, "experts", stack)
        wqk_in, wv_in, wo_in = weights.semaphores
        qk_moved, max_moved = sc.sems("qk_moved0 qk_moved1"), sc.sems("max_moved0 max_moved1")
        max_scores, maxed, scores, exped, summed, out_taken = sc.sems("max_scores maxed scores exped summed out_taken")
        misc_made, added, high_ready, rest_ready, mid_ready, low_ready, max_high, max_split, inverse, normed, \
            gate_ready, k_ones, v_ones, v_taken, turned_taken, sum_clear, own = sc.sems(
                "misc_made added high_ready rest_ready mid_ready low_ready max_high max_split inverse normed "
                "gate_ready k_ones v_ones v_taken turned_taken sum_clear own")
        wqk, wv, wo = weights.buffers
        qs = [sc.sb(f"qs{i}", [MAX_ROWS, HE, S], BF16) for i in range(2)]
        ks = [sc.sb(f"ks{i}", [MAX_ROWS, HE, S], BF16) for i in range(2)]
        parts = sc.sb("parts", [P, 4, 3, S], BF16)
        rest = sc.sb("rest", [P, 2, S])
        vs = [sc.sb(f"vs{i}", [P, TB, HE, DH + 1]) for i in range(2)]
        prob = sc.sb("prob", [P, RING, TB, S])
        out_sb = sc.sb("out_sb", [P, S])
        rinv = sc.sb("rinv", [P, TB, G4])
        on = sc.sb("on", [P, TB, D])
        onT = sc.sb("onT", [P, KC, S])
        nmx = sc.sb("nmx", [P, TB, HE])
        nm = sc.sb("nm", [HC, 2, S], BF16)
        gate = sc.sb("gate", [P, TB])
        ROUTE_HEAD = RING - 4
        assert T * R1 == TB * S and T * P == TB * S
        r_h = prob[:, RING - 1, :, :].rearrange("p a n -> p (a n)").rearrange("p (k n) -> p k n", n=R1)
        r_hT = prob[:, RING - 2, :, :].rearrange("p a n -> p (a n)")
        r_gT = prob[0:E, RING - 3, :, :].rearrange("p a n -> p (a n)")
        small = prob[:, ROUTE_HEAD, :, :].rearrange("p a n -> p (a n)")
        widths = (KC * R1, R1 + E, 2 + E, D, T * E, T * E, T * E, 2 * T * E, T)
        r_w1, r_rows, r_cols, r_ob, r_lg, r_pr, r_cand, r_pick, r_one = [
            small[:, sum(widths[:i]):sum(widths[:i + 1])] for i in range(len(widths))]
        r_w1, r_lg, r_pr, r_cand = by(r_w1, R1), by(r_lg, E), by(r_pr, E), by(r_cand, E)
        r_pick = r_pick.rearrange("p (a k e) -> p a k e", a=2, e=E)
        r_loads = ((r_w1, io["rW1"]), (r_rows, io["r_rows"]), (r_cols, io["r_cols"]), (r_ob[0:E, :], io["ob"]))
        r_loaded, r_made, r_hidden, r_var, r_std, r_normed, r_relu, r_logits, r_centred, r_exp, r_gates, r_turned, r_bias \
            = sc.sems("r_loaded r_made r_hidden r_var r_std r_normed r_relu r_logits r_centred r_exp r_gates r_turned r_bias")
        r_freed = {"route_hidden": r_hidden, "route_turn": r_relu, "route_logits": r_logits, "route_gates": r_turned,
                   "route_bias": r_bias}

        def route_bank(kind, a):
            return t.ps[:, 4 + ROUTE_AT[kind, a] % 2, :]

        MX = t.ps[:, 0:4, :]
        EX = t.ps[:, 4:6, :]
        OUT = t.ps[:, 6, :]
        SH = t.ps[:, 7, :]

        max_count = lambda m, h, half: m * 2 * HE + 2 * h + half + 1
        score_count = lambda m, h, k: m * HE * TB + h * TB + k + 1
        sum_count = lambda m, g: m * HE // G4 + g + 1
        moved_count = lambda m: 16 * 2 * len(Q_PARTS) * (m + 1)
        max_moved_count = lambda m: 16 * 2 * (m + 1)
        row_count = lambda m, c: m * KC + c + 1
        value_count = lambda m, half: 2 * m + half + 1
        misc_count = lambda m, kind, a: MISC_AT[kind, m, a] + 1
        project_count = lambda m, a: 4 * m + a + 1
        freed = {"turn_out": (normed, sum_count), "row_max": (max_split, row_count), "turn_norm": (turned_taken, row_count),
                 "project": (rest_ready, project_count), "project_v": (v_taken, value_count), "add": (added, value_count)}
        block = stack.enter_context(nc.Block())

        @block.sync
        def _(sp):
            def load_qk(e):
                sp.dma_start(wqk[:], io["e_qk"][e]).then_inc(wqk_in, 16)

            def load_v(e):
                sp.dma_start(wv[:], io["e_v"][e]).then_inc(wv_in, 16)

            def load_o(e):
                sp.dma_start(wo[:], io["e_o"][e]).then_inc(wo_in, 16)

            def move_split(r, m, c):
                r.wait(low_ready, project_count, m, 2 * c + 1)
                for a, (dst, order) in enumerate(((qs[m % 2], Q_PARTS), (ks[m % 2], K_PARTS))):
                    for g, part in enumerate(order):
                        sp.dma_start(dst[g * DH:(g + 1) * DH, c * HC:(c + 1) * HC, :], parts[:, 2 * c + a, part, :])\
                            .then_inc(qk_moved[c], 16)

            def move_max(r, m, c):
                r.wait(max_split, row_count, m, c)
                for a in range(2):
                    sp.dma_start(qs[m % 2][SPLIT_ROWS + a:SPLIT_ROWS + a + 1, c * HC:(c + 1) * HC, :], nm[:, a, :])\
                        .then_inc(max_moved[c], 16)

            def start(r, n):
                if 0 <= n + 1 < PAIRS:
                    move_split(r, n + 1, 1)

            def step(r, m, a):
                move_max(r, m, a)

            def projected(r, m, a):
                if a == 3:
                    move_split(r, m, 0)

            def end(r, n):
                for m, semaphore, count, last, load in ((n + 2, rest_ready, project_count, 3, load_qk),
                                                        (n + 1, v_taken, value_count, 1, load_v),
                                                        (n - 1, misc_made, lambda m, a: misc_count(m, "add", a), 1, load_o)):
                    if m % B == B - 1 and B - 1 <= m < PAIRS - 1:
                        r.wait(semaphore, count, m, last)
                        if r.expert is not None:
                            sp.wait_ge(semaphore, 1)
                        load(r.expert_of(m + 1))

            for out, src in r_loads:
                sp.dma_start(out, src).then_inc(r_loaded, 16)
            Rounds(sp, nc, {"start": start, "row_max": step, "project": projected, "end": end})

        @block.tensor
        def _(pe):
            def shared(r, kind, m, a):
                at = MISC_AT[kind, m, a]
                if at:
                    kind, m, a = MISC_LIST[at - 1]
                    r.wait(*freed[kind], m, a)

            def route_free(kind, a):
                at = ROUTE_AT[kind, a]
                if at >= 2:
                    before, _, n = ROUTE_LIST[at - 2]
                    pe.wait_ge(r_freed[before], (n or 0) + 1)

            def route_hidden(r, _, b):
                if b == 0:
                    pe.wait_ge(r_loaded, 16 * len(r_loads))
                route_free("route_hidden", b)
                for i in range(TB):
                    k = b * TB + i
                    for kc in range(KC):
                        last = nc.tensor.matmul(route_bank("route_hidden", b)[:, i * R1:(i + 1) * R1],
                                                t.xnT[:, kc, k * P:(k + 1) * P], r_w1[:, kc, :],
                                                start=kc == 0, stop=kc == KC - 1)
                last.then_inc(r_made, 1)

            def route_turn(r, _, b):
                route_free("route_turn", b)
                pe.wait_ge(r_normed, b + 1)
                for i in range(TB):
                    last = nc.tensor.transpose(route_bank("route_turn", b)[:, i * P:(i + 1) * P], r_h[:, b * TB + i, :],
                                               t.ident)
                last.then_inc(r_made, 1)

            def route_logits(r, _, a):
                route_free("route_logits", a)
                pe.wait_ge(r_relu, B)
                for k in range(T):
                    last = nc.tensor.matmul(route_bank("route_logits", a)[:, k * E:(k + 1) * E],
                                            r_hT[:, k * P:(k + 1) * P], r_cols[:, 2:2 + E], start=True, stop=True)
                last.then_inc(r_made, 1)

            def route_gates(r, _, b):
                route_free("route_gates", b)
                pe.wait_ge(r_gates, 1)
                for i in range(TB):
                    last = nc.tensor.transpose(route_bank("route_gates", b)[0:E, i * P:(i + 1) * P],
                                               t.gates[:, :, b * TB + i], t.ident)
                last.then_inc(r_made, 1)

            def route_bias(r, _, j):
                route_free("route_bias", j)
                pe.wait_ge(r_turned, 2 * j // TB + 1)
                for i in range(2):
                    k = 2 * j + i
                    last = nc.tensor.matmul(route_bank("route_bias", j)[:, i * D:(i + 1) * D], r_gT[:, k * P:(k + 1) * P],
                                            r_ob[0:E, :], start=True, stop=True)
                last.then_inc(r_made, 1)

            def maxima(r, m, a):
                h, half = divmod(a, 2)
                if h % HC == 0 and half == 0:
                    r.wait(qk_moved[h // HC], moved_count, m)
                r.wait(maxed, lambda m: max_count(m, h, half) - 2, m)
                for q in range(2 * half, 2 * half + 2):
                    last = nc.tensor.matmul(MX[:, q, :], qs[m % 2][0:SPLIT_ROWS, h, q * P:(q + 1) * P],
                                            ks[m % 2][0:SPLIT_ROWS, h, :], start=True, stop=True)
                last.then_inc(max_scores, 1)

            def attend(r, m, a):
                h, half = divmod(a, 2)
                if h % HC == 0 and half == 0:
                    r.wait(max_moved[h // HC], max_moved_count, m)
                if 0 <= m < 2 and r.expert is None and a == 0:
                    pe.wait_ge(k_ones, m + 1)
                    pe.wait_ge(r_bias, T // 2)
                for k in (2 * half, 2 * half + 1):
                    r.wait(exped, lambda m: score_count(m, h, k) - 2, m)
                    nc.tensor.matmul(EX[:, k % 2, :], ks[m % 2][:, h, k * P:(k + 1) * P], qs[m % 2][:, h, :],
                                     start=True, stop=True).then_inc(scores, 1)

            def values(r, m, a):
                g, k = divmod(a, TB)
                if k == 0:
                    r.wait(exped, score_count, m, G4 * g + G4 - 1, TB - 1)
                    r.wait(out_taken, lambda m: sum_count(m, g) - 1, m)
                if m == 0 and a == 0:
                    pe.wait_ge(sum_clear, 1)
                    pe.wait_ge(v_ones, 2)
                if a == 0:
                    r.wait(v_taken, value_count, m, 1)
                for j in range(G4):
                    h = G4 * g + j
                    last = nc.tensor.matmul(OUT[32 * j:32 * j + DH + 1, :], vs[m % 2][:, k, h, :],
                                            prob[:, ring_slot(m, h), k, :], start=k == 0, stop=k == TB - 1)
                if k == TB - 1:
                    last.then_inc(summed, 1)

            def turn_out(r, m, g):
                shared(r, "turn_out", m, g)
                r.wait(out_taken, sum_count, m, g)
                for q in range(TB):
                    last = nc.tensor.transpose(SH[:, q * P:(q + 1) * P], out_sb[:, q * P:(q + 1) * P], t.ident)
                last.then_inc(misc_made, 1)

            def row_max(r, m, c):
                shared(r, "row_max", m, c)
                r.wait(maxed, max_count, m, HC * (c + 1) - 1, 1)
                for q in range(TB):
                    last = nc.tensor.transpose(SH[0:HC, q * P:(q + 1) * P], nmx[:, q, c * HC:(c + 1) * HC], t.ident)
                last.then_inc(misc_made, 1)

            def turn_norm(r, m, c):
                shared(r, "turn_norm", m, c)
                r.wait(normed, lambda m: sum_count(m, 2 * c + 1), m)
                for q in range(TB):
                    last = nc.tensor.transpose(SH[:, q * P:(q + 1) * P], on[:, q, c * P:(c + 1) * P], t.ident)
                last.then_inc(misc_made, 1)

            def project(r, m, a):
                shared(r, "project", m, a)
                c, w = divmod(a, 2)
                if m % B == 0 and a == 0:
                    r.wait(wqk_in, lambda m: 16 * (m // B + 1), m)
                for kc in range(KC):
                    col = ((w * KC + c) * KC + kc) * P
                    last = nc.tensor.matmul(SH, wqk[:, col:col + P], t.xnT[:, kc, (m % B) * S:(m % B + 1) * S],
                                            start=kc == 0, stop=kc == KC - 1)
                last.then_inc(misc_made, 1)

            def project_v(r, m, half):
                shared(r, "project_v", m, half)
                if m % B == 0 and half == 0:
                    r.wait(wv_in, lambda m: 16 * (m // B + 1), m)
                for i in range(2):
                    tok = (m % B) * S + (2 * half + i) * P
                    for kc in range(KC):
                        last = nc.tensor.matmul(SH[:, i * D:(i + 1) * D], t.xnT[:, kc, tok:tok + P],
                                                wv[:, kc * D:(kc + 1) * D], start=kc == 0, stop=kc == KC - 1)
                last.then_inc(misc_made, 1)

            def add(r, m, half):
                shared(r, "add", m, half)
                if half == 0:
                    r.wait(turned_taken, row_count, m, KC - 1)
                    if m % B == 0:
                        r.wait(wo_in, lambda m: 16 * (m // B + 1), m)
                for i in range(2):
                    q = 2 * half + i
                    for kc in range(KC):
                        last = nc.tensor.matmul(SH[:, i * D:(i + 1) * D], onT[:, kc, q * P:(q + 1) * P],
                                                wo[:, kc * D:(kc + 1) * D], start=kc == 0, stop=kc == KC - 1)
                last.then_inc(misc_made, 1)

            Rounds(pe, nc, {"maxima": maxima, "attend": attend, "values": values, "turn_out": turn_out,
                            "row_max": row_max, "turn_norm": turn_norm, "project": project, "project_v": project_v,
                            "add": add, "route_hidden": route_hidden, "route_turn": route_turn,
                            "route_logits": route_logits, "route_gates": route_gates, "route_bias": route_bias})

        @block.scalar
        def _(act):
            def route_norm(r, _, a):
                for b in range(B):
                    tiles = slice(b * TB, (b + 1) * TB)
                    act.wait_ge(r_var, b + 1)
                    nc.scalar.activation(t.std[:, tiles], t.mv[:, tiles, 1], ACT.Sqrt, bias=t.eps).then_inc(r_std, 1)

            def route_turn(r, _, b):
                act.wait_ge(r_made, ROUTE_AT["route_turn", b] + 1)
                nc.scalar.activation(r_hT[:, b * S:(b + 1) * S], route_bank("route_turn", b), ACT.Relu,
                                     bias=r_cols[:, 1:2], scale=r_cols[:, 0:1]).then_inc(r_relu, 1)

            def route_pick(r, _, i):
                if i == 1:
                    act.wait_ge(r_centred, 1)
                    nc.scalar.activation(r_pr, r_lg, ACT.Exp).then_inc(r_exp, 1)

            def route_gates(r, _, b):
                act.wait_ge(r_made, ROUTE_AT["route_gates", b] + 1)
                nc.scalar.copy(r_gT[:, b * S:(b + 1) * S], route_bank("route_gates", b)[0:E, :]).then_inc(r_turned, 1)

            def attend(r, m, a):
                h, half = divmod(a, 2)
                if m == 0 and r.expert is None and a == 2 * ROUTE_HEAD:
                    act.wait_ge(r_bias, T // 2)
                if half == 0:
                    r.wait(summed, lambda m: values_before(m, h), m)
                for k in (2 * half, 2 * half + 1):
                    r.wait(scores, score_count, m, h, k)
                    nc.scalar.activation(prob[:, ring_slot(m, h), k, :], EX[:, k % 2, :], ACT.Exp, scale=DH ** -0.5)\
                        .then_inc(exped, 1)

            def project(r, m, a):
                r.wait(misc_made, misc_count, m, "project", a)
                if m >= 1:
                    r.wait(qk_moved[a // 2], moved_count, m - 1)
                w = a % 2
                bias = wqk[:, 4 * KC * P + w * KC + a // 2:4 * KC * P + w * KC + a // 2 + 1]
                nc.scalar.activation(parts[:, a, 0, :], SH, ACT.Identity, bias=bias).then_inc(high_ready, 1)

            def values(r, m, a):
                g, k = divmod(a, TB)
                if k < TB - 1:
                    return
                r.wait(summed, sum_count, m, g)
                if m * (HE // G4) + g >= 1:
                    pm, pg = divmod(m * (HE // G4) + g - 1, HE // G4)
                    r.wait(misc_made, lambda x: misc_count(x, "turn_out", pg), pm)
                nc.scalar.copy(out_sb[:], OUT).then_inc(out_taken, 1)

            def turn_norm(r, m, c):
                r.wait(misc_made, misc_count, m, "turn_norm", c)
                nc.scalar.copy(onT[:, c, :], SH).then_inc(turned_taken, 1)

            Rounds(act, nc, {"attend": attend, "project": project, "values": values, "turn_norm": turn_norm,
                             "route_norm": route_norm, "route_turn": route_turn, "route_pick": route_pick,
                             "route_gates": route_gates})

        @block.vector
        def _(dve):
            def maxima(r, m, a):
                h, half = divmod(a, 2)
                two = slice(2 * half, 2 * half + 2)
                r.wait(max_scores, max_count, m, h, half)
                nc.vector.tensor_reduce(nmx[:, two, h], MX[:, two, :], AX.X, ALU.max, negate=True).then_inc(maxed, 1)

            def project(r, m, a):
                r.wait(high_ready, project_count, m, a)
                k = 4 * m + a
                if k >= 2:
                    r.wait(low_ready, lambda m: project_count(m, a) - 2, m)
                w = a % 2
                bias = wqk[:, 4 * KC * P + w * KC + a // 2:4 * KC * P + w * KC + a // 2 + 1]
                nc.vector.scalar_tensor_tensor(rest[:, a % 2, :], SH, bias, parts[:, a, 0, :], ALU.add, ALU.subtract)\
                    .then_inc(rest_ready, 1)

            def project_v(r, m, half):
                r.wait(misc_made, misc_count, m, "project_v", half)
                if m >= 2:
                    r.wait(summed, sum_count, m - 2, HE // G4 - 1)
                for i in range(2):
                    last = nc.vector.tensor_tensor(vs[m % 2][:, 2 * half + i, :, 0:DH], by(SH[:, i * D:(i + 1) * D], DH),
                                                   by(wv[:, KC * D:VW], DH), ALU.add)
                last.then_inc(v_taken, 1)

            def row_max(r, m, c):
                r.wait(misc_made, misc_count, m, "row_max", c)
                if c:
                    r.wait(max_moved[0], max_moved_count, m)
                elif m >= 1:
                    r.wait(max_moved[1], max_moved_count, m - 1)
                nc.vector.tensor_copy(nm[:, 0, :], SH[0:HC, :]).then_inc(max_high, 1)
                r.wait(max_high, row_count, m, c)
                if m >= 2:
                    r.wait(scores, score_count, m - 2, HC * (c + 1) - 1, TB - 1)
                nc.vector.tensor_tensor(nm[:, 1, :], SH[0:HC, :], nm[:, 0, :], ALU.subtract).then_inc(max_split, 1)

            def turn_out(r, m, g):
                r.wait(misc_made, misc_count, m, "turn_out", g)
                heads = SH.rearrange("p (q j d) -> p q j d", q=TB, j=G4)
                nc.vector.reciprocal(rinv[:], heads[:, :, :, DH]).then_inc(inverse, 1)
                r.wait(inverse, sum_count, m, g)
                for q in range(TB):
                    last = nc.vector.tensor_tensor(by(on[:, q, g * G4 * DH:(g + 1) * G4 * DH], DH), heads[:, q, :, 0:DH],
                                                   bcast(rinv[:, q, :], 2, DH), ALU.mult)
                last.then_inc(normed, 1)

            def add(r, m, half):
                if m == 0 and r.expert is None and half == 0:
                    dve.wait_ge(r_bias, T // 2)
                if half == 0:
                    nc.vector.tensor_copy(gate[:], t.gates[:, r.expert_of(m), (m % B) * TB:(m % B + 1) * TB])\
                        .then_inc(gate_ready, 1)
                r.wait(misc_made, misc_count, m, "add", half)
                r.wait(gate_ready, lambda m: m + 1, m)
                for i in range(2):
                    q = 2 * half + i
                    x = t.x[:, (m % B) * TB + q, :]
                    last = nc.vector.scalar_tensor_tensor(x, SH[:, i * D:(i + 1) * D], gate[:, q:q + 1], x, ALU.mult, ALU.add)
                last.then_inc(added, 1)
                if half == 1 and r.expert is None and m // B == E - 1:
                    dve.wait_ge(added, value_count(m, 1))
                    x_moments(nc, t, steps, m % B)

            def step(ins):
                steps.did(ins)
                steps.wait()

            def route_hidden(r, _, b):
                ks = range(b * TB, (b + 1) * TB)
                dve.wait_ge(r_made, ROUTE_AT["route_hidden", b] + 1)
                nc.vector.tensor_tensor(r_h[:, b * TB:(b + 1) * TB, :], by(route_bank("route_hidden", b), R1),
                                        bcast(r_rows[:, 0:R1], 1, TB), ALU.add).then_inc(r_hidden, 1)
                dve.wait_ge(r_hidden, b + 1)
                for k in ks:
                    steps.did(nc.vector.bn_stats(t.stats[:, k, :], r_h[:, k, :]))
                steps.wait()
                for k in ks:
                    last = nc.vector.bn_aggr(t.mv[:, k, :], t.stats[:, k, :])
                last.then_inc(r_var, 1)

            def route_norm(r, _, a):
                dve.wait_ge(r_std, B)
                step(nc.vector.reciprocal(t.rstd[:], t.std[:]))
                for k in range(T):
                    last = nc.vector.tensor_scalar(r_h[:, k, :], r_h[:, k, :], t.mv[:, k, 0:1], t.rstd[:, k:k + 1],
                                                   ALU.subtract, ALU.mult)
                    if k % TB == TB - 1:
                        last.then_inc(r_normed, 1)

            def largest(n):
                step(nc.vector.tensor_reduce(r_one, r_lg, AX.X, ALU.max))
                step(nc.vector.tensor_tensor(r_cand, r_lg, bcast(r_one, 2, E), ALU.is_equal))
                step(nc.vector.tensor_tensor(r_cand, r_cand, bcast(t.const[:, CONST["first"]], 1, T), ALU.mult))
                step(nc.vector.tensor_reduce(r_one, r_cand, AX.X, ALU.max))
                step(nc.vector.tensor_tensor(r_pick[:, n, :, :], r_cand, bcast(r_one, 2, E), ALU.is_equal))

            def route_pick(r, _, i):
                if i == 0:
                    dve.wait_ge(r_made, ROUTE_AT["route_logits", None] + 1)
                    nc.vector.tensor_tensor(r_lg, by(route_bank("route_logits", None)[:, 0:T * E], E),
                                            bcast(r_rows[:, R1:R1 + E], 1, T), ALU.add).then_inc(r_logits, 1)
                    dve.wait_ge(r_logits, 1)
                    step(nc.vector.tensor_reduce(r_one, r_lg, AX.X, ALU.max))
                    nc.vector.tensor_tensor(r_lg, r_lg, bcast(r_one, 2, E), ALU.subtract).then_inc(r_centred, 1)
                if i == 1:
                    dve.wait_ge(r_exp, 1)
                    step(nc.vector.tensor_reduce(r_one, r_pr, AX.X, ALU.add))
                    step(nc.vector.reciprocal(r_one, r_one))
                    step(nc.vector.tensor_tensor(r_pr, r_pr, bcast(r_one, 2, E), ALU.mult))
                if i == 2:
                    step(nc.vector.tensor_copy(r_lg, r_pr))
                    largest(0)
                if i == 3:
                    step(nc.vector.tensor_scalar(r_cand, r_pick[:, 0, :, :], -2.0, None, ALU.mult))
                    step(nc.vector.tensor_tensor(r_lg, r_lg, r_cand, ALU.add))
                if i == 4:
                    largest(1)
                if i == 5:
                    step(nc.vector.tensor_tensor(r_cand, r_pick[:, 0, :, :], r_pick[:, 1, :, :], ALU.add))
                    step(nc.vector.tensor_tensor(r_pr, r_pr, r_cand, ALU.mult))
                    step(nc.vector.tensor_reduce(r_one, r_pr, AX.X, ALU.add))
                    step(nc.vector.reciprocal(r_one, r_one))
                    nc.vector.tensor_tensor(t.gates[:].rearrange("p e k -> p k e"), r_pr, bcast(r_one, 2, E), ALU.mult)\
                        .then_inc(r_gates, 1)

            def route_bias(r, _, j):
                dve.wait_ge(r_made, ROUTE_AT["route_bias", j] + 1)
                xs = t.x[:, 2 * j:2 * j + 2, :]
                nc.vector.tensor_tensor(xs, xs, by(route_bank("route_bias", j), D), ALU.add).then_inc(r_bias, 1)

            steps = Steps(dve, own)
            nc.vector.memset(OUT, 0.0).then_inc(sum_clear, 1)
            for i in range(2):
                nc.vector.memset(vs[i][:, :, :, DH:DH + 1], 1.0).then_inc(v_ones, 1)
            Rounds(dve, nc, {"maxima": maxima, "project": project, "project_v": project_v, "row_max": row_max,
                             "turn_out": turn_out, "add": add, "route_hidden": route_hidden, "route_norm": route_norm,
                             "route_pick": route_pick, "route_bias": route_bias})

        @block.gpsimd
        def _(pool):
            def project(r, m, a):
                r.wait(rest_ready, project_count, m, a)
                if m >= 1:
                    r.wait(qk_moved[a // 2], moved_count, m - 1)
                nc.gpsimd.tensor_tensor(parts[:, a, 1, :], rest[:, a % 2, :], t.one.broadcast_to([P, S]), ALU.mult)\
                    .then_inc(mid_ready, 1)
                r.wait(mid_ready, project_count, m, a)
                if m >= 2 and a % 2:
                    r.wait(scores, score_count, m - 2, HC * (a // 2 + 1) - 1, TB - 1)
                nc.gpsimd.tensor_tensor(parts[:, a, 2, :], rest[:, a % 2, :], parts[:, a, 1, :], ALU.subtract)\
                    .then_inc(low_ready, 1)
                if a == 3 and m < 2 and r.expert is None:
                    pool.wait_ge(low_ready, project_count(m, a))
                    nc.gpsimd.memset(ks[m][SPLIT_ROWS:MAX_ROWS, :, :], 1.0).then_inc(k_ones, 1)
                    pool.wait_ge(k_ones, m + 1)

            Rounds(pool, nc, {"project": project})


EARLY = 2


def sign_steps():
    steps = [("normalise", 0, None), ("turn", 0, None), ("normalise", 1, None)]
    for c in range(OC):
        steps.append(("layer0", 0, c))
        if c == 0:
            steps.append(("turn", 1, None))
        if c >= 2:
            steps.append(("early", 0, c - 2))
    steps += [("early", 0, OC - 2)] + [("layer1", 0, c) for c in range(EARLY)]
    for b in range(B):
        for c in range(OC):
            if b or c >= EARLY:
                steps.append(("layer1", b, c))
            if b + 1 < B:
                steps.append(("layer0", b + 1, c))
            if b and c < TB:
                steps.append(("output", b - 1, c))
            if b + 2 < B and c in (1, OC // 2):
                steps.append(("normalise" if c == 1 else "turn", b + 2, None))
    return steps + [("output", B - 1, i) for i in range(TB)]


def sign_stage(nc, t, io):
    steps = sign_steps()
    units = [s for s in steps if s[0] in ("layer0", "layer1")]
    unit = {s: i for i, s in enumerate(units)}
    early = [("layer1", 0, c) for c in range(EARLY)]
    turns = [s for s in units if s not in early]
    bank = {s: t.ps[:, i % 4, :] for i, s in enumerate(turns)} | {s: t.ps[:, 4 + i, :] for i, s in enumerate(early)}
    had_before = {s: turns[i - 4] for i, s in enumerate(turns) if i >= 4}
    with ExitStack() as stack:
        sc = Scope(nc, "sign", stack)
        x_high, x_rest, x_mid, x_low = sc.sems("x_high x_rest x_mid x_low")
        std_ready, own, xn_ready, turned = sc.sems("std_ready own xn_ready turned")
        made, kept, high, left, mid, low, y_ready, y_added, stored = sc.sems(
            "made kept high left mid low y_ready y_added stored")
        xn = sc.sb("xn", [P, 2, TB, D])
        xp = sc.sb("xp", [P, 2, 3, KC, S], BF16)
        xr = sc.sb("xr", [P, KC, S])
        hp = [[sc.sb(f"hp{layer}_{i}", [P, 3, OC, S], BF16) for i in range(2)] for layer in range(2)]
        hf = sc.sb("hf", [P, 2, S])
        hr = sc.sb("hr", [P, 2, S])
        block = stack.enter_context(nc.Block())

        def layer_of(kind):
            return 0 if kind == "layer0" else 1

        @block.sync
        def _(sp):
            for b in range(B):
                sp.wait_ge(y_added, (b + 1) * TB)
                sp.dma_start(io["out"][:, b * TB:(b + 1) * TB, :], t.x[:, b * TB:(b + 1) * TB, :]).then_inc(stored, 16)
            sp.wait_ge(stored, 16 * B)

        @block.tensor
        def _(pe):
            pe.wait_ge(t.signs_ready, 3)

            def add_chunk(target, w, src, k, n, c):
                for part in range(3):
                    last = nc.tensor.matmul(target, w[:, k, c * P:(c + 1) * P], src[:, part, k, :],
                                            start=k == 0 and part == 0, stop=k == n - 1 and part == 2)
                return last

            def sum_early(k):
                pe.wait_ge(low, unit["layer0", 0, k] + 1)
                for c in range(EARLY):
                    add_chunk(bank["layer1", 0, c], t.w1, hp[0][0], k, OC, c)

            def products(kind, b, c):
                this = kind, b, c
                w, src, n = (t.w0, xp[:, b % 2, :, :, :], KC) if kind == "layer0" else (t.w1, hp[0][b % 2], OC)
                if kind == "layer0":
                    pe.wait_ge(x_low, b + 1)
                if this in had_before:
                    pe.wait_ge(kept, unit[had_before[this]] + 1)
                for k in range(OC - 1 if this in early else 0, n):
                    if kind == "layer1" and c == 0:
                        pe.wait_ge(low, unit["layer0", b, k] + 1)
                    last = add_chunk(bank[this], w, src, k, n, c)
                last.then_inc(made, 1)

            def output(b, i):
                j = b * TB + i
                if j < EARLY:
                    pe.wait_ge(kept, unit["layer1", 0, j] + 1)
                if j >= 2:
                    pe.wait_ge(y_added, j - 1)
                for k in range(OC):
                    if i == 0:
                        pe.wait_ge(low, unit["layer1", b, k] + 1)
                    for part in range(3):
                        last = nc.tensor.matmul(t.ps[:, 4 + j % 2, 0:D], hp[1][b % 2][:, part, k, i * P:(i + 1) * P],
                                                t.w2[:, k, :], start=k == 0 and part == 0, stop=k == OC - 1 and part == 2)
                last.then_inc(y_ready, 1)

            for kind, b, a in steps:
                if kind == "turn":
                    pe.wait_ge(xn_ready, b + 1)
                    if b:
                        pe.wait_ge(x_rest, b)
                    for c in range(KC):
                        for i in range(TB):
                            last = nc.tensor.transpose(t.ps[:, 6 + c, i * P:(i + 1) * P],
                                                       xn[:, b % 2, i, c * P:(c + 1) * P], t.ident)
                    last.then_inc(turned, 1)
                elif kind == "output":
                    output(b, a)
                elif kind == "early":
                    sum_early(a)
                elif kind != "normalise":
                    products(kind, b, a)

        @block.scalar
        def _(act):
            def root(b):
                nc.scalar.activation(t.std[:, b * TB:(b + 1) * TB], t.x_mv[:, b * TB:(b + 1) * TB, 1], ACT.Sqrt,
                                     bias=t.eps).then_inc(std_ready, 1)

            def x_part(b):
                if b >= 2:
                    act.wait_ge(made, unit["layer0", b - 2, OC - 1] + 1)
                act.wait_ge(turned, b + 1)
                nc.scalar.copy(xp[:, b % 2, 0, :, :], t.ps[:, 6:6 + KC, :]).then_inc(x_high, 1)

            for b in range(B):
                root(b)
            for kind, b, c in steps:
                if kind == "turn":
                    x_part(b)
                if kind not in ("layer0", "layer1"):
                    continue
                u, layer = unit[kind, b, c], layer_of(kind)
                act.wait_ge(made, u + 1)
                if u >= 2:
                    act.wait_ge(left, u - 1)
                nc.scalar.activation(hf[:, u % 2, :], bank[kind, b, c], ACT.Relu, scale=t.sv4[:, layer:layer + 1])\
                    .then_inc(kept, 1)
                act.wait_ge(kept, u + 1)
                if c == 0 and b >= 2:
                    if layer == 0:
                        act.wait_ge(made, unit["layer1", b - 2, OC - 1] + 1)
                    else:
                        act.wait_ge(y_ready, (b - 1) * TB)
                nc.scalar.copy(hp[layer][b % 2][:, 0, c, :], hf[:, u % 2, :]).then_inc(high, 1)

        @block.vector
        def _(dve):
            own_steps = Steps(dve, own)

            def normalise(b):
                dve.wait_ge(std_ready, b + 1)
                own_steps.did(nc.vector.reciprocal(t.rstd[:, b * TB:(b + 1) * TB], t.std[:, b * TB:(b + 1) * TB]))
                if b >= 2:
                    dve.wait_ge(turned, b - 1)
                own_steps.wait()
                for i in range(TB):
                    k = b * TB + i
                    last = nc.vector.tensor_scalar(xn[:, b % 2, i, :], t.x[:, k, :], t.x_mv[:, k, 0:1], t.rstd[:, k:k + 1],
                                                   ALU.subtract, ALU.mult)
                last.then_inc(xn_ready, 1)

            def x_part(b):
                dve.wait_ge(x_high, b + 1)
                if b:
                    dve.wait_ge(x_low, b)
                nc.vector.tensor_tensor(xr[:], t.ps[:, 6:6 + KC, :], xp[:, b % 2, 0, :, :], ALU.subtract)\
                    .then_inc(x_rest, 1)
                dve.wait_ge(x_rest, b + 1)
                nc.vector.tensor_copy(xp[:, b % 2, 1, :, :], xr[:]).then_inc(x_mid, 1)
                dve.wait_ge(x_mid, b + 1)
                nc.vector.tensor_tensor(xp[:, b % 2, 2, :, :], xr[:], xp[:, b % 2, 1, :, :], ALU.subtract)\
                    .then_inc(x_low, 1)

            for kind, b, a in steps:
                if kind == "normalise":
                    normalise(b)
                elif kind == "turn":
                    x_part(b)
                elif kind == "output":
                    j = b * TB + a
                    dve.wait_ge(y_ready, j + 1)
                    nc.vector.scalar_tensor_tensor(t.x[:, j, :], t.ps[:, 4 + j % 2, 0:D], t.sv[:, 2:3], t.x[:, j, :],
                                                   ALU.mult, ALU.add).then_inc(y_added, 1)
                elif kind != "early":
                    u, parts = unit[kind, b, a], hp[layer_of(kind)][b % 2]
                    dve.wait_ge(high, u + 1)
                    nc.vector.tensor_tensor(hr[:, u % 2, :], hf[:, u % 2, :], parts[:, 0, a, :], ALU.subtract)\
                        .then_inc(left, 1)
                    dve.wait_ge(left, u + 1)
                    nc.vector.tensor_copy(parts[:, 1, a, :], hr[:, u % 2, :]).then_inc(mid, 1)
                    dve.wait_ge(mid, u + 1)
                    nc.vector.tensor_tensor(parts[:, 2, a, :], hr[:, u % 2, :], parts[:, 1, a, :], ALU.subtract)\
                        .then_inc(low, 1)


class State:
    pass


def build(nc, io):
    with ExitStack() as stack:
        sc = Scope(nc, "main", stack)
        t = State()
        t.ps = stack.enter_context(nc.psum_tensor("ps", [P, 8, 512], F32))
        t.const = sc.sb("const", [P, NCONST])
        t.x = sc.sb("x", [P, T, D])
        t.xnT = sc.sb("xnT", [P, KC, B * S])
        t.gates = sc.sb("gates", [P, E, T])
        t.stats = sc.sb("stats", [P, T, 6])
        t.mv = sc.sb("mv", [P, T, 2])
        t.x_mv = sc.sb("x_mv", [P, T, 2])
        t.std = sc.sb("std", [P, T])
        t.rstd = sc.sb("rstd", [P, T])
        t.ident = t.const[:, CONST["ident"]]
        t.eps = t.const[:, CONST["eps"]]
        t.one = t.const[:, CONST["one"]]
        t.heads = {16: t.const[:, CONST["heads16"]], 8: t.const[:, CONST["heads8"]]}

        def context_buffers(si):
            t.ctxT = si.sb("ctxT", [P, KC, NCTX])
            t.ctxT2 = si.sb("ctxT2", [P, KC, B, 2, S2])
            t.ctxnT = si.sb("ctxnT", [P, KC, NCTX])
            t.bound = si.sb("bound", [P, NCTX])
            t.pre = si.sb("pre", [P, 2, KC])

        with ExitStack() as inner:
            si = Scope(nc, "first", inner)
            context_buffers(si)
            rot = si.sb("rot", [P, 2 * S + P])
            t.rot, t.exchange = [rot[:, 0:S], rot[:, S:2 * S]], rot[:, 2 * S:]
            order = ("q", "k", "v", "o")
            W, W_in = si.sb("w", [P, KC, len(order), D]), si.sem("w_in")
            prepare_stage(nc, t, io, "prepare0", [(t.const, io["const"])], si.sems("x_in0 x_in1 x_in2 x_in3"),
                          [(rot, io["rot"], W_in), (W, io["a0"], W_in)], None, 1)
            context_attention(nc, t, io, "attn0", H0, W, W_in, order, (D // H0) ** -0.5, True, t.ctxT, None, False)

        with ExitStack() as inner:
            weights = ExpertWeights(Scope(nc, "expert_weights", inner), io)
            layernorm_stage(nc, t, "ln1", weights.load_first)
            expert_stage(nc, t, io, weights)

        t.w0 = sc.sb("w0", [P, KC, FF], BF16)
        t.w1 = sc.sb("w1", [P, OC, FF], BF16)
        t.w2 = sc.sb("w2", [P, OC, D], BF16)
        t.sv = sc.sb("sv", [P, 3])
        t.sv4 = sc.sb("sv4", [P, 3])
        t.signs_ready = sc.sem("signs_ready")
        with ExitStack() as inner:
            si = Scope(nc, "second", inner)
            context_buffers(si)
            order = ("q", "k", "v", "o")
            W, W_in, signs_in = si.sb("w", [P, KC, len(order), D]), si.sem("w_in"), si.sem("signs_in")
            words = [si.sb(f"words{i}", [P, rows, width // 4], U32)
                     for i, (rows, width) in enumerate(((2 * KC, FF), (OC, FF), (OC, D)))]

            def make_signs(dve):
                signs = [w[:].bitcast(U8) for w in words]
                dve.wait_ge(signs_in, 16 * 4)
                nc.vector.tensor_tensor(t.w0[:], signs[0][:, 0:KC, :], signs[0][:, KC:2 * KC, :], ALU.subtract)
                nc.vector.tensor_scalar(t.w1[:], signs[1], 2.0, -1.0, ALU.mult, ALU.add).then_inc(t.signs_ready, 1)
                nc.vector.tensor_scalar(t.w2[:], signs[2], 2.0, -1.0, ALU.mult, ALU.add).then_inc(t.signs_ready, 1)
                nc.vector.tensor_scalar(t.sv4[:, 0:1], t.sv[:, 0:1], 4.0, None, ALU.mult)
                nc.vector.tensor_scalar(t.sv4[:, 1:2], t.sv[:, 1:2], 2.0, None, ALU.mult).then_inc(t.signs_ready, 1)

            prepare_stage(nc, t, io, "prepare1", [], None, [(W, io["a1"], W_in)] + [
                (out, io[n], signs_in) for out, n in zip(words + [t.sv], ("k0", "k1", "k2", "sv"))],
                          (t.pre[:, 0, :], t.pre[:, 1, :]), 2)
            context_attention(nc, t, io, "attn1", H1, W, W_in, order, D ** -0.5, False, t.ctxnT, 1e4 * D ** 0.5,
                              True, make_signs)
        sign_stage(nc, t, io)


def constants():
    const = np.zeros((P, NCONST), np.float32)
    rows = np.arange(P)
    const[:, CONST["ident"]] = np.eye(P)
    dh = D // H0
    for heads in (H0, H1):
        const[:, CONST[f"heads{heads}"]] = rows[:, None] // (D // heads) == np.arange(heads // KC)[None]
    const[:, CONST["first"]] = np.arange(E, 0, -1)
    const[:, CONST["eps"]] = EPS
    const[:, CONST["one"]] = 1
    div = np.exp(np.arange(0, dh, 2, dtype=np.float32) * np.float32(-np.log(10000.0) / dh))
    angle = (np.arange(S, dtype=np.float32)[:, None] * div).T
    which = rows % dh
    sign = np.where(which < dh // 2, -1, 1).astype(np.float32)[:, None]
    exchange = np.eye(P)[(rows // dh) * dh + (rows + dh // 2) % dh]
    rot = np.concatenate([np.cos(angle)[which % (dh // 2)], np.sin(angle)[which % (dh // 2)] * sign, exchange], 1)
    return const, rot.astype(np.float32)


def lay_out(i):
    f = lambda name: np.asarray(i[name])
    chunks = lambda w: w.reshape(w.shape[0] // P, P, -1).transpose(1, 0, 2)
    rep = lambda row: np.broadcast_to(row, (P,) + row.shape)
    cols = lambda v: v.reshape(-1, P).T
    a = {}
    a["const"], a["rot"] = constants()
    a["x"] = f("x").reshape(T, P, D).transpose(1, 0, 2)
    a["ctx"] = f("ctx_1024").reshape(NCTX // P, P, D).transpose(1, 0, 2)
    a["mask"] = rep(f("mask_BxS2_bf1").view(np.uint8).reshape(NCTX))
    a["pre"] = np.stack([cols(f("L1_xattn_pre_g")), cols(f("L1_xattn_pre_b"))], 1)
    wq, wkv, wo = f("L0_xattn_Wq"), f("L0_xattn_Wkv"), f("L0_xattn_Wout")
    a["a0"] = np.stack([chunks(w) for w in (wq, wkv[:, :D], wkv[:, D:], wo)], 2)
    a["a1"] = np.stack([chunks(f(f"L1_xattn_W{n}")) for n in "qkvo"], 2)
    a["a1_cols"] = np.stack([cols(f("L1_xattn_ln_g")), cols(f("L1_xattn_ln_b"))], 1)
    a["rW1"] = chunks(f("L0_ffn_rW1").T)
    a["r_rows"] = np.concatenate([rep(f("L0_ffn_rb1")), rep(f("L0_ffn_rb2"))], 1)
    a["r_cols"] = np.concatenate([f("L0_ffn_ln_g")[:, None], f("L0_ffn_ln_b")[:, None], f("L0_ffn_rW2").T], 1)
    a["ob"] = f("L0_ffn_ob")
    order = np.arange(D).reshape(KC, HC, DH).transpose(0, 2, 1).reshape(KC, P)
    qk, biases = [], []
    for n in "qk":
        w = f(f"L0_ffn_{n}W").transpose(0, 2, 1)
        w = w.reshape(E, KC, P, D)[:, :, :, order]
        qk.append(w.transpose(0, 2, 3, 1, 4).reshape(E, P, -1))
        biases.append(f(f"L0_ffn_{n}b")[:, order].transpose(0, 2, 1))
    a["e_qk"] = np.concatenate(qk + biases, 2)
    wide = lambda w: w.transpose(0, 2, 1).reshape(E, KC, P, D).transpose(0, 2, 1, 3).reshape(E, P, KC * D)
    a["e_v"] = np.concatenate([wide(f("L0_ffn_vW")), np.broadcast_to(f("L0_ffn_vb")[:, None], (E, P, D))], 2)
    a["e_o"] = wide(f("L0_ffn_oW"))
    for n in range(3):
        a[f"k{n}"] = np.ascontiguousarray(chunks(f(f"L1_ffn_k{n}").view(np.uint8))).view(np.uint32)
    a["sv"] = np.stack([np.broadcast_to(f(f"L1_ffn_s{n}").reshape(()), (P,)) for n in range(3)], 1)
    return {n: np.ascontiguousarray(v) for n, v in a.items()}


def kernel(**inputs):
    import concourse.bacc as bacc
    from concourse.bass_utils import run_bass_kernel_spmd

    arrays = lay_out(inputs)
    nc = bacc.Bacc("TRN2", target_bir_lowering=False, num_devices=1)
    io = {n: nc.dram_tensor(f"in_{n}", v.shape, mybir.dt.from_np(v.dtype), kind="ExternalInput").ap()
          for n, v in arrays.items()}
    io["out"] = nc.dram_tensor("out_x", (P, T, D), F32, kind="ExternalOutput").ap()
    build(nc, io)
    r = run_bass_kernel_spmd(nc, [{f"in_{n}": v for n, v in arrays.items()}], core_ids=[0])
    out = r.results[0]["out_x"]
    return np.ascontiguousarray(out.transpose(1, 0, 2)).reshape(B, S, D)
```
